# Optimizing a Trainium2 kernel written in Bass

```python
import numpy as np
import jax
import jax.numpy as jnp

def _softmax(x, axis=-1):
    return jax.nn.softmax(x, axis=axis)

def _gelu(x):
    return jax.nn.gelu(x, approximate=True)

def _silu(x):
    return jax.nn.silu(x)

def _sigmoid(x):
    return jax.nn.sigmoid(x)

def _layernorm(x, axis=-1, eps=1e-05):
    m = jnp.mean(x, axis=axis, keepdims=True)
    v = jnp.var(x, axis=axis, keepdims=True)
    return (x - m) / jnp.sqrt(v + eps)

def _scatter_add(tgt, idx, src, axis=0):
    return tgt.at[idx].add(src)

def _segment_sum(src, seg, n):
    return jax.ops.segment_sum(src, seg, n)
kernel_name = 'mk_gnn_preln_d4_gnn_r32_8c9f20'

def setup_inputs(seed: int=0):
    np.random.seed(seed)
    _w = jnp.asarray

    def _rec_inputs():
        import jax
        import jax.numpy as jnp
        _gk = jax.random.key(seed)
        x = -0.000202 + 1 * jax.random.normal(jax.random.fold_in(_gk, 1), (3125, 128), jnp.float32)
        src = jax.random.randint(jax.random.fold_in(_gk, 2), (100000,), 0, 3125, jnp.int32)
        dst = jax.random.randint(jax.random.fold_in(_gk, 3), (100000,), 0, 3125, jnp.int32)
        _o = jnp.argsort(dst, stable=True)
        src = src[_o]
        dst = dst[_o]
        edge_type_4 = jax.random.randint(jax.random.fold_in(_gk, 14), (100000,), 0, 4, jnp.int32)
        return (x, src, dst, edge_type_4)
    x, src, dst, edge_type_4 = _rec_inputs()

    def _L0_gnn_setup():
        import jax, jax.numpy as jnp
        import numpy as np
        N_NODES = 50000
        N_EDGES = 25000
        D_IN, D_HID, D_OUT = (128, 256, 128)

        def _seg_mean(msgs, dst, num_segments):
            s = jax.ops.segment_sum(msgs, dst, num_segments=num_segments)
            cnt = jax.ops.segment_sum(jnp.ones((dst.shape[0], 1), msgs.dtype), dst, num_segments=num_segments)
            return s / jnp.maximum(cnt, 1.0)

        def _sage_conv(x, edge_index, W_l, b_l, W_r):
            src, dst = (edge_index[0], edge_index[1])
            agg = _seg_mean(x[src], dst, x.shape[0])
            return agg @ W_l + b_l + x @ W_r
        key = jax.random.key(seed)
        ks = jax.random.split(key, 8)
        x = jax.random.normal(ks[0], (N_NODES, D_IN), dtype=jnp.float32)
        edge_index = jax.random.randint(ks[1], (2, N_EDGES), 0, N_NODES, dtype=jnp.int64)

        def glorot(k, shape):
            lim = float(np.sqrt(6.0 / (shape[0] + shape[1])))
            return jax.random.uniform(k, shape, jnp.float32, -lim, lim)
        return {'x': x, 'edge_index': edge_index, 'W_l1': glorot(ks[2], (D_IN, D_HID)), 'b_l1': jnp.zeros((D_HID,), jnp.float32), 'W_r1': glorot(ks[3], (D_IN, D_HID)), 'W_l2': glorot(ks[4], (D_HID, D_OUT)), 'b_l2': jnp.zeros((D_OUT,), jnp.float32), 'W_r2': glorot(ks[5], (D_HID, D_OUT))}
    _L0_gnn_all = _L0_gnn_setup()
    _L0_gnn_in = {k: v for k, v in _L0_gnn_all.items() if k in ('W_l1', 'b_l1', 'W_r1', 'W_l2', 'b_l2', 'W_r2')}
    del _L0_gnn_all

    def _L1_gnn_setup():
        import jax, jax.numpy as jnp
        import numpy as np
        N = 3125
        E = 50000
        D = 128
        G = 128
        K = 4
        STEPS = 3

        def _gru_cell(a, h, W_ih, b_ih, W_hh, b_hh):
            gi = a @ W_ih.T + b_ih
            gh = h @ W_hh.T + b_hh
            ir, iz, in_ = jnp.split(gi, 3, axis=1)
            hr, hz, hn = jnp.split(gh, 3, axis=1)
            r = jax.nn.sigmoid(ir + hr)
            z = jax.nn.sigmoid(iz + hz)
            n = jnp.tanh(in_ + r * hn)
            return (1.0 - z) * n + z * h
        key = jax.random.key(seed)
        ks = jax.random.split(key, 16)
        s = 0.05
        return {'features': jax.random.normal(ks[0], (N, D), jnp.float32), 'src': jax.random.randint(ks[1], (E,), 0, N, jnp.int32), 'dst': jax.random.randint(ks[2], (E,), 0, N, jnp.int32), 'etypes': jax.random.randint(ks[3], (E,), 0, K, jnp.int32), 'W_et': jax.random.normal(ks[4], (K, D, D), jnp.float32) * s, 'b_et': jax.random.normal(ks[5], (K, D), jnp.float32) * s, 'W_ih': jax.random.normal(ks[6], (3 * D, D), jnp.float32) * s, 'b_ih': jax.random.normal(ks[7], (3 * D,), jnp.float32) * s, 'W_hh': jax.random.normal(ks[8], (3 * D, D), jnp.float32) * s, 'b_hh': jax.random.normal(ks[9], (3 * D,), jnp.float32) * s, 'i_w': jax.random.normal(ks[10], (G, D + D), jnp.float32) * s, 'i_b': jax.random.normal(ks[11], (G,), jnp.float32) * s, 'j_w': jax.random.normal(ks[12], (G, D), jnp.float32) * s, 'j_b': jax.random.normal(ks[13], (G,), jnp.float32) * s}
    _L1_gnn_all = _L1_gnn_setup()
    _L1_gnn_in = {k: v for k, v in _L1_gnn_all.items() if k in ('W_et', 'b_et', 'W_ih', 'b_ih', 'W_hh', 'b_hh', 'i_w', 'i_b', 'j_w', 'j_b')}
    del _L1_gnn_all

    def _L2_gnn_setup():
        import jax, jax.numpy as jnp
        import numpy as np
        NEG_SLOPE = 0.01

        def gcn_conv(x, src, dst, W, b, n_nodes):
            ones = jnp.ones(src.shape[0], dtype=x.dtype)
            deg = jax.ops.segment_sum(ones, dst, num_segments=n_nodes)
            dis = jnp.where(deg > 0, jax.lax.rsqrt(deg), jnp.zeros_like(deg))
            norm = dis[src] * dis[dst]
            h = x @ W
            msg = h[src] * norm[:, None]
            out = jax.ops.segment_sum(msg, dst, num_segments=n_nodes)
            return out + b
        key = jax.random.key(seed)
        k1, k2, k3, k4 = jax.random.split(key, 4)
        N, E, IN_C, H_C, OUT_C = (50000, 25000, 128, 128, 128)
        x = jax.random.normal(k1, (N, IN_C), dtype=jnp.float32)
        edge_index = jax.random.randint(k2, (2, E), 0, N, dtype=jnp.int32)
        W1 = jax.random.normal(k3, (IN_C, H_C), dtype=jnp.float32) * (1.0 / np.sqrt(IN_C))
        b1 = jnp.zeros((H_C,), dtype=jnp.float32)
        W2 = jax.random.normal(k4, (H_C, OUT_C), dtype=jnp.float32) * (1.0 / np.sqrt(H_C))
        b2 = jnp.zeros((OUT_C,), dtype=jnp.float32)
        return {'x': x, 'edge_index': edge_index, 'W1': W1, 'b1': b1, 'W2': W2, 'b2': b2}
    _L2_gnn_all = _L2_gnn_setup()
    _L2_gnn_in = {k: v for k, v in _L2_gnn_all.items() if k in ('W1', 'b1', 'W2', 'b2')}
    del _L2_gnn_all

    def _L3_gnn_setup():
        import jax, jax.numpy as jnp
        import numpy as np
        N, E, D_IN, D_OUT = (10000, 20000, 128, 128)
        key = jax.random.key(seed)
        ks = jax.random.split(key, 7)
        feat = jax.random.normal(ks[0], (N, D_IN), dtype=jnp.float32)
        W = jax.random.normal(ks[1], (D_OUT, D_IN), dtype=jnp.float32) * (1.0 / np.sqrt(D_IN))
        b = jax.random.normal(ks[2], (D_OUT,), dtype=jnp.float32) * (1.0 / np.sqrt(D_IN))
        in_norm = jax.random.uniform(ks[3], (N,), dtype=jnp.float32) + 0.5
        out_norm = jax.random.uniform(ks[4], (N,), dtype=jnp.float32) + 0.5
        src = jax.random.randint(ks[5], (E,), 0, N, dtype=jnp.int32)
        dst = jax.random.randint(ks[6], (E,), 0, N, dtype=jnp.int32)
        return {'feat': feat, 'W': W, 'b': b, 'in_norm': in_norm, 'out_norm': out_norm, 'src': src, 'dst': dst}
    _L3_gnn_all = _L3_gnn_setup()
    _L3_gnn_in = {k: v for k, v in _L3_gnn_all.items() if k in ('W', 'b')}
    del _L3_gnn_all
    return {'x': x, 'src': src, 'dst': dst, 'edge_type_4': edge_type_4, 'L0_gnn_W_l1': _L0_gnn_in['W_l1'], 'L0_gnn_b_l1': _L0_gnn_in['b_l1'], 'L0_gnn_W_r1': _L0_gnn_in['W_r1'], 'L0_gnn_W_l2': _L0_gnn_in['W_l2'], 'L0_gnn_b_l2': _L0_gnn_in['b_l2'], 'L0_gnn_W_r2': _L0_gnn_in['W_r2'], 'L1_gnn_W_et': _L1_gnn_in['W_et'], 'L1_gnn_b_et': _L1_gnn_in['b_et'], 'L1_gnn_W_ih': _L1_gnn_in['W_ih'], 'L1_gnn_b_ih': _L1_gnn_in['b_ih'], 'L1_gnn_W_hh': _L1_gnn_in['W_hh'], 'L1_gnn_b_hh': _L1_gnn_in['b_hh'], 'L1_gnn_i_w': _L1_gnn_in['i_w'], 'L1_gnn_i_b': _L1_gnn_in['i_b'], 'L1_gnn_j_w': _L1_gnn_in['j_w'], 'L1_gnn_j_b': _L1_gnn_in['j_b'], 'L2_gnn_W1': _L2_gnn_in['W1'], 'L2_gnn_b1': _L2_gnn_in['b1'], 'L2_gnn_W2': _L2_gnn_in['W2'], 'L2_gnn_b2': _L2_gnn_in['b2'], 'L3_gnn_W': _L3_gnn_in['W'], 'L3_gnn_b': _L3_gnn_in['b']}

def reference(x, src, dst, edge_type_4, L0_gnn_W_l1, L0_gnn_b_l1, L0_gnn_W_r1, L0_gnn_W_l2, L0_gnn_b_l2, L0_gnn_W_r2, L1_gnn_W_et, L1_gnn_b_et, L1_gnn_W_ih, L1_gnn_b_ih, L1_gnn_W_hh, L1_gnn_b_hh, L1_gnn_i_w, L1_gnn_i_b, L1_gnn_j_w, L1_gnn_j_b, L2_gnn_W1, L2_gnn_b1, L2_gnn_W2, L2_gnn_b2, L3_gnn_W, L3_gnn_b):
    import jax
    import jax.numpy as jnp

    def _L0_gnn_ref(x, edge_index, W_l1, b_l1, W_r1, W_l2, b_l2, W_r2):
        import jax, jax.numpy as jnp
        import numpy as np
        N_NODES = 50000
        N_EDGES = 25000
        D_IN, D_HID, D_OUT = (128, 256, 128)

        def _seg_mean(msgs, dst, num_segments):
            s = jax.ops.segment_sum(msgs, dst, num_segments=num_segments)
            cnt = jax.ops.segment_sum(jnp.ones((dst.shape[0], 1), msgs.dtype), dst, num_segments=num_segments)
            return s / jnp.maximum(cnt, 1.0)

        def _sage_conv(x, edge_index, W_l, b_l, W_r):
            src, dst = (edge_index[0], edge_index[1])
            agg = _seg_mean(x[src], dst, x.shape[0])
            return agg @ W_l + b_l + x @ W_r
        h = _sage_conv(x, edge_index, W_l1, b_l1, W_r1)
        out = _sage_conv(h, edge_index, W_l2, b_l2, W_r2)
        return out

    def _L1_gnn_ref(features, src, dst, etypes, W_et, b_et, W_ih, b_ih, W_hh, b_hh, i_w, i_b, j_w, j_b):
        import jax, jax.numpy as jnp
        import numpy as np
        N = 3125
        E = 50000
        D = 128
        G = 128
        K = 4
        STEPS = 3

        def _gru_cell(a, h, W_ih, b_ih, W_hh, b_hh):
            gi = a @ W_ih.T + b_ih
            gh = h @ W_hh.T + b_hh
            ir, iz, in_ = jnp.split(gi, 3, axis=1)
            hr, hz, hn = jnp.split(gh, 3, axis=1)
            r = jax.nn.sigmoid(ir + hr)
            z = jax.nn.sigmoid(iz + hz)
            n = jnp.tanh(in_ + r * hn)
            return (1.0 - z) * n + z * h
        n_nodes = features.shape[0]
        h = features
        for _ in range(STEPS):
            t = jnp.einsum('nd,kod->kno', h, W_et) + b_et[:, None, :]
            msg = t[etypes, src]
            a = jax.ops.segment_sum(msg, dst, num_segments=n_nodes)
            h = _gru_cell(a, h, W_ih, b_ih, W_hh, b_hh)
        gate = jax.nn.sigmoid(jnp.concatenate([h, features], axis=1) @ i_w.T + i_b)
        return gate * (h @ j_w.T + j_b)

    def _L2_gnn_ref(x, edge_index, W1, b1, W2, b2):
        import jax, jax.numpy as jnp
        import numpy as np
        NEG_SLOPE = 0.01

        def gcn_conv(x, src, dst, W, b, n_nodes):
            ones = jnp.ones(src.shape[0], dtype=x.dtype)
            deg = jax.ops.segment_sum(ones, dst, num_segments=n_nodes)
            dis = jnp.where(deg > 0, jax.lax.rsqrt(deg), jnp.zeros_like(deg))
            norm = dis[src] * dis[dst]
            h = x @ W
            msg = h[src] * norm[:, None]
            out = jax.ops.segment_sum(msg, dst, num_segments=n_nodes)
            return out + b
        n_nodes = x.shape[0]
        loop = jnp.arange(n_nodes, dtype=edge_index.dtype)
        src = jnp.concatenate([edge_index[0], loop])
        dst = jnp.concatenate([edge_index[1], loop])
        h = gcn_conv(x, src, dst, W1, b1, n_nodes)
        h = jnp.where(h >= 0, h, NEG_SLOPE * h)
        out = gcn_conv(h, src, dst, W2, b2, n_nodes)
        return out

    def _L3_gnn_ref(feat, W, b, in_norm, out_norm, src, dst):
        import jax, jax.numpy as jnp
        import numpy as np
        N, E, D_IN, D_OUT = (10000, 20000, 128, 128)
        h = feat / out_norm[:, None]
        msg = jnp.take(h, src, axis=0)
        agg = jax.ops.segment_sum(msg, dst, num_segments=feat.shape[0])
        return agg / in_norm[:, None] @ W.T + b
    edge_index = jnp.stack([src, dst])
    deg = jnp.maximum(jax.ops.segment_sum(jnp.ones(dst.shape, jnp.float32), dst, num_segments=3125), 1.0)
    h = jnp.maximum(_layernorm(x, axis=-1), 0.0)
    x = x + _L0_gnn_ref(h, edge_index, L0_gnn_W_l1, L0_gnn_b_l1, L0_gnn_W_r1, L0_gnn_W_l2, L0_gnn_b_l2, L0_gnn_W_r2)
    h = jnp.maximum(_layernorm(x, axis=-1), 0.0)
    x = x + _L1_gnn_ref(h, src, dst, edge_type_4, L1_gnn_W_et, L1_gnn_b_et, L1_gnn_W_ih, L1_gnn_b_ih, L1_gnn_W_hh, L1_gnn_b_hh, L1_gnn_i_w, L1_gnn_i_b, L1_gnn_j_w, L1_gnn_j_b)
    h = jnp.maximum(_layernorm(x, axis=-1), 0.0)
    x = x + _L2_gnn_ref(h, edge_index, L2_gnn_W1, L2_gnn_b1, L2_gnn_W2, L2_gnn_b2)
    h = jnp.maximum(_layernorm(x, axis=-1), 0.0)
    x = x + _L3_gnn_ref(h, L3_gnn_W, L3_gnn_b, deg, deg, src, dst)
    return x

_drawn_inputs = setup_inputs


def setup_inputs(seed=0):
    import zlib

    import numpy as np

    out = dict(_drawn_inputs(seed))
    spreads = {'L0_gnn_b_l1': (0.0, 0.1),
     'L0_gnn_b_l2': (0.0, 0.1),
     'L2_gnn_b1': (0.0, 0.1),
     'L2_gnn_b2': (0.0, 0.1)}
    factors = {'L1_gnn_b_ih': 7.788,
     'L1_gnn_b_hh': 8.0,
     'L1_gnn_i_b': 8.0,
     'L1_gnn_j_b': 3.028,
     'L3_gnn_W': 5.12}
    for name, (base, spread) in spreads.items():
        noise = np.random.default_rng([zlib.crc32(name.encode()), seed]).standard_normal(out[name].shape)
        drawn = base * np.exp(spread * noise) if base else spread * noise
        out[name] = jnp.asarray(drawn.astype(out[name].dtype))
    for name, factor in factors.items():
        out[name] = (out[name] * factor).astype(out[name].dtype)
    return out
```

```python
from contextlib import ExitStack

import concourse.bass as bass
from concourse import mybir

ALU = mybir.AluOpType
ACT = mybir.ActivationFunctionType
AX = mybir.AxisListType
F32, F16, BF16 = mybir.dt.float32, mybir.dt.float16, mybir.dt.bfloat16
I32, U8, F8 = mybir.dt.int32, mybir.dt.uint8, mybir.dt.float8e4

P = 128
N = 3125
D = 128
E = 100000
KT = 4
NB = (N + P - 1) // P
NLAST = N - (NB - 1) * P
CH = 448
NCH = (N + CH - 1) // CH
NT = NCH * CH
NP = NB * P
ER, EC = 125, 800
WD = 2
NW = NT // WD
WP = 112
WG = NW // WP
CAP = 128
CELL = (KT + 1) * NB * WD
TCELL = KT * NB * WD
GD = 32
GW = GD // WD
NG = NT // GD
GC = CH // GD
PIECE = NB * CH
EPS = 1e-5
OHW = P + CELL
QW = 4
GQ = GW // QW
RING = 4
UNTYPED = KT
NQ = NB // 4 + 1
AGG = {"l0a": 0, "l0b": 1, "l2a": 2, "l2b": 3, "l3a": 4}
BLK = {"l0p": 0, "l0o": 1, "l2p": 2, "l2o": 3, "l3o": 4}
TR = {"l0h": 0, "l1h": 1, "l1t0": 2, "l1t1": 3, "l2h": 4}
DEG = {"deg0": 0, "deg2": 1, "deg3": 2}
LN = {"l0": 0, "l1": 1, "l2": 2, "l3": 3}
GP = {"count": 0, "l0a": 1, "l0b": 2, "l1s0": 3, "l1s1": 7, "l1s2": 11, "l2a": 15, "l2b": 16, "l3a": 17}
GCALL = list(GP)
GX = 5
MULT_MAX = 16


class Chain:

    def __init__(self, eng, sem):
        self.eng, self.sem, self.n, self.i, self.m = eng, sem, 0, None, 0

    def __call__(self, ins):
        self.n += 1
        ins.then_inc(self.sem, 1)
        at = self.n if self.i is None else self.i * self.m + self.n
        self.eng.wait_ge(self.sem, at)

    def enter(self, i, m):
        self.i, self.m, self.start = i, m, self.n

    def leave(self, trips):
        assert self.n - self.start == self.m, (self.n - self.start, self.m)
        self.n, self.i = self.start + trips * self.m, None


def build(nc, a, out, packed, adj, table, sums):
    ctx = ExitStack()
    with ctx:
        def sb(name, shape, dt):
            return ctx.enter_context(nc.sbuf_tensor(name, shape, dt))

        sems = {}

        def S(name):
            if name not in sems:
                sems[name] = ctx.enter_context(nc.semaphore(name))
            return sems[name]

        ctx.enter_context(nc.allow_non_contiguous_dma(reason="small bias columns and row heads"))

        ident = sb("ident", [P, P], F32)
        ones = sb("ones", [P, P], F32)
        ones16 = sb("ones16", [P, 2], F16)
        epsc = sb("epsc", [P, 1], F32)
        iota_i = sb("iota_i", [P, CELL], I32)
        iota16 = sb("iota16", [P, CELL], F16)
        pairs = lambda n: iota16[:, 0:n].rearrange("p (c two) -> p c two", two=2).unsqueeze(1).broadcast_to([P, GW, n // 2, 2])
        wbase_i = sb("wbase_i", [WP, WG], I32)
        wbase = sb("wbase", [WP, WG], F32)

        x_nm = sb("x_nm", [P, NB, D], F32)
        hn = sb("hn", [P, NB, D], F32)
        op = sb("op", [P, NB, 3, D], F16)
        opb = op[:, :, :, :].bitcast(BF16)
        T = sb("T", [P, 4 * NP], F32)
        T0, T1, T2, T3 = (T[:, i * NP:(i + 1) * NP] for i in range(4))
        ring = sb("ring", [P, RING, PIECE], U8)
        ring8 = ring[:, :, :].bitcast(F8).rearrange("p s (g h d) -> p s h g d", g=GC, h=NB)
        tmp = sb("tmp", [P, 11, CH], F32)
        keys = tmp[:, :, :].rearrange("p a b -> p (a b)").bitcast(F16)[:, 0:6 * NW].rearrange("p (q w two) -> p q w two", q=3, two=2)
        cntT = sb("cntT", [KT, NP], F32)
        row = sb("row", [P, NT], F32)
        deg_nm = sb("deg_nm", [P, NB], F32)
        rdeg_nm = sb("rdeg_nm", [P, NB], F32)
        dis_nm = sb("dis_nm", [P, NB], F32)
        st = sb("st", [P, 4, NB], F32)
        small = sb("small", [P, 8, WG], F32)
        small_i = sb("small_i", [P, 2, WG], I32)
        cnt8 = sb("cnt8", [WP, WG, WD * KT], F32)
        rowmax = sb("rowmax", [P, NG + 2], F32)
        fl = sb("fl", [P, 8], F32)
        flag_i = sb("flag_i", [1, 1], I32)
        rf_i = sb("rf_i", [1, ER], I32)
        rf = sb("rf", [1, ER], F32)
        rfb = sb("rfb", [P, ER], F32)
        pad_i = sb("pad_i", [1, CAP], I32)
        wl1 = sb("wl1", [D, 2 * D], F32)
        wr1 = sb("wr1", [D, 2 * D], F32)
        wl2 = sb("wl2", [D, 2, D], F32)
        wr2 = sb("wr2", [D, 2, D], F32)
        w1 = sb("w1", [D, D], F32)
        w2 = sb("w2", [D, D], F32)
        WT = sb("WT", [D, 14, D], F32)
        ET, IH, HH, IW, JW, W3 = 0, 4, 7, 10, 12, 13
        bet = sb("bet", [KT, D], F32)
        bcol = sb("bcol", [D, 9], F32)
        brz = sb("brz", [D, 2], F32)
        brow = sb("brow", [1, 5, D], F32)
        BL2, BI, BJ, B2, B3 = range(5)
        raww = hn[:, :, :].rearrange("p a b -> p (a b)")[:, 0:14 * D].rearrange("p (w d) -> p w d", w=14)
        e_dst, e_src, e_typ = (T[0:ER, i * EC:(i + 1) * EC].bitcast(I32) for i in range(3))
        rows_i = [T[0:WP, (3 + i) * EC:(4 + i) * EC].bitcast(I32) for i in range(4)]
        rows_f = T[0:WP, 7 * EC:8 * EC]
        junk = T[0:WP, 8 * EC:9 * EC]
        WA = WG * CAP
        wa = [T[0:WP, i * WA:(i + 1) * WA] for i in range(7)]
        ring_b = ring[:, :, :].rearrange("p s b -> p (s b)")
        OHB = GW * OHW * 2
        oh = ring_b[:, 0:2 * OHB].bitcast(F16).rearrange("p (s w c) -> p s w c", s=2, c=OHW)
        SB = (KT + 1) * NB * GD
        stage = ring_b[:, 2 * OHB:2 * OHB + 2 * SB].rearrange("p (s b) -> p s b", s=2)
        stage8 = stage.bitcast(F8).rearrange("p s (c d) -> p s c d", d=GD)

        at = [0]

        def carve(cols, dt, rows=P):
            size = cols * (2 if dt == F16 else 4)
            at[0] += size
            return ring_b[0:rows, at[0] - size:at[0]].bitcast(dt)

        g_out = carve(NT, F32)
        g_iota = carve(NT, F32, ER)
        g_hot = carve(NT, F16, ER)
        g_src, g_dst, g_typ = (carve(EC, I32, ER) for _ in range(3))
        g_x = carve(3 * D, F16, ER)
        g_idx = carve(1, I32, ER)
        g_thot = carve(KT, F16, ER)
        g_zero = carve(CH, F16)
        g_key = tmp[0:ER, 0:2, :].rearrange("p a b -> p (a b)")[:, 0:EC]
        ringf = ring[:, :, 0:4 * CH].bitcast(F32)

        ps = ctx.enter_context(nc.psum_tensor("ps", [P, 8, 512], F32))

        adj_w = adj.rearrange("k c p (g b) -> p k c g b", g=GC)
        NSTEP = 3

        block = ctx.enter_context(nc.Block())

        @block.sync
        def _(sp):
            def gate(sem, value):
                sp.wait_ge(sem, value)
                sp.sem_inc(S("sp_passed"), 1)

            for t, name in ((e_dst, "dst"), (e_src, "src"), (e_typ, "edge_type_4")):
                sp.dma_start(t, a[name].rearrange("(r c) -> r c", c=EC)).then_inc(S("edges_in"), 16)
            sp.dma_start(rf_i[:, :], a["dst"].rearrange("(o r c) -> o r c", o=1, c=EC)[:, :, 0]).then_inc(S("heads_in"), 16)
            sp.wait_ge(S("pack_ready"), 1)
            sp.wait_ge(S("pad"), 1)
            sp.dma_start(packed[0:E].rearrange("(r c) -> r c", c=EC), e_dst).then_inc(S("packed_out"), 16)
            sp.dma_start(packed[E:E + CAP].rearrange("(o c) -> o c", o=1), pad_i[:, :]).then_inc(S("packed_out"), 16)
            sp.sem_inc(S("stage_free0"), 1)
            sp.sem_inc(S("stage_free1"), 1)
            with sp.Fori(0, NCH) as c:
                with sp.Fori(0, GC // 2) as j:
                    it = c * (GC // 2) + j
                    for s in range(2):
                        gate(S(f"stage_ready{s}"), it * GQ + GQ)
                        dst = adj_w[:, :, bass.ds(c, 1), bass.ds(j * 2 + s, 1), :]
                        sp.dma_start(dst, stage[:, s, :].rearrange("p (k c g b) -> p k c g b", k=KT + 1, c=1, g=1)
                                     ).then_inc(S(f"stage_out{s}"), 16)
                    for s in range(2):
                        sp.wait_ge(S(f"stage_out{s}"), it * 16 + 16)
                        sp.sem_inc(S(f"stage_free{s}"), 1)

            sp.wait_ge(S("flag"), 1)
            fast = sp.value_load(flag_i[:, :], min_val=0, max_val=1)

            def general(name, ready, types=1):
                with sp.If(fast < 1):
                    for sem, n in ready:
                        sp.wait_ge(S(sem), n)
                    call = GCALL.index(name)
                    if name != "count":
                        sp.dma_start(table.rearrange("(b p) f -> p b f", p=P), op[:, :, :, :].rearrange("p b r d -> p b (r d)")
                                     ).then_inc(S("g_table"), 16)
                    for t, e in ((g_src, "src"), (g_dst, "dst"), (g_typ, "edge_type_4")):
                        sp.dma_start(t, a[e].rearrange("(r c) -> r c", c=EC)).then_inc(S("g_edges"), 16)
                    if name != "count":
                        sp.wait_ge(S("g_table"), 16 * call)
                        sp.sem_inc(S("g_rows"), 1)
                        for k in range(types):
                            sp.wait_ge(S("g_evac"), GP[name] + k + 1)
                            sp.dma_start(sums[k].rearrange("c p d -> p c d"), g_out.rearrange("p (c d) -> p c d", d=CH)
                                         ).then_inc(S("g_sums"), 16)
                            sp.wait_ge(S("g_sums"), 16 * (GP[name] + k))

            def piece(k, c, slot, sem):
                with sp.If(fast > 0):
                    sp.dma_start(ring[:, slot:slot + 1, :], adj[k, c].rearrange("c p b -> p c b")).then_inc(S(sem), 16)
                with sp.Else():
                    sp.dma_start(ringf[:, slot:slot + 1, :], sums[k % KT, c].rearrange("c p d -> p c d")).then_inc(S(sem), 16)

            general("count", [("stage_free0", NG // 2 + 1), ("stage_free1", NG // 2 + 1)])

            def untyped(name):
                def load(c, s, n):
                    gate(S(f"ag_mm{s}"), n)
                    piece(UNTYPED, c, s, f"ag_piece{s}")
                n0, n1 = AGG[name] * (NCH // 2 + 1), AGG[name] * (NCH // 2)
                with sp.Fori(0, NCH // 2) as i:
                    load(bass.ds(i * 2, 1), 0, i + n0 + 1)
                    load(bass.ds(i * 2 + 1, 1), 1, i + n1 + 1)
                load(slice(NCH - 1, NCH), 0, n0 + NCH // 2 + 1)

            def typed(step):
                with sp.Fori(0, NCH) as c:
                    for k in range(KT):
                        gate(S(f"ty_mm{k}"), c + step * NCH + 1)
                        piece(k, bass.ds(c, 1), k, f"ty_piece{k}")

            for s in range(2):
                sp.sem_inc(S(f"ag_mm{s}"), 1)
            for k in range(KT):
                sp.sem_inc(S(f"ty_mm{k}"), 1)
            general("l0a", [("ln_op", 1)])
            untyped("l0a")
            general("l0b", [("blk_used", NQ)])
            untyped("l0b")
            sp.wait_ge(S("ag_mm0"), 1 + 2 * (NCH // 2 + 1))
            sp.wait_ge(S("ag_mm1"), 1 + 2 * (NCH // 2))
            for step in range(NSTEP):
                general(f"l1s{step}", [("ln_op", 2), ("tr_copied", (step + 2) * NQ)] +
                        [(f"ty_mm{k}", 1 + step * NCH) for k in range(KT)], KT)
                typed(step)
            for k in range(2):
                sp.wait_ge(S(f"ty_mm{k}"), 1 + NSTEP * NCH)
            general("l2a", [("ln_op", 3)])
            untyped("l2a")
            general("l2b", [("l2p_op", 1)])
            untyped("l2b")
            general("l3a", [("ln_op", 4)])
            untyped("l3a")

            sp.wait_ge(S("l3_out"), NQ)
            sp.dma_start(out[0:(NB - 1) * P, :].rearrange("(b p) d -> p b d", p=P), x_nm[:, 0:NB - 1, :]).then_inc(S("stored"), 16)
            sp.dma_start(out[(NB - 1) * P:N, :], x_nm[0:NLAST, NB - 1, :]).then_inc(S("stored"), 16)
            sp.wait_ge(S("stored"), 32)

        @block.gpsimd
        def _(pool):
            g = nc.gpsimd
            g.iota(iota_i[:, :], [[1, CELL]], base=0, channel_multiplier=0).then_inc(S("consts"), 1)
            g.iota(pad_i[:, :], [[1, CAP]], base=4095 << 14, channel_multiplier=0).then_inc(S("pad"), 1)
            g.iota(wbase_i[:, :], [[WD * WP, WG]], base=0, channel_multiplier=WD).then_inc(S("consts"), 1)
            g.memset(ident[:, :], 0.0).then_inc(S("ident_zero"), 1)
            pool.wait_ge(S("ident_zero"), 1)
            g.affine_select(out=ident[:, :], in_=ident[:, :], compare_op=ALU.not_equal, fill=1.0, base=0,
                            pattern=[[-1, P]], channel_multiplier=1).then_inc(S("ident"), 1)
            pool.wait_ge(S("rowidx"), 1)
            for w in range(WG):
                if w >= 4:
                    pool.wait_ge(S("row_used"), w - 3)
                pool.indirect_dma_start(out=rows_i[w % 4], out_offset=None, in_=a["dst"].rearrange("(r c) -> r c", c=EC),
                                        in_offset=bass.IndirectOffsetOnAxis(ap=small_i[0:WP, 0, w:w + 1], axis=0)
                                        ).then_inc(S(f"row_in{w % 4}"), 16)
            pool.wait_ge(S("startidx"), 1)
            pool.wait_ge(S("packed_out"), 32)
            for w in range(WG):
                pool.indirect_dma_start(out=wa[0][:, w * CAP:(w + 1) * CAP].bitcast(I32), out_offset=None,
                                        in_=packed.rearrange("(e o) -> e o", o=1),
                                        in_offset=bass.IndirectOffsetOnAxis(ap=small_i[0:WP, 1, w:w + 1], axis=0)
                                        ).then_inc(S("windows_in"), 16)

            pool.wait_ge(S("flag"), 1)
            fast = pool.value_load(flag_i[:, :], min_val=0, max_val=1)
            with pool.If(fast < 1):
                for name, first in GP.items():
                    pool.wait_ge(S("g_edges"), 48 * (GCALL.index(name) + 1))
                    g.iota(g_iota.bitcast(I32), [[1, NT]], base=0, channel_multiplier=0).then_inc(S("g_iota"), 1)
                    if name == "count":
                        continue
                    pool.wait_ge(S("g_rows"), GCALL.index(name))
                    for k in range(KT if name.startswith("l1") else 1):
                        with pool.Fori(0, EC) as e:
                            pool.wait_ge(S("g_idx"), e + (first + k) * EC + 1)
                            pool.sem_inc(S("pool_passed"), 1)
                            pool.indirect_dma_start(out=g_x, out_offset=None, in_=table,
                                                    in_offset=bass.IndirectOffsetOnAxis(ap=g_idx, axis=0)
                                                    ).then_inc(S(f"g_x{(first + k - 1) // GX}"), 16)

        @block.tensor
        def _(pe):
            mm = nc.tensor.matmul

            pe.wait_ge(S("heads"), 1)
            pe.wait_ge(S("ones"), 1)
            mm(ps[:, 0, 0:ER], ones[0:1, :], rf[:, :], start=True, stop=True).then_inc(S("heads_mm"), 1)

            pe.wait_ge(S("ident"), 1)
            pe.wait_ge(S("raw_in"), 16 * 6)
            for q in range(4):
                if q >= 2:
                    pe.wait_ge(S("wt_copied"), q - 1)
                js = range(4 * q, min(4 * q + 4, 14))
                for j in js:
                    t = nc.tensor.transpose(ps[:, 1 + q % 2, (j % 4) * P:(j % 4 + 1) * P], raww[:, j, :], ident[:, :])
                t.then_inc(S("wt"), 1)

            pe.wait_ge(S("cnt8"), 1)
            for q in range(8):
                d, g0 = q // 4, 4 * (q % 4)
                if q >= 2:
                    pe.wait_ge(S("cnt_copied"), q - 1)
                for g in range(g0, min(g0 + 4, WG)):
                    t = nc.tensor.transpose(ps[0:KT, 3 + q % 2, (g - g0) * WP:(g - g0 + 1) * WP],
                                            cnt8[:, g, d * KT:(d + 1) * KT], ident[0:WP, 0:WP])
                t.then_inc(S("cnt_t"), 1)

            pe.wait_ge(S("codes"), 1)
            for q in range(12):
                kq, g0 = q // 4, 4 * (q % 4)
                if q >= 2:
                    pe.wait_ge(S("keys"), q - 1)
                for g in range(g0, min(g0 + 4, WG)):
                    t = nc.tensor.transpose(ps[:, 5 + q % 2, (g - g0) * WP:(g - g0 + 1) * WP],
                                            wa[kq][:, g * CAP:(g + 1) * CAP], ident[0:WP, 0:WP])
                t.then_inc(S("keys_t"), 1)
            pe.wait_ge(S("keys"), 12)
            pe.wait_ge(S("cnt_copied"), 8)
            pe.wait_ge(S("wt_copied"), 4)
            pe.wait_ge(S("heads_copied"), 1)

            with pe.Fori(0, NG // 2) as i:
                for s in range(2):
                    pe.wait_ge(S("oh_ready"), i * 2 + s + 1)
                    for w in range(GW):
                        q = w // QW
                        if w % QW == 0:
                            pe.wait_ge(S(f"quad_free{q % 2}"), i * GQ + s * (GQ // 2) + q // 2 + 1)
                        at = w % QW % 2 * 256
                        mm(ps[:, q % 2 * 2 + w % QW // 2, at:at + CELL], oh[:, s, w, 0:P], oh[:, s, w, P:OHW],
                           start=True, stop=True)
                        t = mm(ps[:, 6 + s, w:w + 1], oh[:, s, w, 0:P], ones16[:, 0:1], start=True, stop=True)
                        if w % QW == QW - 1:
                            t.then_inc(S("quad_mm"), 1)

            pe.wait_ge(S("quads_done"), 1)
            pe.wait_ge(S("fl_a"), 1)
            mm(ps[0:1, 4, 0:1], fl[0:WP, 0:1], ones[0:WP, 0:1], start=True, stop=True)
            nc.tensor.transpose(ps[0:1, 4, 128:256], fl[:, 1:2], ident[:, :]).then_inc(S("fl_b"), 1)
            pe.wait_ge(S("flag"), 1)
            fast = pe.value_load(flag_i[:, :], min_val=0, max_val=1)

            def general(name, parts, f8view=None, types=1):
                with pe.If(fast < 1):
                    pe.wait_ge(S("g_zero"), GCALL.index(name) + 1)
                    for k in range(types):
                        n = GP[name] + k
                        rows = KT if name == "count" else P
                        for c in range(NCH):
                            mm(ps[0:rows, c, 0:CH], g_zero[:, 0:rows], g_zero[:, :], start=True, stop=False, skip_group_check=True)
                        with pe.Fori(0, EC) as e:
                            pe.wait_ge(S("g_hot"), e + n * EC + 1)
                            pe.sem_inc(S("pe_passed"), 1)
                            if name != "count":
                                pe.wait_ge(S(f"g_x{(n - 1) // GX}"), e * 16 + ((n - 1) % GX * EC + 1) * 16)
                                pe.sem_inc(S("pe_passed"), 1)
                            x = g_x.bitcast(f8view) if f8view is not None else g_x
                            for r in range(parts):
                                lhs = g_thot if name == "count" else x[:, r * D:(r + 1) * D]
                                for c in range(NCH):
                                    t = mm(ps[0:rows, c, 0:CH], lhs, g_hot[:, c * CH:(c + 1) * CH], start=False, stop=False,
                                           skip_group_check=True)
                            t.then_inc(S("g_mm"), 1)
                        pe.wait_ge(S("g_evac"), n + 1)

            general("count", 1)

            def degree_row(name):
                n0 = DEG[name] * NCH
                for c in range(NCH):
                    if n0 + c >= 2:
                        pe.wait_ge(S("deg_used"), n0 + c - 1)
                    mm(ps[:, 6 + c % 2, 0:CH], ones[0:KT, :], cntT[:, c * CH:(c + 1) * CH], start=True, stop=True
                       ).then_inc(S("deg_mm"), 1)

            degree_row("deg0")
            for b in range(NB):
                t = mm(ps[:, 5, b:b + 1], cntT[:, b * P:(b + 1) * P], ones[0:KT, 0:1], start=True, stop=True)
            t.then_inc(S("degn"), 1)
            def transposes(name, src, wait):
                wait()
                n0 = TR[name] * NQ
                for q in range(NQ):
                    if n0 + q >= 2:
                        pe.wait_ge(S("tr_copied"), n0 + q - 1)
                    for b in range(4 * q, min(4 * q + 4, NB)):
                        t = nc.tensor.transpose(ps[:, 6 + q % 2, (b % 4) * P:(b % 4 + 1) * P], src(b), ident[:, :])
                    t.then_inc(S("tr_mm"), 1)

            def accumulate(bank, slot, parts, src, sem):
                with pe.If(fast > 0):
                    for b in range(NB):
                        for r in range(parts):
                            t = mm(ps[:, bank, 0:CH].rearrange("p (g d) -> p g d", d=GD), src(b, r), ring8[:, slot, b],
                                   start=(b == 0 and r == 0), stop=(b == NB - 1 and r == parts - 1))
                    t.then_inc(S(sem), 1)
                with pe.Else():
                    mm(ps[:, bank, 0:CH], ident[:, :], ringf[:, slot, :], start=True, stop=True).then_inc(S(sem), 1)

            def gate(sem, value):
                pe.wait_ge(sem, value)
                pe.sem_inc(S("pe_passed"), 1)

            def untyped(name, parts, src, wait):
                wait()
                general(name, parts, BF16 if parts == 3 else None)
                turns = (AGG[name] * (NCH // 2 + 1), AGG[name] * (NCH // 2))

                def chunk(s, i):
                    gate(S(f"ag_piece{s}"), (i + turns[s] + 1) * 16)
                    gate(S(f"ag_bank{s}"), i + turns[s] + 1)
                    accumulate(s, s, parts, src, f"ag_mm{s}")
                with pe.Fori(0, NCH // 2) as i:
                    for s in range(2):
                        chunk(s, i)
                chunk(0, NCH // 2)

            def blocks(name, ready, terms, bank0=2):
                n0 = BLK[name] * NQ
                for q in range(NQ):
                    ready(q)
                    if n0 + q >= 2:
                        pe.wait_ge(S("blk_used"), n0 + q - 1)
                    for b in range(4 * q, min(4 * q + 4, NB)):
                        ts = terms(b)
                        for j, (l, r) in enumerate(ts):
                            t = mm(ps[:, bank0 + q % 2, (b % 4) * P:(b % 4 + 1) * P], l, r,
                                   start=(j == 0), stop=(j == len(ts) - 1))
                    t.then_inc(S("blk_mm"), 1)

            def once(*waits):
                def f(q=0):
                    if q == 0:
                        for s, v in waits:
                            pe.wait_ge(S(s), v)
                return f

            def blk(Tb):
                return lambda b: Tb[:, b * P:(b + 1) * P]

            f16 = lambda b, r: op[:, b, r, :]
            b16 = lambda b, r: opb[:, b, r, :]

            transposes("l0h", lambda b: hn[:, b, :], once(("ln_ln", 1), ("flag", 1), ("deg_used", NCH)))
            untyped("l0a", 2, f16, once(("ln_op", 1), ("tr_copied", NQ)))
            pe.wait_ge(S("ag_post"), NCH)
            pe.wait_ge(S("tr_copied"), NQ)
            with pe.Fori(0, NCH) as c:
                for m in range(2):
                    pe.wait_ge(S(f"l0d_bank{m}"), c + 1)
                    mm(ps[:, 2 + m, 0:CH], wl1[:, m * D:(m + 1) * D], T1[:, bass.ds(c * CH, CH)], start=True, stop=False)
                    mm(ps[:, 2 + m, 0:CH], wr1[:, m * D:(m + 1) * D], T0[:, bass.ds(c * CH, CH)], start=False, stop=True
                       ).then_inc(S("l0d"), 1)
            blocks("l0p", once(("l0d_copied", 2 * NCH)), lambda b: [(blk(T2)(b), wl2[:, 0, :]), (blk(T3)(b), wl2[:, 1, :])])
            untyped("l0b", 3, b16, once(("blk_used", NQ)))
            blocks("l0o", once(("ag_post", 2 * NCH)), lambda b: [
                (blk(T1)(b), ident[:, :]), (blk(T2)(b), wr2[:, 0, :]), (blk(T3)(b), wr2[:, 1, :]),
                (ones[0:1, :], brow[:, BL2, :])])

            degree_row("deg2")
            pe.wait_ge(S("deg_used"), 2 * NCH)
            transposes("l1h", lambda b: hn[:, b, :], once(("ln_ln", 2)))
            for step in range(NSTEP):
                pe.wait_ge(S("ln_op"), 2)
                pe.wait_ge(S("tr_copied"), (step + 2) * NQ)
                general(f"l1s{step}", 2, None, KT)
                with pe.Fori(0, NCH) as i:
                    c = i + step * NCH
                    for k in range(KT):
                        gate(S(f"ty_piece{k}"), c * 16 + 16)
                        gate(S(f"ty_bank{k % 2}"), c * 2 + k // 2 + 1)
                        accumulate(k % 2, k, 2, f16, f"ty_mm{k}")
                    mm(ps[:, 2, 0:CH], bet[:, :], cntT[:, bass.ds(i * CH, CH)], start=True, stop=False)
                    for k in range(KT):
                        pe.wait_ge(S("ty_sum"), c * KT + k + 1)
                        t = mm(ps[:, 2, 0:CH], WT[:, ET + k, :], tmp[:, k, :], start=False, stop=(k == KT - 1))
                    t.then_inc(S("gru_msg"), 1)
                    hc = T1[:, bass.ds(i * CH, CH)]
                    pe.wait_ge(S("gru_h"), c + 1)
                    mm(ps[:, 3, 0:CH], WT[:, HH + 0, :], hc, start=True, stop=False)
                    mm(ps[:, 4, 0:CH], WT[:, HH + 1, :], hc, start=True, stop=False)
                    mm(ps[:, 5, 0:CH], WT[:, HH + 2, :], hc, start=True, stop=True)
                    pe.wait_ge(S("gru_a"), c + 1)
                    mm(ps[:, 3, 0:CH], WT[:, IH + 0, :], tmp[:, 4, :], start=False, stop=True).then_inc(S("gru_mm"), 1)
                    mm(ps[:, 4, 0:CH], WT[:, IH + 1, :], tmp[:, 4, :], start=False, stop=True).then_inc(S("gru_mm"), 1)
                    mm(ps[:, 6, 0:CH], WT[:, IH + 2, :], tmp[:, 4, :], start=True, stop=True).then_inc(S("gru_mm"), 1)
                if step < NSTEP - 1:
                    transposes(f"l1t{step}", blk(T1), once(("gru_h", (step + 1) * NCH + 1)))
            pe.wait_ge(S("gru_h"), NSTEP * NCH + 1)
            for q in range(NQ):
                if q >= 2:
                    pe.wait_ge(S("l1o_used"), q - 1)
                for b in range(4 * q, min(4 * q + 4, NB)):
                    og = ps[:, 2 * (q % 2), (b % 4) * P:(b % 4 + 1) * P]
                    ov = ps[:, 2 * (q % 2) + 1, (b % 4) * P:(b % 4 + 1) * P]
                    mm(og, blk(T1)(b), WT[:, IW, :], start=True, stop=False)
                    mm(og, blk(T0)(b), WT[:, IW + 1, :], start=False, stop=False)
                    mm(og, ones[0:1, :], brow[:, BI, :], start=False, stop=True)
                    mm(ov, blk(T1)(b), WT[:, JW, :], start=True, stop=False)
                    t = mm(ov, ones[0:1, :], brow[:, BJ, :], start=False, stop=True)
                t.then_inc(S("l1o_mm"), 1)

            transposes("l2h", lambda b: hn[:, b, :], once(("ln_ln", 3)))
            untyped("l2a", 2, f16, once(("ln_op", 3), ("tr_copied", 5 * NQ)))
            pe.wait_ge(S("ag_post"), 3 * NCH)
            with pe.Fori(0, NCH) as c:
                pe.wait_ge(S("l2d_bank"), c + 1)
                mm(ps[:, 2, 0:CH], w1[:, :], T1[:, bass.ds(c * CH, CH)], start=True, stop=True).then_inc(S("l2d"), 1)
            blocks("l2p", once(("l2d_done", NCH)), lambda b: [(blk(T2)(b), w2[:, :])])
            untyped("l2b", 3, b16, once(("l2p_op", 1)))
            blocks("l2o", once(("ag_post", 4 * NCH)), lambda b: [(blk(T1)(b), ident[:, :]), (ones[0:1, :], brow[:, B2, :])])

            degree_row("deg3")
            untyped("l3a", 2, f16, once(("ln_op", 4), ("deg_used", 3 * NCH)))
            blocks("l3o", once(("ag_post", 5 * NCH)), lambda b: [(blk(T1)(b), WT[:, W3, :]), (ones[0:1, :], brow[:, B3, :])])

        @block.scalar
        def _(act):
            A = nc.scalar.activation
            act.dma_start(x_nm[:, 0:NB - 1, :], a["x"][0:(NB - 1) * P, :].rearrange("(b p) d -> p b d", p=P)).then_inc(S("x_in"), 16)
            raw = [("L1_gnn_W_et", lambda w: w.rearrange("k o d -> o k d"), 0, 4),
                   ("L1_gnn_W_ih", lambda w: w.rearrange("(g o) d -> o g d", o=D), 4, 7),
                   ("L1_gnn_W_hh", lambda w: w.rearrange("(g o) d -> o g d", o=D), 7, 10),
                   ("L1_gnn_i_w", lambda w: w.rearrange("g (h d) -> g h d", d=D), 10, 12)]
            for name, f, lo, hi in raw:
                act.dma_start(raww[:, lo:hi, :], f(a[name])).then_inc(S("raw_in"), 16)
            act.dma_start(raww[:, 12, :], a["L1_gnn_j_w"]).then_inc(S("raw_in"), 16)
            act.dma_start(raww[:, 13, :], a["L3_gnn_W"]).then_inc(S("raw_in"), 16)
            act.dma_start(wl1[:, :], a["L0_gnn_W_l1"]).then_inc(S("w_in"), 16)
            act.dma_start(wr1[:, :], a["L0_gnn_W_r1"]).then_inc(S("w_in"), 16)
            act.dma_start(wl2[:, :, :], a["L0_gnn_W_l2"].rearrange("(h d) o -> d h o", d=D)).then_inc(S("w_in"), 16)
            act.dma_start(wr2[:, :, :], a["L0_gnn_W_r2"].rearrange("(h d) o -> d h o", d=D)).then_inc(S("w_in"), 16)
            act.dma_start(w1[:, :], a["L2_gnn_W1"]).then_inc(S("w_in"), 16)
            act.dma_start(w2[:, :], a["L2_gnn_W2"]).then_inc(S("w_in"), 16)
            act.dma_start(bet[:, :], a["L1_gnn_b_et"]).then_inc(S("w_in"), 16)
            for name, lo, n in (("L0_gnn_b_l1", 0, 2), ("L1_gnn_b_ih", 2, 3), ("L1_gnn_b_hh", 5, 3), ("L2_gnn_b1", 8, 1)):
                act.dma_start(bcol[:, lo:lo + n], a[name].rearrange("(g o) -> o g", o=D)).then_inc(S("w_in"), 16)
            for i, name in enumerate(("L0_gnn_b_l2", "L1_gnn_i_b", "L1_gnn_j_b", "L2_gnn_b2", "L3_gnn_b")):
                act.dma_start(brow[:, i, :], a[name].rearrange("(o d) -> o d", o=1)).then_inc(S("w_in"), 16)
            act.wait_ge(S("x_pad"), 1)
            act.dma_start(x_nm[0:NLAST, NB - 1, :], a["x"][(NB - 1) * P:N, :]).then_inc(S("x_in"), 16)

            for q in range(4):
                act.wait_ge(S("wt"), q + 1)
                n = min(4, 14 - 4 * q)
                A(WT[:, 4 * q:4 * q + n, :].rearrange("p a b -> p (a b)"), ps[:, 1 + q % 2, 0:n * P], ACT.Copy).then_inc(S("wt_copied"), 1)
            act.wait_ge(S("cnt_pad"), 1)
            for q in range(8):
                d, g0 = q // 4, 4 * (q % 4)
                n = min(4, WG - g0)
                act.wait_ge(S("cnt_t"), q + 1)
                dst = cntT[:, g0 * WP * WD:(g0 + n) * WP * WD].rearrange("k (w d) -> k w d", d=WD)[:, :, d]
                A(dst, ps[0:KT, 3 + q % 2, 0:n * WP], ACT.Copy).then_inc(S("cnt_copied"), 1)
            act.wait_ge(S("w_in"), 16 * 16)
            for q in range(12):
                kq, g0 = q // 4, 4 * (q % 4)
                n = min(4, WG - g0)
                act.wait_ge(S("keys_t"), q + 1)
                A(keys[:, kq, g0 * WP:(g0 + n) * WP, :], ps[:, 5 + q % 2, 0:n * WP].unsqueeze(2).broadcast_to([P, n * WP, 2]),
                  ACT.Copy).then_inc(S("keys"), 1)

            for b in range(2):
                act.sem_inc(S(f"quad_free{b}"), 1)
            with act.Fori(0, NG // 2) as i:
                for s in range(2):
                    act.wait_ge(S(f"stage_free{s}"), i + 1)
                    act.sem_inc(S("act_passed"), 1)
                    for q in range(GQ):
                        act.wait_ge(S("quad_mm"), i * (2 * GQ) + s * GQ + q + 1 + 2 * GQ)
                        act.sem_inc(S("act_passed"), 1)
                        src = ps[:, q % 2 * 2:q % 2 * 2 + 2, :].rearrange("p b (h c) -> p (b h) c", h=2)[:, :, 0:CELL]
                        src = src.rearrange("p w (c d) -> p c w d", d=WD)
                        dst = stage8[:, s, :, QW * WD * q:QW * WD * (q + 1)].rearrange("p c (w d) -> p c w d", w=QW)
                        A(dst, src, ACT.Copy, saturate=False).then_inc(S(f"stage_ready{s}"), 1)
                        act.wait_ge(S(f"stage_ready{s}"), i * GQ + q + 1)
                        act.sem_inc(S(f"quad_free{q % 2}"), 1)
            act.sem_inc(S("quads_done"), 1)

            act.wait_ge(S("degn"), 1)
            A(dis_nm[:, :], ps[:, 5, 0:NB], ACT.Sqrt, bias=ones[:, 0:1]).then_inc(S("degn_root"), 1)

            def layernorm(name):
                n = LN[name] + 1
                act.wait_ge(S("ln_centred"), n)
                A(T3, hn[:, :, :].rearrange("p a b -> p (a b)"), ACT.Square).then_inc(S("ln_squared"), 1)
                act.wait_ge(S("ln_var"), n)
                A(st[:, 2, :], st[:, 1, :], ACT.Sqrt, bias=epsc[:, 0:1], scale=1.0 / D).then_inc(S("ln_std"), 1)

            def copy_blocks(name, dst):
                for q in range(NQ):
                    n = min(4, NB - 4 * q) * P
                    act.wait_ge(S("tr_mm"), TR[name] * NQ + q + 1)
                    A(dst(q, n), ps[:, 6 + q % 2, 0:n], ACT.Copy).then_inc(S("tr_copied"), 1)

            cols = lambda Tb: (lambda q, n: Tb[:, 4 * q * P:4 * q * P + n])

            layernorm("l0")
            copy_blocks("l0h", cols(T0))
            for m in range(2):
                act.sem_inc(S(f"l0d_bank{m}"), 1)
            act.wait_ge(S("t_pads"), 1)
            with act.Fori(0, NCH) as c:
                for m in range(2):
                    act.wait_ge(S("l0d"), c * 2 + m + 1)
                    A((T2, T3)[m][:, bass.ds(c * CH, CH)], ps[:, 2 + m, 0:CH], ACT.Identity, bias=bcol[:, m:m + 1]
                      ).then_inc(S("l0d_copied"), 1)
                    act.wait_ge(S("l0d_copied"), c * 2 + m + 1)
                    act.sem_inc(S(f"l0d_bank{m}"), 1)

            for c in range(NCH):
                act.wait_ge(S("deg_mm"), NCH + c + 1)
                act.wait_ge(S("ag_post"), 2 * NCH)
                A(row[:, c * CH:(c + 1) * CH], ps[:, 6 + c % 2, 0:CH], ACT.Sqrt, bias=ones[:, 0:1]).then_inc(S("deg2_root"), 1)
            layernorm("l1")
            for q in range(NQ):
                n = min(4, NB - 4 * q) * P
                act.wait_ge(S("tr_mm"), TR["l1h"] * NQ + q + 1)
                A(T0[:, 4 * q * P:4 * q * P + n], ps[:, 6 + q % 2, 0:n], ACT.Copy)
                A(T1[:, 4 * q * P:4 * q * P + n], ps[:, 6 + q % 2, 0:n], ACT.Copy).then_inc(S("tr_copied"), 1)
            for step in range(NSTEP):
                with act.Fori(0, NCH) as i:
                    c = i + step * NCH
                    for k in range(KT):
                        act.wait_ge(S(f"ty_mm{k}"), c + 2)
                        A(tmp[:, k, :], ps[:, k % 2, 0:CH], ACT.Copy).then_inc(S("ty_sum"), 1)
                        act.wait_ge(S("ty_sum"), c * KT + k + 1)
                        act.sem_inc(S(f"ty_bank{k % 2}"), 1)
                    act.wait_ge(S("gru_msg"), c + 1)
                    A(tmp[:, 4, :], ps[:, 2, 0:CH], ACT.Copy).then_inc(S("gru_a"), 1)
                    act.wait_ge(S("gru_mm"), c * 3 + 1)
                    A(tmp[:, 5, :], ps[:, 3, 0:CH], ACT.Sigmoid, bias=brz[:, 0:1]).then_inc(S("gru_r"), 1)
                    act.wait_ge(S("gru_mm"), c * 3 + 2)
                    A(tmp[:, 6, :], ps[:, 4, 0:CH], ACT.Sigmoid, bias=brz[:, 1:2]).then_inc(S("gru_z"), 1)
                    act.wait_ge(S("gru_pre"), c + 1)
                    A(tmp[:, 8, :], tmp[:, 7, :], ACT.Tanh, bias=bcol[:, 4:5]).then_inc(S("gru_n"), 1)
                if step < NSTEP - 1:
                    for q in range(NQ):
                        n = min(4, NB - 4 * q)
                        act.wait_ge(S("tr_mm"), TR[f"l1t{step}"] * NQ + q + 1)
                        A(op[:, 4 * q:4 * q + n, 0, :], ps[:, 6 + q % 2, 0:n * P].rearrange("p (b d) -> p b d", d=D), ACT.Copy
                          ).then_inc(S("high"), 1)
            for q in range(NQ):
                n = min(4, NB - 4 * q) * P
                act.wait_ge(S("l1o_mm"), q + 1)
                if q >= 2:
                    act.wait_ge(S("l1o_used"), q - 1)
                A(tmp[:, 2 * (q % 2):2 * (q % 2) + 2, :].rearrange("p a b -> p (a b)")[:, 0:n], ps[:, 2 * (q % 2), 0:n], ACT.Sigmoid
                  ).then_inc(S("l1o_sig"), 1)

            layernorm("l2")
            copy_blocks("l2h", cols(T0))
            act.sem_inc(S("l2d_bank"), 1)
            with act.Fori(0, NCH) as c:
                act.wait_ge(S("l2d"), c + 1)
                A(T2[:, bass.ds(c * CH, CH)], ps[:, 2, 0:CH], ACT.Identity, bias=bcol[:, 8:9]).then_inc(S("l2d_bias"), 1)
                act.wait_ge(S("l2d_bias"), c + 1)
                act.sem_inc(S("l2d_bank"), 1)
            layernorm("l3")

        @block.vector
        def _(dve):
            v = nc.vector
            link = Chain(dve, S("dve_chain"))
            v.memset(ones[:, :], 1.0).then_inc(S("ones"), 1)
            link(v.memset(ones16[:, :], 1.0))
            link(v.memset(epsc[:, :], EPS))
            link(v.memset(op[:, :, 2, :], 0.0))
            v.memset(x_nm[:, NB - 1, :], 0.0).then_inc(S("x_pad"), 1)
            v.memset(cntT[:, :], 0.0).then_inc(S("cnt_pad"), 1)
            dve.wait_ge(S("consts"), 2)
            v.tensor_copy(iota16[:, :], iota_i[:, :])
            link(v.tensor_copy(wbase[:, :], wbase_i[:, :]))
            dve.wait_ge(S("heads_in"), 16)
            v.tensor_copy(rf[:, :], rf_i[:, :]).then_inc(S("heads"), 1)
            dve.wait_ge(S("edges_in"), 48)
            link(v.tensor_scalar(e_dst, e_dst, 14, None, ALU.logical_shift_left))
            link(v.tensor_scalar(e_typ, e_typ, 12, None, ALU.logical_shift_left))
            link(v.tensor_tensor(e_dst, e_dst, e_typ, ALU.bitwise_or))
            v.tensor_tensor(e_dst, e_dst, e_src, ALU.bitwise_or).then_inc(S("pack_ready"), 1)

            dve.wait_ge(S("heads_mm"), 1)
            v.tensor_copy(rfb[:, :], ps[:, 0, 0:ER]).then_inc(S("heads_copied"), 1)
            dve.wait_ge(S("heads_copied"), 1)
            for w in range(WG):
                t = v.tensor_scalar(junk[:, 0:ER], rfb[0:WP, :], wbase[:, w:w + 1], None, ALU.is_lt, ALU.add,
                                    accum_out=small[0:WP, 0, w:w + 1])
                link(t)
            link(v.tensor_scalar(small[0:WP, 1, :], small[0:WP, 0, :], -1.0, 0.0, ALU.add, ALU.max))
            v.tensor_copy(small_i[0:WP, 0, :], small[0:WP, 1, :]).then_inc(S("rowidx"), 1)
            for w in range(WG):
                dve.wait_ge(S(f"row_in{w % 4}"), 16 * (w // 4 + 1))
                v.tensor_copy(rows_f, rows_i[w % 4]).then_inc(S("row_used"), 1)
                dve.wait_ge(S("row_used"), w + 1)
                link(v.tensor_scalar(junk, rows_f, wbase[:, w:w + 1], None, ALU.is_lt, ALU.add,
                                     accum_out=small[0:WP, 2, w:w + 1]))
            link(v.scalar_tensor_tensor(out=small[0:WP, 3, :], in0=small[0:WP, 1, :], scalar=float(EC), in1=small[0:WP, 2, :],
                                        op0=ALU.mult, op1=ALU.add))
            v.tensor_copy(small_i[0:WP, 1, :], small[0:WP, 3, :]).then_inc(S("startidx"), 1)

            pk, lo, ct, cu, ty, rel, m = wa[0], wa[6], wa[1], wa[2], wa[3], wa[4], wa[5]
            I = lambda t: t.bitcast(I32)
            dve.wait_ge(S("windows_in"), 16 * WG)
            dve.wait_ge(S("packed_out"), 32)
            link(v.tensor_scalar(I(m), I(pk), 7, 31, ALU.logical_shift_right, ALU.bitwise_and))
            link(v.tensor_copy(cu, I(m)))
            link(v.tensor_scalar(I(m), I(pk), 12, 3, ALU.logical_shift_right, ALU.bitwise_and))
            link(v.tensor_copy(ty, I(m)))
            link(v.tensor_scalar(I(m), I(pk), 14, None, ALU.logical_shift_right))
            link(v.tensor_copy(rel, I(m)))
            r3 = lambda t: t.rearrange("p (g e) -> p g e", e=CAP)
            link(v.tensor_tensor(r3(rel), r3(rel), wbase[:, :].unsqueeze(2).broadcast_to([WP, WG, CAP]), ALU.subtract))
            link(v.tensor_scalar(I(m), I(pk), 127, None, ALU.bitwise_and))
            link(v.tensor_copy(lo, I(m)))
            link(v.tensor_copy(pk, lo))
            link(v.tensor_scalar(m, rel, 0.0, None, ALU.is_ge))
            link(v.scalar_tensor_tensor(out=m, in0=rel, scalar=float(WD), in1=m, op0=ALU.is_lt, op1=ALU.mult))
            link(v.tensor_reduce(fl[0:WP, 0:1], m, AX.X, ALU.add))
            link(v.scalar_tensor_tensor(out=cu, in0=cu, scalar=float(WD), in1=rel, op0=ALU.mult, op1=ALU.add))
            link(v.scalar_tensor_tensor(out=ct, in0=ty, scalar=float(NB * WD), in1=cu, op0=ALU.mult, op1=ALU.add))
            link(v.scalar_tensor_tensor(out=cu, in0=cu, scalar=1.0, in1=m, op0=ALU.add, op1=ALU.mult))
            link(v.scalar_tensor_tensor(out=ct, in0=ct, scalar=1.0, in1=m, op0=ALU.add, op1=ALU.mult))
            link(v.tensor_scalar(cu, cu, -1.0, None, ALU.add))
            link(v.tensor_scalar(ct, ct, -1.0, None, ALU.add))
            link(v.scalar_tensor_tensor(out=rel, in0=rel, scalar=float(KT), in1=ty, op0=ALU.mult, op1=ALU.add))
            link(v.scalar_tensor_tensor(out=rel, in0=rel, scalar=1.0, in1=m, op0=ALU.add, op1=ALU.mult))
            v.engine_nop().then_inc(S("codes"), 1)
            for j in range(WD * KT):
                link(v.tensor_scalar(ty, rel, float(j + 1), None, ALU.is_equal))
                link(v.tensor_reduce(cnt8[:, :, j], r3(ty), AX.X, ALU.add))
            v.engine_nop().then_inc(S("cnt8"), 1)

            dve.sem_inc(S("quad_mm"), 2 * GQ)
            dve.wait_ge(S("keys"), 12)
            for s in range(2):
                v.memset(ps[:, 6 + s, 0:GW], 0.0)
            def most(s, g):
                link(v.tensor_reduce(rowmax[:, g], ps[:, 6 + s, 0:GW], AX.X, ALU.max))
            link(v.memset(rowmax[:, :], 0.0))
            with dve.Fori(0, NG // 2) as i:
                link.enter(i, 2)
                for s in range(2):
                    dve.wait_ge(S("quad_mm"), i * (2 * GQ) + (s + 1) * GQ)
                    most(s, bass.ds(i * 2 + s, 1))
                    o = oh[:, s, :, :]
                    key = lambda q, n: keys[:, q, bass.ds(i * (2 * GW) + s * GW, GW), :].unsqueeze(2).broadcast_to([P, GW, n // 2, 2])
                    cols = lambda lo, n: o[:, :, lo:lo + n].rearrange("p w (c two) -> p w c two", two=2)
                    for q, lo, n in ((0, 0, P), (1, P, TCELL), (2, P + TCELL, CELL - TCELL)):
                        t = v.tensor_tensor(cols(lo, n), pairs(n), key(q, n), ALU.is_equal)
                    t.then_inc(S("oh_ready"), 1)
            link.leave(NG // 2)
            for s in range(2):
                dve.wait_ge(S("quad_mm"), NG * GQ + (s + 1) * GQ)
                most(s, slice(NG + s, NG + s + 1))
            v.tensor_reduce(fl[:, 1:2], rowmax[:, :], AX.X, ALU.max).then_inc(S("fl_a"), 1)

            dve.wait_ge(S("fl_b"), 1)
            link(v.tensor_scalar(fl[0:1, 2:3], ps[0:1, 4, 0:1], float(E), None, ALU.is_equal))
            link(v.tensor_reduce(fl[0:1, 3:4], ps[0:1, 4, 128:256], AX.X, ALU.max))
            link(v.tensor_scalar(fl[0:1, 4:5], fl[0:1, 3:4], float(MULT_MAX), None, ALU.is_le))
            link(v.tensor_tensor(fl[0:1, 5:6], fl[0:1, 2:3], fl[0:1, 4:5], ALU.mult))
            v.tensor_copy(flag_i[:, :], fl[0:1, 5:6]).then_inc(S("flag"), 1)
            dve.wait_ge(S("flag"), 1)
            fast = dve.value_load(flag_i[:, :], min_val=0, max_val=1)
            g_link = Chain(dve, S("g_chain"))

            def general(name, types=1):
                with dve.If(fast < 1):
                    dve.wait_ge(S("g_edges"), 48 * (GCALL.index(name) + 1))
                    dve.wait_ge(S("g_iota"), GCALL.index(name) + 1)
                    if name == "count":
                        dve.sem_inc(S("g_mm"), 1)
                    g_link(v.tensor_copy(g_iota, g_iota.bitcast(I32)))
                    g_link(v.tensor_copy(g_dst.bitcast(F32), g_dst))
                    g_link(v.tensor_copy(g_typ.bitcast(F32), g_typ))
                    v.memset(g_zero, 0.0).then_inc(S("g_zero"), 1)
                    for k in range(types):
                        n = GP[name] + k
                        if types > 1:
                            g_link(v.tensor_scalar(g_key, g_typ.bitcast(F32), float(k), 4096.0, ALU.not_equal, ALU.mult))
                            g_link(v.tensor_tensor(g_key, g_key, g_dst.bitcast(F32), ALU.add))
                        else:
                            g_link(v.tensor_copy(g_key, g_dst.bitcast(F32)))
                        with dve.Fori(0, EC) as e:
                            dve.wait_ge(S("g_mm"), e + n * EC + 1)
                            v.tensor_copy(g_idx, g_src[:, bass.ds(e, 1)]).then_inc(S("g_idx"), 1)
                            if name == "count":
                                v.tensor_scalar(g_thot, iota16[0:ER, 0:KT], g_typ.bitcast(F32)[:, bass.ds(e, 1)], None, ALU.is_equal)
                            v.tensor_scalar(g_hot, g_iota, g_key[:, bass.ds(e, 1)], None, ALU.is_equal).then_inc(S("g_hot"), 1)
                        dve.wait_ge(S("g_mm"), (n + 1) * EC + 1)
                        if n > 1:
                            dve.wait_ge(S("g_sums"), 16 * (n - 1))
                        for c in range(NCH):
                            if name == "count":
                                t = v.tensor_copy(cntT[:, c * CH:(c + 1) * CH], ps[0:KT, c, 0:CH])
                            else:
                                t = v.tensor_copy(g_out[:, c * CH:(c + 1) * CH], ps[:, c, 0:CH])
                        t.then_inc(S("g_evac"), 1)
                        dve.wait_ge(S("g_evac"), n + 1)

            general("count")

            def mean_row(name):
                n0 = DEG[name] * NCH
                for c in range(NCH):
                    cc = slice(c * CH, (c + 1) * CH)
                    dve.wait_ge(S("deg_mm"), n0 + c + 1)
                    v.tensor_scalar(row[:, cc], ps[:, 6 + c % 2, 0:CH], 1.0, None, ALU.max).then_inc(S("deg_used"), 1)
                    dve.wait_ge(S("deg_used"), n0 + c + 1)
                    link(v.reciprocal(row[:, cc], row[:, cc]))

            mean_row("deg0")
            dve.wait_ge(S("degn_root"), 1)
            link(v.tensor_scalar(deg_nm[:, :], ps[:, 5, 0:NB], 1.0, None, ALU.max))
            link(v.reciprocal(rdeg_nm[:, :], deg_nm[:, :]))
            link(v.reciprocal(dis_nm[:, :], dis_nm[:, :]))
            dve.wait_ge(S("w_in"), 16 * 16)
            link(v.tensor_tensor(brz[:, :], bcol[:, 2:4], bcol[:, 5:7], ALU.add))
            for Tb in (T0, T1, T2, T3):
                t = v.memset(Tb[:, NT:NP], 0.0)
            t.then_inc(S("t_pads"), 1)
            dve.wait_ge(S("t_pads"), 1)

            hn2 = hn[:, :, :].rearrange("p a b -> p (a b)")

            def wide(col):
                return col.unsqueeze(2).broadcast_to([P, NB, D])

            def layernorm(name, scale=None):
                link(v.tensor_reduce(st[:, 0, :], x_nm[:, :, :], AX.X, ALU.add))
                link(v.tensor_scalar(st[:, 0, :], st[:, 0, :], 1.0 / D, None, ALU.mult))
                v.tensor_tensor(hn[:, :, :], x_nm[:, :, :], wide(st[:, 0, :]), ALU.subtract).then_inc(S("ln_centred"), 1)
                dve.wait_ge(S("ln_squared"), LN[name] + 1)
                v.tensor_reduce(st[:, 1, :], T3.rearrange("p (a b) -> p a b", b=D), AX.X, ALU.add).then_inc(S("ln_var"), 1)
                dve.wait_ge(S("ln_std"), LN[name] + 1)
                link(v.reciprocal(st[:, 3, :], st[:, 2, :]))
                link(v.tensor_tensor(hn[:, :, :], hn[:, :, :], wide(st[:, 3, :]), ALU.mult))
                t = v.tensor_scalar(hn2, hn2, 0.0, None, ALU.max)
                if scale is not None:
                    link(t)
                    t = v.tensor_tensor(hn[:, :, :], hn[:, :, :], wide(scale), ALU.mult)
                t.then_inc(S("ln_ln"), 1)
                dve.wait_ge(S("ln_ln"), LN[name] + 1)
                link(v.tensor_copy(op[:, :, 0, :], hn[:, :, :]))
                v.tensor_tensor(op[:, :, 1, :], hn[:, :, :], op[:, :, 0, :], ALU.subtract).then_inc(S("ln_op"), 1)

            def post(name, row, add=None):
                general(name)
                at = AGG[name] * NCH

                turns = (AGG[name] * (NCH // 2 + 1), AGG[name] * (NCH // 2))

                def chunk(s, i, c):
                    n = c + at + 1
                    dve.wait_ge(S(f"ag_mm{s}"), i + turns[s] + 2)
                    cc = bass.ds(c * CH, CH)
                    if add is None:
                        t = v.tensor_tensor(T1[:, cc], ps[:, s, 0:CH], row[:, cc], ALU.mult)
                    else:
                        v.tensor_tensor(T1[:, cc], ps[:, s, 0:CH], add[:, cc], ALU.add).then_inc(S("self_loop"), 1)
                        dve.wait_ge(S("self_loop"), c + 1)
                        t = v.tensor_tensor(T1[:, cc], T1[:, cc], row[:, cc], ALU.mult)
                    t.then_inc(S("ag_post"), 1)
                    dve.wait_ge(S("ag_post"), n)
                    dve.sem_inc(S(f"ag_bank{s}"), 1)
                with dve.Fori(0, NCH // 2) as i:
                    for s in range(2):
                        chunk(s, i, i * 2 + s)
                chunk(0, NCH // 2, NCH - 1)

            def split3(b0, n, q3):
                o = lambda r: opb[:, b0:b0 + n, r, :]
                h = hn[:, b0:b0 + n, :]
                link(v.tensor_copy(o(0), q3))
                link(v.tensor_tensor(h, q3, o(0), ALU.subtract))
                link(v.tensor_copy(o(1), h))
                return v.tensor_tensor(o(2), h, o(1), ALU.subtract)

            def quads(name, f):
                for q in range(NQ):
                    n = min(4, NB - 4 * q)
                    dve.wait_ge(S("blk_mm"), BLK[name] * NQ + q + 1)
                    f(q, n, 4 * q, ps[:, 2 + q % 2, 0:n * P].rearrange("p (b d) -> p b d", d=D)).then_inc(S("blk_used"), 1)
                    dve.wait_ge(S("blk_used"), BLK[name] * NQ + q + 1)

            add_x = lambda q, n, b0, p3: v.tensor_tensor(x_nm[:, b0:b0 + n, :], x_nm[:, b0:b0 + n, :], p3, ALU.add)

            for s in range(2):
                dve.sem_inc(S(f"ag_bank{s}"), 1)
                dve.sem_inc(S(f"ty_bank{s}"), 1)
            dve.sem_inc(S("gru_h"), 1)
            dve.wait_ge(S("x_in"), 32)
            dve.wait_ge(S("wt_copied"), 4)
            layernorm("l0")
            post("l0a", row)
            quads("l0p", lambda q, n, b0, p3: split3(b0, n, p3))
            post("l0b", row)
            quads("l0o", add_x)

            for c in range(NCH):
                dve.wait_ge(S("deg2_root"), c + 1)
                v.reciprocal(row[:, c * CH:(c + 1) * CH], row[:, c * CH:(c + 1) * CH]).then_inc(S("deg_used"), 1)

            layernorm("l1")
            dve.wait_ge(S("tr_copied"), (TR["l1h"] + 1) * NQ)
            for step in range(NSTEP):
                general(f"l1s{step}", KT)
                with dve.Fori(0, NCH) as i:
                    link.enter(i, 4)
                    c = i + step * NCH
                    hc = T1[:, bass.ds(i * CH, CH)]
                    pre, nt, zs, rs = tmp[:, 7, :], tmp[:, 8, :], tmp[:, 6, :], tmp[:, 5, :]
                    t1, t2 = tmp[:, 9, :], tmp[:, 10, :]
                    dve.wait_ge(S("gru_r"), c + 1)
                    link(v.scalar_tensor_tensor(out=t1, in0=ps[:, 5, 0:CH], scalar=bcol[:, 7:8], in1=rs, op0=ALU.add, op1=ALU.mult))
                    dve.wait_ge(S("gru_mm"), c * 3 + 3)
                    v.tensor_tensor(pre, t1, ps[:, 6, 0:CH], ALU.add).then_inc(S("gru_pre"), 1)
                    dve.wait_ge(S("gru_n"), c + 1)
                    link(v.tensor_tensor(t2, hc, nt, ALU.subtract))
                    dve.wait_ge(S("gru_z"), c + 1)
                    link(v.tensor_tensor(t2, t2, zs, ALU.mult))
                    link(v.tensor_tensor(hc, t2, nt, ALU.add))
                    dve.sem_inc(S("gru_h"), 1)
                link.leave(NCH)
                if step < NSTEP - 1:
                    for q in range(NQ):
                        n = min(4, NB - 4 * q)
                        dve.wait_ge(S("high"), step * NQ + q + 1)
                        v.tensor_tensor(op[:, 4 * q:4 * q + n, 1, :], ps[:, 6 + q % 2, 0:n * P].rearrange("p (b d) -> p b d", d=D),
                                        op[:, 4 * q:4 * q + n, 0, :], ALU.subtract).then_inc(S("tr_copied"), 1)
            for q in range(NQ):
                n = min(4, NB - 4 * q)
                sig = tmp[:, 2 * (q % 2):2 * (q % 2) + 2, :].rearrange("p a b -> p (a b)")[:, 0:n * P]
                dve.wait_ge(S("l1o_sig"), q + 1)
                link(v.tensor_tensor(sig, sig, ps[:, 2 * (q % 2) + 1, 0:n * P], ALU.mult))
                v.tensor_tensor(x_nm[:, 4 * q:4 * q + n, :], x_nm[:, 4 * q:4 * q + n, :], sig.rearrange("p (b d) -> p b d", d=D),
                                ALU.add).then_inc(S("l1o_used"), 1)
                dve.wait_ge(S("l1o_used"), q + 1)

            layernorm("l2", dis_nm[:, :])
            dve.wait_ge(S("tr_copied"), (TR["l2h"] + 1) * NQ)
            post("l2a", row, T0)
            with dve.Fori(0, NCH) as c:
                cc = bass.ds(c * CH, CH)
                dve.wait_ge(S("l2d_bias"), c + 1)
                v.scalar_tensor_tensor(out=T2[:, cc], in0=T2[:, cc], scalar=0.01, in1=T2[:, cc], op0=ALU.mult, op1=ALU.max
                                       ).then_inc(S("l2d_done"), 1)
            quads("l2p", lambda q, n, b0, p3: v.tensor_tensor(
                hn[:, b0:b0 + n, :], p3, dis_nm[:, b0:b0 + n].unsqueeze(2).broadcast_to([P, n, D]), ALU.mult))
            T3b = T3.rearrange("p (a b) -> p a b", b=D)
            link(v.tensor_tensor(T3b, hn[:, :, :], wide(dis_nm[:, :]), ALU.mult))
            link(v.tensor_tensor(x_nm[:, :, :], x_nm[:, :, :], T3b, ALU.add))
            link(v.tensor_copy(opb[:, :, 0, :], hn[:, :, :]))
            link(v.tensor_tensor(T3b, hn[:, :, :], opb[:, :, 0, :], ALU.subtract))
            link(v.tensor_copy(opb[:, :, 1, :], T3b))
            v.tensor_tensor(opb[:, :, 2, :], T3b, opb[:, :, 1, :], ALU.subtract).then_inc(S("l2p_op"), 1)
            dve.wait_ge(S("l2p_op"), 1)
            post("l2b", row)
            quads("l2o", add_x)

            mean_row("deg3")
            layernorm("l3", rdeg_nm[:, :])
            post("l3a", row)
            for q in range(NQ):
                n = min(4, NB - 4 * q)
                dve.wait_ge(S("blk_mm"), BLK["l3o"] * NQ + q + 1)
                add_x(q, n, 4 * q, ps[:, 2 + q % 2, 0:n * P].rearrange("p (b d) -> p b d", d=D)).then_inc(S("blk_used"), 1)
                dve.wait_ge(S("blk_used"), BLK["l3o"] * NQ + q + 1)
                dve.sem_inc(S("l3_out"), 1)


INPUTS = ["x", "src", "dst", "edge_type_4", "L0_gnn_W_l1", "L0_gnn_b_l1", "L0_gnn_W_r1", "L0_gnn_W_l2", "L0_gnn_b_l2",
          "L0_gnn_W_r2", "L1_gnn_W_et", "L1_gnn_b_et", "L1_gnn_W_ih", "L1_gnn_b_ih", "L1_gnn_W_hh", "L1_gnn_b_hh",
          "L1_gnn_i_w", "L1_gnn_i_b", "L1_gnn_j_w", "L1_gnn_j_b", "L2_gnn_W1", "L2_gnn_b1", "L2_gnn_W2", "L2_gnn_b2",
          "L3_gnn_W", "L3_gnn_b"]


def kernel(**inputs):
    import numpy as _np
    import concourse.bacc as _bacc
    from concourse import mybir as _mybir
    from concourse.bass_utils import run_bass_kernel_spmd as _run

    nc = _bacc.Bacc("TRN2", target_bir_lowering=False, num_devices=1)
    arrays, aps = {}, {}
    for name in INPUTS:
        arr = _np.ascontiguousarray(inputs[name])
        arrays[f"in_{name}"] = arr
        aps[name] = nc.dram_tensor(f"in_{name}", arr.shape, _mybir.dt.from_np(arr.dtype), kind="ExternalInput").ap()
    out = nc.dram_tensor("out_0", (N, D), _mybir.dt.float32, kind="ExternalOutput").ap()
    packed = nc.dram_tensor("packed_edges", (E + CAP,), _mybir.dt.int32, kind="Internal").ap()
    adj = nc.dram_tensor("adjacency", (KT + 1, NCH, P, PIECE), _mybir.dt.uint8, kind="Internal").ap()
    table = nc.dram_tensor("operand_rows", (NP, 3 * D), _mybir.dt.float16, kind="Internal").ap()
    sums = nc.dram_tensor("general_sums", (KT, NCH, P, CH), _mybir.dt.float32, kind="Internal").ap()
    build(nc, aps, out, packed, adj, table, sums)
    r = _run(nc, [arrays], core_ids=[0])
    return r.results[0]["out_0"]
```

```python
from contextlib import ExitStack

import concourse.bass as bass
from concourse import mybir

ALU = mybir.AluOpType
ACT = mybir.ActivationFunctionType
AX = mybir.AxisListType
F32, F16 = mybir.dt.float32, mybir.dt.float16
I32, U8, F8 = mybir.dt.int32, mybir.dt.uint8, mybir.dt.float8e4

P = 128
N = 3125
D = 128
E = 100000
KT = 4
NB = (N + P - 1) // P
NLAST = N - (NB - 1) * P
CH = 448
NCH = (N + CH - 1) // CH
NT = NCH * CH
NP = NB * P
ER, EC = 125, 800
WD = 2
NW = NT // WD
WP = 112
WG = NW // WP
CAP = 128
CELL = (KT + 1) * NB * WD
TCELL = KT * NB * WD
GD = 32
GW = GD // WD
NG = NT // GD
GC = CH // GD
SS = GC // 2
PIECE = NB * CH
EPS = 1e-5
OHW = P + CELL
QW = 4
GQ = GW // QW
RING = 4
UNTYPED = KT
NQ = NB // 4 + 1
AGG = {"l0a": 0, "l0b": 1, "l2a": 2, "l2b": 3, "l3a": 4}
BLK = {"l0p": 0, "l0o": 1, "l2p": 2, "l2o": 3, "l3o": 4}
TR = {"l0h": 0, "l1h": 1, "l1t0": 2, "l1t1": 3, "l2h": 4}
DEG = {"deg0": 0, "deg3": 1}
LN = {"l0": 0, "l1": 1, "l2": 2, "l3": 3}
GP = {"count": 0, "l0a": 1, "l0b": 2, "l1s0": 3, "l1s1": 7, "l1s2": 11, "l2a": 15, "l2b": 16, "l3a": 17}
GCALL = list(GP)
GX = 5
HALVES = ((0, 12), (12, NB))
MULT_MAX = 16


class Chain:

    def __init__(self, eng, sem):
        self.eng, self.sem, self.n, self.i, self.m = eng, sem, 0, None, 0

    def __call__(self, ins):
        self.n += 1
        ins.then_inc(self.sem, 1)
        at = self.n if self.i is None else self.i * self.m + self.n
        self.eng.wait_ge(self.sem, at)

    def enter(self, i, m):
        self.i, self.m, self.start = i, m, self.n

    def leave(self, trips):
        assert self.n - self.start == self.m, (self.n - self.start, self.m)
        self.n, self.i = self.start + trips * self.m, None


def build(nc, a, out, packed, adj, table, sums):
    ctx = ExitStack()
    with ctx:
        def sb(name, shape, dt):
            return ctx.enter_context(nc.sbuf_tensor(name, shape, dt))

        sems = {}

        def S(name):
            if name not in sems:
                sems[name] = ctx.enter_context(nc.semaphore(name))
            return sems[name]

        ctx.enter_context(nc.allow_non_contiguous_dma(reason="small bias columns and row heads"))

        ident = sb("ident", [P, P], F32)
        ones = sb("ones", [P, P], F32)
        ones16 = sb("ones16", [P, 2], F16)
        epsc = sb("epsc", [P, 1], F32)
        iota_i = sb("iota_i", [P, CELL], I32)
        iota16 = sb("iota16", [P, CELL], F16)
        pairs = lambda n: iota16[:, 0:n].rearrange("p (c two) -> p c two", two=2).unsqueeze(1).broadcast_to([P, GW, n // 2, 2])
        wbase_i = sb("wbase_i", [WP, WG], I32)
        wbase = sb("wbase", [WP, WG], F32)

        x_nm = sb("x_nm", [P, NB, D], F32)
        hn = sb("hn", [P, NB, D], F32)
        op = sb("op", [P, NB, 2, D], F16)
        T = sb("T", [P, 4 * NP], F32)
        T0, T1, T2, T3 = (T[:, i * NP:(i + 1) * NP] for i in range(4))
        ring = sb("ring", [P, RING, PIECE], U8)
        ring8 = ring[:, :, :].bitcast(F8).rearrange("p s (g h d) -> p s h g d", g=GC, h=NB)
        tmp = sb("tmp", [P, 11, CH], F32)
        squares = tmp[:, :, :].rearrange("p a b -> p (a b)")[:, 0:NP]
        keys = tmp[:, :, :].rearrange("p a b -> p (a b)").bitcast(F16)[:, 0:6 * NW].rearrange("p (q w two) -> p q w two", q=3, two=2)
        cntT = sb("cntT", [KT, NP], F32)
        row = sb("row", [P, NT], F32)
        deg_nm = sb("deg_nm", [P, NB], F32)
        rdeg_nm = sb("rdeg_nm", [P, NB], F32)
        dis_nm = sb("dis_nm", [P, NB], F32)
        st = sb("st", [P, 4, NB], F32)
        small = sb("small", [P, 8, WG], F32)
        small_i = sb("small_i", [P, 2, WG], I32)
        cnt8 = sb("cnt8", [WP, WG, WD * KT], F32)
        rowmax = sb("rowmax", [P, NG + 2], F32)
        fl = sb("fl", [P, 8], F32)
        most_q = sb("most_q", [P, NQ + 1], F32)
        sc = sb("sc", [P, 4], F32)
        biasb = sb("biasb", [P, 5, D], F32)
        flag_i = sb("flag_i", [1, 1], I32)
        rf_i = sb("rf_i", [1, ER], I32)
        rf = sb("rf", [1, ER], F32)
        rfb = sb("rfb", [P, ER], F32)
        pad_i = sb("pad_i", [1, CAP], I32)
        wl1 = sb("wl1", [D, 2 * D], F32)
        wr1 = sb("wr1", [D, 2 * D], F32)
        wl2 = sb("wl2", [D, 2, D], F32)
        wr2 = sb("wr2", [D, 2, D], F32)
        w1 = sb("w1", [D, D], F32)
        w2 = sb("w2", [D, D], F32)
        WT = sb("WT", [D, 14, D], F32)
        ET, IH, HH, IW, JW, W3 = 0, 4, 7, 10, 12, 13
        bet = sb("bet", [KT, D], F32)
        bcol = sb("bcol", [D, 9], F32)
        brz = sb("brz", [D, 2], F32)
        brow = sb("brow", [1, 5, D], F32)
        BL2, BI, BJ, B2, B3 = range(5)
        raww = hn[:, :, :].rearrange("p a b -> p (a b)")[:, 0:14 * D].rearrange("p (w d) -> p w d", w=14)
        e_dst, e_src, e_typ = (T[0:ER, i * EC:(i + 1) * EC].bitcast(I32) for i in range(3))
        rows_i = [T[0:WP, (3 + i) * EC:(4 + i) * EC].bitcast(I32) for i in range(4)]
        rows_f = T[0:WP, 7 * EC:8 * EC]
        junk = T[0:WP, 8 * EC:9 * EC]
        WA = WG * CAP
        wa = [T[0:WP, i * WA:(i + 1) * WA] for i in range(7)]
        ring_b = ring[:, :, :].rearrange("p s b -> p (s b)")
        OHB = GW * OHW * 2
        oh = ring_b[:, 0:2 * OHB].bitcast(F16).rearrange("p (s w c) -> p s w c", s=2, c=OHW)
        SB = (KT + 1) * NB * GD
        row_b = row[:, :].bitcast(U8)
        stage = [ring_b[:, 2 * OHB + z * SB:2 * OHB + (z + 1) * SB] if 2 * OHB + (z + 1) * SB <= RING * PIECE else
                 row_b[:, (SS - 1 - z) * SB:(SS - z) * SB] for z in range(SS)]
        stage8 = [z.bitcast(F8).rearrange("p (c d) -> p c d", d=GD) for z in stage]

        at = [0]

        def carve(cols, dt, rows=P):
            size = cols * (2 if dt == F16 else 4)
            at[0] += size
            return ring_b[0:rows, at[0] - size:at[0]].bitcast(dt)

        g_out = carve(NT, F32)
        g_iota = carve(NT, F32, ER)
        g_hot = carve(NT, F16, ER)
        g_src, g_dst, g_typ = (carve(EC, I32, ER) for _ in range(3))
        g_x = carve(2 * D, F16, ER)
        g_idx = carve(1, I32, ER)
        g_thot = carve(KT, F16, ER)
        g_zero = carve(CH, F16)
        g_key = tmp[0:ER, 0:2, :].rearrange("p a b -> p (a b)")[:, 0:EC]
        ringf = ring[:, :, 0:4 * CH].bitcast(F32)

        ps = ctx.enter_context(nc.psum_tensor("ps", [P, 8, 512], F32))

        adj_w = adj.rearrange("k c p (g b) -> p k c g b", g=GC)
        NSTEP = 3

        block = ctx.enter_context(nc.Block())

        @block.sync
        def _(sp):
            def gate(sem, value):
                sp.wait_ge(sem, value)
                sp.sem_inc(S("sp_passed"), 1)

            for t, name in ((e_dst, "dst"), (e_src, "src"), (e_typ, "edge_type_4")):
                sp.dma_start(t, a[name].rearrange("(r c) -> r c", c=EC)).then_inc(S("edges_in"), 16)
            sp.dma_start(rf_i[:, :], a["dst"].rearrange("(o r c) -> o r c", o=1, c=EC)[:, :, 0]).then_inc(S("heads_in"), 16)
            sp.wait_ge(S("pack_ready"), 1)
            sp.wait_ge(S("pad"), 1)
            sp.dma_start(packed[0:E].rearrange("(r c) -> r c", c=EC), e_dst).then_inc(S("packed_out"), 16)
            sp.dma_start(packed[E:E + CAP].rearrange("(o c) -> o c", o=1), pad_i[:, :]).then_inc(S("packed_out"), 16)
            for z in range(SS):
                sp.sem_inc(S(f"stage_out{z}"), 16)
            with sp.Fori(0, NCH) as c:
                for g in range(GC):
                    gate(S("stage_ready"), c * (GC * GQ) + (g + 1) * GQ + 2)
                    dst = adj_w[:, :, bass.ds(c, 1), g:g + 1, :]
                    sp.dma_start(dst, stage[g % SS].rearrange("p (k c g b) -> p k c g b", k=KT + 1, c=1, g=1)
                                 ).then_inc(S(f"stage_out{g % SS}"), 16)
            for z in range(SS):
                sp.wait_ge(S(f"stage_out{z}"), 16 * (NCH * GC // SS + 1))
            sp.sem_inc(S("adjacency_out"), 1)

            sp.wait_ge(S("flag"), 1)
            fast = sp.value_load(flag_i[:, :], min_val=0, max_val=1)

            def general(name, ready, types=1):
                with sp.If(fast < 1):
                    for sem, n in ready:
                        sp.wait_ge(S(sem), n)
                    call = GCALL.index(name)
                    if name != "count":
                        sp.dma_start(table.rearrange("(b p) f -> p b f", p=P), op[:, :, :, :].rearrange("p b r d -> p b (r d)")
                                     ).then_inc(S("g_table"), 16)
                    for t, e in ((g_src, "src"), (g_dst, "dst"), (g_typ, "edge_type_4")):
                        sp.dma_start(t, a[e].rearrange("(r c) -> r c", c=EC)).then_inc(S("g_edges"), 16)
                    if name != "count":
                        sp.wait_ge(S("g_table"), 16 * call)
                        sp.sem_inc(S("g_rows"), 1)
                        for k in range(types):
                            sp.wait_ge(S("g_evac"), GP[name] + k + 1)
                            sp.dma_start(sums[k].rearrange("c p d -> p c d"), g_out.rearrange("p (c d) -> p c d", d=CH)
                                         ).then_inc(S("g_sums"), 16)
                            sp.wait_ge(S("g_sums"), 16 * (GP[name] + k))

            def piece(k, c, slot, sem):
                with sp.If(fast > 0):
                    sp.dma_start(ring[:, slot:slot + 1, :], adj[k, c].rearrange("c p b -> p c b")).then_inc(S(sem), 16)
                with sp.Else():
                    sp.dma_start(ringf[:, slot:slot + 1, :], sums[k % KT, c].rearrange("c p d -> p c d")).then_inc(S(sem), 16)

            general("count", [("adjacency_out", 1)])

            def untyped(name):
                def load(c, s, n):
                    gate(S(f"ag_mm{s}"), n)
                    piece(UNTYPED, c, s, f"ag_piece{s}")
                n0, n1 = AGG[name] * (NCH // 2 + 1), AGG[name] * (NCH // 2)
                with sp.Fori(0, NCH // 2) as i:
                    load(bass.ds(i * 2, 1), 0, i + n0 + 1)
                    load(bass.ds(i * 2 + 1, 1), 1, i + n1 + 1)
                load(slice(NCH - 1, NCH), 0, n0 + NCH // 2 + 1)

            def typed(step):
                with sp.Fori(0, NCH) as c:
                    for k in range(KT):
                        gate(S(f"ty_mm{k}"), c + step * NCH + 1)
                        piece(k, bass.ds(c, 1), k, f"ty_piece{k}")

            for s in range(2):
                sp.sem_inc(S(f"ag_mm{s}"), 1)
            for k in range(KT):
                sp.sem_inc(S(f"ty_mm{k}"), 1)
            general("l0a", [("ln_op", 2), ("deg_used", NCH)])
            untyped("l0a")
            general("l0b", [("q_op", 2)])
            untyped("l0b")
            sp.wait_ge(S("ag_mm0"), 1 + 2 * (NCH // 2 + 1))
            sp.wait_ge(S("ag_mm1"), 1 + 2 * (NCH // 2))
            for step in range(NSTEP):
                general(f"l1s{step}", [("ln_op", 4), ("tr_copied", (step + 2) * NQ)] +
                        [(f"ty_mm{k}", 1 + step * NCH) for k in range(KT)], KT)
                typed(step)
            for k in range(2):
                sp.wait_ge(S(f"ty_mm{k}"), 1 + NSTEP * NCH)
            general("l2a", [("ln_op", 6)])
            untyped("l2a")
            general("l2b", [("q_op", 4)])
            untyped("l2b")
            general("l3a", [("ln_op", 8)])
            untyped("l3a")

            sp.wait_ge(S("l3_out"), NQ)
            sp.dma_start(out[0:(NB - 1) * P, :].rearrange("(b p) d -> p b d", p=P), x_nm[:, 0:NB - 1, :]).then_inc(S("stored"), 16)
            sp.dma_start(out[(NB - 1) * P:N, :], x_nm[0:NLAST, NB - 1, :]).then_inc(S("stored"), 16)
            sp.wait_ge(S("stored"), 32)

        @block.gpsimd
        def _(pool):
            g = nc.gpsimd
            g.iota(iota_i[:, :], [[1, CELL]], base=0, channel_multiplier=0).then_inc(S("consts"), 1)
            g.iota(pad_i[:, :], [[1, CAP]], base=4095 << 14, channel_multiplier=0).then_inc(S("pad"), 1)
            g.iota(wbase_i[:, :], [[WD * WP, WG]], base=0, channel_multiplier=WD).then_inc(S("consts"), 1)
            g.memset(ident[:, :], 0.0).then_inc(S("ident_zero"), 1)
            pool.wait_ge(S("ident_zero"), 1)
            g.affine_select(out=ident[:, :], in_=ident[:, :], compare_op=ALU.not_equal, fill=1.0, base=0,
                            pattern=[[-1, P]], channel_multiplier=1).then_inc(S("ident"), 1)
            pool.wait_ge(S("rowidx"), 1)
            for w in range(WG):
                if w >= 4:
                    pool.wait_ge(S("row_used"), w - 3)
                pool.indirect_dma_start(out=rows_i[w % 4], out_offset=None, in_=a["dst"].rearrange("(r c) -> r c", c=EC),
                                        in_offset=bass.IndirectOffsetOnAxis(ap=small_i[0:WP, 0, w:w + 1], axis=0)
                                        ).then_inc(S(f"row_in{w % 4}"), 16)
            pool.wait_ge(S("startidx"), 1)
            pool.wait_ge(S("packed_out"), 32)
            for w in range(WG):
                pool.indirect_dma_start(out=wa[0][:, w * CAP:(w + 1) * CAP].bitcast(I32), out_offset=None,
                                        in_=packed.rearrange("(e o) -> e o", o=1),
                                        in_offset=bass.IndirectOffsetOnAxis(ap=small_i[0:WP, 1, w:w + 1], axis=0)
                                        ).then_inc(S("windows_in"), 16)

            pool_link = Chain(pool, S("pool_chain"))
            pool.wait_ge(S("codes"), 1)
            for j in range(WD * KT):
                pool_link(g.tensor_scalar(wa[3], wa[4], float(j + 1), None, ALU.is_equal))
                half, hit = CAP // 2, wa[3].rearrange("p (g e) -> p g e", e=CAP)
                while half >= 1:
                    dst = hit[:, :, 0:half] if half > 1 else cnt8[:, :, j:j + 1]
                    pool_link(g.tensor_tensor(dst, hit[:, :, 0:half], hit[:, :, half:2 * half], ALU.add))
                    half //= 2
            pool.sem_inc(S("cnt8"), 1)

            pool.wait_ge(S("flag"), 1)
            fast = pool.value_load(flag_i[:, :], min_val=0, max_val=1)
            with pool.If(fast < 1):
                for name, first in GP.items():
                    pool.wait_ge(S("g_edges"), 48 * (GCALL.index(name) + 1))
                    g.iota(g_iota.bitcast(I32), [[1, NT]], base=0, channel_multiplier=0).then_inc(S("g_iota"), 1)
                    if name == "count":
                        continue
                    pool.wait_ge(S("g_rows"), GCALL.index(name))
                    for k in range(KT if name.startswith("l1") else 1):
                        with pool.Fori(0, EC) as e:
                            pool.wait_ge(S("g_idx"), e + (first + k) * EC + 1)
                            pool.sem_inc(S("pool_passed"), 1)
                            pool.indirect_dma_start(out=g_x, out_offset=None, in_=table,
                                                    in_offset=bass.IndirectOffsetOnAxis(ap=g_idx, axis=0)
                                                    ).then_inc(S(f"g_x{(first + k - 1) // GX}"), 16)

        @block.tensor
        def _(pe):
            mm = nc.tensor.matmul

            def transposes(name, src, wait):
                wait()
                n0 = TR[name] * NQ
                for q in range(NQ):
                    if n0 + q >= 2:
                        pe.wait_ge(S("tr_copied"), n0 + q - 1)
                    for b in range(4 * q, min(4 * q + 4, NB)):
                        t = nc.tensor.transpose(ps[:, 6 + q % 2, (b % 4) * P:(b % 4 + 1) * P], src(b), ident[:, :])
                    t.then_inc(S("tr_mm"), 1)

            def once(*waits):
                def f(q=0):
                    if q == 0:
                        for s, v in waits:
                            pe.wait_ge(S(s), v)
                return f

            pe.wait_ge(S("heads"), 1)
            pe.wait_ge(S("ones"), 1)
            mm(ps[:, 0, 0:ER], ones[0:1, :], rf[:, :], start=True, stop=True).then_inc(S("heads_mm"), 1)

            pe.wait_ge(S("ident"), 1)
            pe.wait_ge(S("raw_in"), 16 * 6)
            for q in range(4):
                if q >= 2:
                    pe.wait_ge(S("wt_copied"), q - 1)
                js = range(4 * q, min(4 * q + 4, 14))
                for j in js:
                    t = nc.tensor.transpose(ps[:, 1 + q % 2, (j % 4) * P:(j % 4 + 1) * P], raww[:, j, :], ident[:, :])
                t.then_inc(S("wt"), 1)

            pe.wait_ge(S("brow_in"), 80)
            mm(ps[:, 3, 0:4 * D], ones[0:1, :], brow[:, 0:4, :].rearrange("o a b -> o (a b)"), start=True, stop=True)
            mm(ps[:, 4, 0:D], ones[0:1, :], brow[:, 4, :], start=True, stop=True).then_inc(S("bias_mm"), 1)

            pe.wait_ge(S("codes"), 1)
            for q in range(12):
                kq, g0 = q // 4, 4 * (q % 4)
                if q >= 2:
                    pe.wait_ge(S("keys"), q - 1)
                for g in range(g0, min(g0 + 4, WG)):
                    t = nc.tensor.transpose(ps[:, 5 + q % 2, (g - g0) * WP:(g - g0 + 1) * WP],
                                            wa[kq][:, g * CAP:(g + 1) * CAP], ident[0:WP, 0:WP])
                t.then_inc(S("keys_t"), 1)
            pe.wait_ge(S("keys"), 12)
            pe.wait_ge(S("wt_copied"), 4)
            pe.wait_ge(S("heads_copied"), 1)

            transposes("l0h", lambda b: hn[:, b, :], once(("ln_ln", 2)))

            with pe.Fori(0, NCH) as i:
                for gr in range(GC):
                    s = gr % 2
                    pe.wait_ge(S("oh_ready"), i * GC + gr + 1)
                    for w in range(GW):
                        q = w // QW
                        if w % QW == 0:
                            pe.wait_ge(S("stage_ready"), i * (GC * GQ) + gr * GQ + q + 1)
                        at = w % QW % 2 * 256
                        mm(ps[:, q % 2 * 2 + w % QW // 2, at:at + CELL], oh[:, s, w, 0:P], oh[:, s, w, P:OHW],
                           start=True, stop=True)
                        t = mm(ps[:, 6 + s, w:w + 1], oh[:, s, w, 0:P], ones16[:, 0:1], start=True, stop=True)
                        if w % QW == QW - 1:
                            t.then_inc(S("quad_mm"), 1)

            pe.wait_ge(S("cnt8"), 1)
            pe.wait_ge(S("quads_done"), 1)
            for q in range(8):
                d, g0 = q // 4, 4 * (q % 4)
                if q >= 2:
                    pe.wait_ge(S("cnt_copied"), q - 1)
                for g in range(g0, min(g0 + 4, WG)):
                    t = nc.tensor.transpose(ps[0:KT, 3 + q % 2, (g - g0) * WP:(g - g0 + 1) * WP],
                                            cnt8[:, g, d * KT:(d + 1) * KT], ident[0:WP, 0:WP])
                t.then_inc(S("cnt_t"), 1)

            pe.wait_ge(S("cnt_copied"), 8)
            pe.wait_ge(S("fl_a"), 1)
            mm(ps[0:1, 5, 0:1], fl[0:WP, 0:1], ones[0:WP, 0:1], start=True, stop=True)
            nc.tensor.transpose(ps[0:1, 5, 128:256], fl[:, 1:2], ident[:, :]).then_inc(S("fl_b"), 1)
            pe.wait_ge(S("flag"), 1)
            fast = pe.value_load(flag_i[:, :], min_val=0, max_val=1)

            def general(name, parts, types=1):
                with pe.If(fast < 1):
                    pe.wait_ge(S("g_zero"), GCALL.index(name) + 1)
                    for k in range(types):
                        n = GP[name] + k
                        rows = KT if name == "count" else P
                        for c in range(NCH):
                            mm(ps[0:rows, c, 0:CH], g_zero[:, 0:rows], g_zero[:, :], start=True, stop=False, skip_group_check=True)
                        with pe.Fori(0, EC) as e:
                            pe.wait_ge(S("g_hot"), e + n * EC + 1)
                            pe.sem_inc(S("pe_passed"), 1)
                            if name != "count":
                                pe.wait_ge(S(f"g_x{(n - 1) // GX}"), e * 16 + ((n - 1) % GX * EC + 1) * 16)
                                pe.sem_inc(S("pe_passed"), 1)
                            for r in range(parts):
                                lhs = g_thot if name == "count" else g_x[:, r * D:(r + 1) * D]
                                for c in range(NCH):
                                    t = mm(ps[0:rows, c, 0:CH], lhs, g_hot[:, c * CH:(c + 1) * CH], start=False, stop=False,
                                           skip_group_check=True)
                            t.then_inc(S("g_mm"), 1)
                        pe.wait_ge(S("g_evac"), n + 1)

            general("count", 1)

            def degree_row(n0, used):
                for c in range(NCH):
                    if n0 + c >= 2:
                        pe.wait_ge(S(used), n0 + c - 1)
                    mm(ps[:, 6 + c % 2, 0:CH], ones[0:KT, :], cntT[:, c * CH:(c + 1) * CH], start=True, stop=True
                       ).then_inc(S("deg_mm"), 1)

            degree_row(0, "deg_used")
            for b in range(NB):
                t = mm(ps[:, 5, b:b + 1], cntT[:, b * P:(b + 1) * P], ones[0:KT, 0:1], start=True, stop=True)
            t.then_inc(S("degn"), 1)
            def accumulate(bank, slot, sem):
                with pe.If(fast > 0):
                    for b in range(NB):
                        for r in range(2):
                            t = mm(ps[:, bank, 0:CH].rearrange("p (g d) -> p g d", d=GD), op[:, b, r, :], ring8[:, slot, b],
                                   start=(b == 0 and r == 0), stop=(b == NB - 1 and r == 1))
                    t.then_inc(S(sem), 1)
                with pe.Else():
                    mm(ps[:, bank, 0:CH], ident[:, :], ringf[:, slot, :], start=True, stop=True).then_inc(S(sem), 1)

            def gate(sem, value):
                pe.wait_ge(sem, value)
                pe.sem_inc(S("pe_passed"), 1)

            def untyped(name, wait):
                wait()
                general(name, 2)
                turns = (AGG[name] * (NCH // 2 + 1), AGG[name] * (NCH // 2))

                def chunk(s, i):
                    gate(S(f"ag_piece{s}"), (i + turns[s] + 1) * 16)
                    gate(S(f"ag_bank{s}"), i + turns[s] + 1)
                    accumulate(s, s, f"ag_mm{s}")
                with pe.Fori(0, NCH // 2) as i:
                    for s in range(2):
                        chunk(s, i)
                chunk(0, NCH // 2)

            def blocks(name, ready, terms, bank0=2):
                n0 = BLK[name] * NQ
                for q in range(NQ):
                    ready(q)
                    if n0 + q >= 2:
                        pe.wait_ge(S("blk_used"), n0 + q - 1)
                    for b in range(4 * q, min(4 * q + 4, NB)):
                        ts = terms(b)
                        for j, (l, r) in enumerate(ts):
                            t = mm(ps[:, bank0 + q % 2, (b % 4) * P:(b % 4 + 1) * P], l, r,
                                   start=(j == 0), stop=(j == len(ts) - 1))
                    t.then_inc(S("blk_mm"), 1)

            def blk(Tb):
                return lambda b: Tb[:, b * P:(b + 1) * P]

            def largest(name, use):
                pe.wait_ge(S("scale_in"), 2 * use + 1)
                nc.tensor.transpose(ps[0:1, 4, 0:P], sc[:, 0:1], ident[:, :]).then_inc(S("scale_mm"), 1)
                pe.wait_ge(S("scale_in"), 2 * use + 2)
                mm(ps[:, 4, P:P + 1], ones[0:1, :], sc[0:1, 1:2], start=True, stop=True).then_inc(S("scale_mm"), 1)

            untyped("l0a", once(("ln_op", 2), ("tr_copied", NQ)))
            pe.wait_ge(S("ag_post"), NCH)
            pe.wait_ge(S("tr_copied"), NQ)
            with pe.Fori(0, NCH) as c:
                for m in range(2):
                    pe.wait_ge(S(f"l0d_bank{m}"), c + 1)
                    mm(ps[:, 2 + m, 0:CH], wl1[:, m * D:(m + 1) * D], T1[:, bass.ds(c * CH, CH)], start=True, stop=False)
                    mm(ps[:, 2 + m, 0:CH], wr1[:, m * D:(m + 1) * D], T0[:, bass.ds(c * CH, CH)], start=False, stop=True
                       ).then_inc(S("l0d"), 1)
            blocks("l0p", once(("l0d_copied", 2 * NCH)), lambda b: [(blk(T2)(b), wl2[:, 0, :]), (blk(T3)(b), wl2[:, 1, :])])
            largest("l0p", 0)
            untyped("l0b", once(("q_op", 2)))
            blocks("l0o", once(("ag_post", 2 * NCH)), lambda b: [
                (blk(T1)(b), ident[:, :]), (blk(T2)(b), wr2[:, 0, :]), (blk(T3)(b), wr2[:, 1, :])])

            pe.wait_ge(S("deg_used"), NCH)
            transposes("l1h", lambda b: hn[:, b, :], once(("ln_ln", 4)))
            pe.wait_ge(S("tr_copied"), 2 * NQ)
            degree_row(0, "deg2_root")
            pe.wait_ge(S("deg2_root"), NCH)
            degree_row(NCH, "deg_used")
            pe.wait_ge(S("deg_used"), 2 * NCH)
            for c in range(NCH):
                if c >= 2:
                    pe.wait_ge(S("msg_bias"), c - 1)
                mm(ps[:, 6 + c % 2, 0:CH], bet[:, :], cntT[:, c * CH:(c + 1) * CH], start=True, stop=True).then_inc(S("msg_bias_mm"), 1)
            pe.wait_ge(S("msg_bias"), NCH)
            for step in range(NSTEP):
                pe.wait_ge(S("ln_op"), 4)
                pe.wait_ge(S("tr_copied"), (step + 2) * NQ)
                general(f"l1s{step}", 2, KT)
                with pe.Fori(0, NCH) as i:
                    c = i + step * NCH
                    for k in range(KT):
                        gate(S(f"ty_piece{k}"), c * 16 + 16)
                        gate(S(f"ty_bank{k % 2}"), c * 2 + k // 2 + 1)
                        accumulate(k % 2, k, f"ty_mm{k}")
                    hc = T1[:, bass.ds(i * CH, CH)]
                    pe.wait_ge(S("gru_h"), c + 1)
                    mm(ps[:, 3, 0:CH], WT[:, HH + 0, :], hc, start=True, stop=False)
                    mm(ps[:, 4, 0:CH], WT[:, HH + 1, :], hc, start=True, stop=False)
                    mm(ps[:, 5, 0:CH], WT[:, HH + 2, :], hc, start=True, stop=True)
                    for k in range(KT):
                        pe.wait_ge(S("ty_sum"), c * KT + k + 1)
                        t = mm(ps[:, 2, 0:CH], WT[:, ET + k, :], tmp[:, k, :], start=(k == 0), stop=(k == KT - 1))
                    t.then_inc(S("gru_msg"), 1)
                    pe.wait_ge(S("gru_a"), c + 1)
                    mm(ps[:, 3, 0:CH], WT[:, IH + 0, :], tmp[:, 4, :], start=False, stop=True).then_inc(S("gru_mm"), 1)
                    mm(ps[:, 4, 0:CH], WT[:, IH + 1, :], tmp[:, 4, :], start=False, stop=True).then_inc(S("gru_mm"), 1)
                    mm(ps[:, 6, 0:CH], WT[:, IH + 2, :], tmp[:, 4, :], start=True, stop=True).then_inc(S("gru_mm"), 1)
                if step < NSTEP - 1:
                    transposes(f"l1t{step}", blk(T1), once(("gru_h", (step + 1) * NCH + 1)))
            pe.wait_ge(S("gru_h"), NSTEP * NCH + 1)
            for q in range(NQ):
                if q >= 2:
                    pe.wait_ge(S("l1o_used"), q - 1)
                for b in range(4 * q, min(4 * q + 4, NB)):
                    og = ps[:, 2 * (q % 2), (b % 4) * P:(b % 4 + 1) * P]
                    ov = ps[:, 2 * (q % 2) + 1, (b % 4) * P:(b % 4 + 1) * P]
                    mm(og, blk(T1)(b), WT[:, IW, :], start=True, stop=False)
                    mm(og, blk(T0)(b), WT[:, IW + 1, :], start=False, stop=False)
                    mm(og, ones[0:1, :], brow[:, BI, :], start=False, stop=True)
                    t = mm(ov, blk(T1)(b), WT[:, JW, :], start=True, stop=True)
                t.then_inc(S("l1o_mm"), 1)

            transposes("l2h", lambda b: hn[:, b, :], once(("ln_ln", 6)))
            untyped("l2a", once(("ln_op", 6), ("tr_copied", 5 * NQ)))
            pe.wait_ge(S("ag_post"), 3 * NCH)
            with pe.Fori(0, NCH) as c:
                pe.wait_ge(S("l2d_bank"), c + 1)
                mm(ps[:, 2, 0:CH], w1[:, :], T1[:, bass.ds(c * CH, CH)], start=True, stop=True).then_inc(S("l2d"), 1)
            blocks("l2p", once(("l2d_done", NCH)), lambda b: [(blk(T2)(b), w2[:, :])])
            largest("l2p", 1)
            untyped("l2b", once(("q_op", 4)))
            blocks("l2o", once(("ag_post", 4 * NCH)), lambda b: [(blk(T1)(b), ident[:, :])])

            untyped("l3a", once(("ln_op", 8)))
            blocks("l3o", once(("ag_post", 5 * NCH)), lambda b: [(blk(T1)(b), WT[:, W3, :])])

        @block.scalar
        def _(act):
            A = nc.scalar.activation
            act.dma_start(x_nm[:, 0:NB - 1, :], a["x"][0:(NB - 1) * P, :].rearrange("(b p) d -> p b d", p=P)).then_inc(S("x_in"), 16)
            raw = [("L1_gnn_W_et", lambda w: w.rearrange("k o d -> o k d"), 0, 4),
                   ("L1_gnn_W_ih", lambda w: w.rearrange("(g o) d -> o g d", o=D), 4, 7),
                   ("L1_gnn_W_hh", lambda w: w.rearrange("(g o) d -> o g d", o=D), 7, 10),
                   ("L1_gnn_i_w", lambda w: w.rearrange("g (h d) -> g h d", d=D), 10, 12)]
            for name, f, lo, hi in raw:
                act.dma_start(raww[:, lo:hi, :], f(a[name])).then_inc(S("raw_in"), 16)
            act.dma_start(raww[:, 12, :], a["L1_gnn_j_w"]).then_inc(S("raw_in"), 16)
            act.dma_start(raww[:, 13, :], a["L3_gnn_W"]).then_inc(S("raw_in"), 16)
            act.dma_start(wl1[:, :], a["L0_gnn_W_l1"]).then_inc(S("w_in"), 16)
            act.dma_start(wr1[:, :], a["L0_gnn_W_r1"]).then_inc(S("w_in"), 16)
            act.dma_start(wl2[:, :, :], a["L0_gnn_W_l2"].rearrange("(h d) o -> d h o", d=D)).then_inc(S("w_in"), 16)
            act.dma_start(wr2[:, :, :], a["L0_gnn_W_r2"].rearrange("(h d) o -> d h o", d=D)).then_inc(S("w_in"), 16)
            act.dma_start(w1[:, :], a["L2_gnn_W1"]).then_inc(S("w_in"), 16)
            act.dma_start(w2[:, :], a["L2_gnn_W2"]).then_inc(S("w_in"), 16)
            act.dma_start(bet[:, :], a["L1_gnn_b_et"]).then_inc(S("w_in"), 16)
            for name, lo, n in (("L0_gnn_b_l1", 0, 2), ("L1_gnn_b_ih", 2, 3), ("L1_gnn_b_hh", 5, 3), ("L2_gnn_b1", 8, 1)):
                act.dma_start(bcol[:, lo:lo + n], a[name].rearrange("(g o) -> o g", o=D)).then_inc(S("w_in"), 16)
            for i, name in enumerate(("L0_gnn_b_l2", "L1_gnn_i_b", "L1_gnn_j_b", "L2_gnn_b2", "L3_gnn_b")):
                act.dma_start(brow[:, i, :], a[name].rearrange("(o d) -> o d", o=1)).then_inc(S("brow_in"), 16)
            act.wait_ge(S("x_pad"), 1)
            act.dma_start(x_nm[0:NLAST, NB - 1, :], a["x"][(NB - 1) * P:N, :]).then_inc(S("x_in"), 16)

            for q in range(4):
                act.wait_ge(S("wt"), q + 1)
                n = min(4, 14 - 4 * q)
                A(WT[:, 4 * q:4 * q + n, :].rearrange("p a b -> p (a b)"), ps[:, 1 + q % 2, 0:n * P], ACT.Copy).then_inc(S("wt_copied"), 1)
            act.wait_ge(S("w_in"), 16 * 11)
            act.wait_ge(S("bias_mm"), 1)
            A(biasb[:, 0:4, :].rearrange("p a b -> p (a b)"), ps[:, 3, 0:4 * D], ACT.Copy)
            A(biasb[:, 4, :], ps[:, 4, 0:D], ACT.Copy).then_inc(S("bias_copied"), 1)

            def layernorm(name):
                n = 2 * LN[name] + 1
                for h, (lo, hi) in enumerate(HALVES):
                    act.wait_ge(S("ln_centred"), n + h)
                    A(squares[:, lo * D:hi * D], hn[:, lo:hi, :].rearrange("p a b -> p (a b)"), ACT.Square).then_inc(S("ln_squared"), 1)
                for h, (lo, hi) in enumerate(HALVES):
                    act.wait_ge(S("ln_var"), n + h)
                    A(st[:, 2, lo:hi], st[:, 1, lo:hi], ACT.Sqrt, bias=epsc[:, 0:1], scale=1.0 / D).then_inc(S("ln_std"), 1)
                for h, (lo, hi) in enumerate(HALVES):
                    act.wait_ge(S("ln_ln"), n + h)
                    A(op[:, lo:hi, 0, :], hn[:, lo:hi, :], ACT.Relu).then_inc(S("ln_high"), 1)

            def copy_blocks(name, dst):
                for q in range(NQ):
                    n = min(4, NB - 4 * q) * P
                    act.wait_ge(S("tr_mm"), TR[name] * NQ + q + 1)
                    A(dst(q, n), ps[:, 6 + q % 2, 0:n], ACT.Relu).then_inc(S("tr_copied"), 1)

            def high_part(use):
                act.wait_ge(S("scaled"), use + 1)
                for lo, hi in HALVES:
                    A(op[:, lo:hi, 0, :], hn[:, lo:hi, :], ACT.Copy, scale=sc[:, 3:4]).then_inc(S("q_high"), 1)

            cols = lambda Tb: (lambda q, n: Tb[:, 4 * q * P:4 * q * P + n])

            layernorm("l0")
            for q in range(12):
                kq, g0 = q // 4, 4 * (q % 4)
                n = min(4, WG - g0)
                act.wait_ge(S("keys_t"), q + 1)
                A(keys[:, kq, g0 * WP:(g0 + n) * WP, :], ps[:, 5 + q % 2, 0:n * WP].unsqueeze(2).broadcast_to([P, n * WP, 2]),
                  ACT.Copy).then_inc(S("keys"), 1)

            copy_blocks("l0h", cols(T0))

            act.sem_inc(S("stage_ready"), 2)
            with act.Fori(0, NCH) as i:
                for gr in range(GC):
                    s = gr % SS
                    act.wait_ge(S(f"stage_out{s}"), i * (GC // SS * 16) + (gr // SS + 1) * 16)
                    act.sem_inc(S("act_passed"), 1)
                    for q in range(GQ):
                        act.wait_ge(S("quad_mm"), i * (GC * GQ) + gr * GQ + q + 1 + 2 * GQ)
                        act.sem_inc(S("act_passed"), 1)
                        src = ps[:, q % 2 * 2:q % 2 * 2 + 2, :].rearrange("p b (h c) -> p (b h) c", h=2)[:, :, 0:CELL]
                        src = src.rearrange("p w (c d) -> p c w d", d=WD)
                        dst = stage8[s][:, :, QW * WD * q:QW * WD * (q + 1)].rearrange("p c (w d) -> p c w d", w=QW)
                        A(dst, src, ACT.Copy, saturate=False).then_inc(S("stage_ready"), 1)
            act.wait_ge(S("stage_ready"), NG * GQ + 2)
            act.sem_inc(S("quads_done"), 1)
            act.wait_ge(S("cnt_pad"), 1)
            for q in range(8):
                d, g0 = q // 4, 4 * (q % 4)
                n = min(4, WG - g0)
                act.wait_ge(S("cnt_t"), q + 1)
                dst = cntT[:, g0 * WP * WD:(g0 + n) * WP * WD].rearrange("k (w d) -> k w d", d=WD)[:, :, d]
                A(dst, ps[0:KT, 3 + q % 2, 0:n * WP], ACT.Copy).then_inc(S("cnt_copied"), 1)

            act.wait_ge(S("degn"), 1)
            A(dis_nm[:, :], ps[:, 5, 0:NB], ACT.Sqrt, bias=ones[:, 0:1]).then_inc(S("degn_root"), 1)

            for m in range(2):
                act.sem_inc(S(f"l0d_bank{m}"), 1)
            act.wait_ge(S("t_pads"), 1)
            with act.Fori(0, NCH) as c:
                for m in range(2):
                    act.wait_ge(S("l0d"), c * 2 + m + 1)
                    A((T2, T3)[m][:, bass.ds(c * CH, CH)], ps[:, 2 + m, 0:CH], ACT.Identity, bias=bcol[:, m:m + 1]
                      ).then_inc(S("l0d_copied"), 1)
                    act.wait_ge(S("l0d_copied"), c * 2 + m + 1)
                    act.sem_inc(S(f"l0d_bank{m}"), 1)

            high_part(0)
            layernorm("l1")
            for q in range(NQ):
                n = min(4, NB - 4 * q) * P
                act.wait_ge(S("tr_mm"), TR["l1h"] * NQ + q + 1)
                A(T0[:, 4 * q * P:4 * q * P + n], ps[:, 6 + q % 2, 0:n], ACT.Relu)
                A(T1[:, 4 * q * P:4 * q * P + n], ps[:, 6 + q % 2, 0:n], ACT.Relu).then_inc(S("tr_copied"), 1)
            for c in range(NCH):
                act.wait_ge(S("deg_mm"), NCH + c + 1)
                A(row[:, c * CH:(c + 1) * CH], ps[:, 6 + c % 2, 0:CH], ACT.Sqrt, bias=ones[:, 0:1]).then_inc(S("deg2_root"), 1)
            for c in range(NCH):
                act.wait_ge(S("msg_bias_mm"), c + 1)
                A(T2[:, c * CH:(c + 1) * CH], ps[:, 6 + c % 2, 0:CH], ACT.Copy).then_inc(S("msg_bias"), 1)
            for step in range(NSTEP):
                with act.Fori(0, NCH) as i:
                    c = i + step * NCH
                    for k in range(KT):
                        act.wait_ge(S(f"ty_mm{k}"), c + 2)
                        A(tmp[:, k, :], ps[:, k % 2, 0:CH], ACT.Copy).then_inc(S("ty_sum"), 1)
                        act.wait_ge(S("ty_sum"), c * KT + k + 1)
                        act.sem_inc(S(f"ty_bank{k % 2}"), 1)
                    act.wait_ge(S("gru_mm"), c * 3 + 1)
                    A(tmp[:, 5, :], ps[:, 3, 0:CH], ACT.Sigmoid, bias=brz[:, 0:1]).then_inc(S("gru_r"), 1)
                    act.wait_ge(S("gru_mm"), c * 3 + 2)
                    A(tmp[:, 6, :], ps[:, 4, 0:CH], ACT.Sigmoid, bias=brz[:, 1:2]).then_inc(S("gru_z"), 1)
                    act.wait_ge(S("gru_pre"), c + 1)
                    A(tmp[:, 8, :], tmp[:, 7, :], ACT.Tanh, bias=bcol[:, 4:5]).then_inc(S("gru_n"), 1)
                if step < NSTEP - 1:
                    for q in range(NQ):
                        n = min(4, NB - 4 * q)
                        act.wait_ge(S("tr_mm"), TR[f"l1t{step}"] * NQ + q + 1)
                        A(op[:, 4 * q:4 * q + n, 0, :], ps[:, 6 + q % 2, 0:n * P].rearrange("p (b d) -> p b d", d=D), ACT.Copy
                          ).then_inc(S("high"), 1)
            for q in range(NQ):
                n = min(4, NB - 4 * q) * P
                act.wait_ge(S("l1o_mm"), q + 1)
                if q >= 2:
                    act.wait_ge(S("l1o_used"), q - 1)
                A(tmp[:, 2 * (q % 2):2 * (q % 2) + 2, :].rearrange("p a b -> p (a b)")[:, 0:n], ps[:, 2 * (q % 2), 0:n], ACT.Sigmoid
                  ).then_inc(S("l1o_sig"), 1)

            layernorm("l2")
            copy_blocks("l2h", cols(T0))
            act.sem_inc(S("l2d_bank"), 1)
            with act.Fori(0, NCH) as c:
                act.wait_ge(S("l2d"), c + 1)
                A(T2[:, bass.ds(c * CH, CH)], ps[:, 2, 0:CH], ACT.Identity, bias=bcol[:, 8:9]).then_inc(S("l2d_bias"), 1)
                act.wait_ge(S("l2d_bias"), c + 1)
                act.sem_inc(S("l2d_bank"), 1)
            high_part(1)
            layernorm("l3")

        @block.vector
        def _(dve):
            v = nc.vector
            link = Chain(dve, S("dve_chain"))
            v.memset(ones[:, :], 1.0).then_inc(S("ones"), 1)
            link(v.memset(ones16[:, :], 1.0))
            link(v.memset(epsc[:, :], EPS))
            v.memset(x_nm[:, NB - 1, :], 0.0).then_inc(S("x_pad"), 1)
            v.memset(cntT[:, :], 0.0).then_inc(S("cnt_pad"), 1)
            dve.wait_ge(S("consts"), 2)
            v.tensor_copy(iota16[:, :], iota_i[:, :])
            link(v.tensor_copy(wbase[:, :], wbase_i[:, :]))
            dve.wait_ge(S("heads_in"), 16)
            v.tensor_copy(rf[:, :], rf_i[:, :]).then_inc(S("heads"), 1)
            dve.wait_ge(S("edges_in"), 48)
            link(v.tensor_scalar(e_dst, e_dst, 14, None, ALU.logical_shift_left))
            link(v.tensor_scalar(e_typ, e_typ, 12, None, ALU.logical_shift_left))
            link(v.tensor_tensor(e_dst, e_dst, e_typ, ALU.bitwise_or))
            v.tensor_tensor(e_dst, e_dst, e_src, ALU.bitwise_or).then_inc(S("pack_ready"), 1)

            dve.wait_ge(S("heads_mm"), 1)
            v.tensor_copy(rfb[:, :], ps[:, 0, 0:ER]).then_inc(S("heads_copied"), 1)
            dve.wait_ge(S("heads_copied"), 1)
            for w in range(WG):
                t = v.tensor_scalar(junk[:, 0:ER], rfb[0:WP, :], wbase[:, w:w + 1], None, ALU.is_lt, ALU.add,
                                    accum_out=small[0:WP, 0, w:w + 1])
                link(t)
            link(v.tensor_scalar(small[0:WP, 1, :], small[0:WP, 0, :], -1.0, 0.0, ALU.add, ALU.max))
            v.tensor_copy(small_i[0:WP, 0, :], small[0:WP, 1, :]).then_inc(S("rowidx"), 1)
            for w in range(WG):
                dve.wait_ge(S(f"row_in{w % 4}"), 16 * (w // 4 + 1))
                v.tensor_copy(rows_f, rows_i[w % 4]).then_inc(S("row_used"), 1)
                dve.wait_ge(S("row_used"), w + 1)
                link(v.tensor_scalar(junk, rows_f, wbase[:, w:w + 1], None, ALU.is_lt, ALU.add,
                                     accum_out=small[0:WP, 2, w:w + 1]))
            link(v.scalar_tensor_tensor(out=small[0:WP, 3, :], in0=small[0:WP, 1, :], scalar=float(EC), in1=small[0:WP, 2, :],
                                        op0=ALU.mult, op1=ALU.add))
            v.tensor_copy(small_i[0:WP, 1, :], small[0:WP, 3, :]).then_inc(S("startidx"), 1)

            def wide(col):
                return col.unsqueeze(2).broadcast_to([P, col.shape[1], D])

            def layernorm(name, scale=None):
                n = 2 * LN[name] + 1
                for lo, hi in HALVES:
                    link(v.tensor_reduce(st[:, 0, lo:hi], x_nm[:, lo:hi, :], AX.X, ALU.add))
                link(v.tensor_scalar(st[:, 0, :], st[:, 0, :], 1.0 / D, None, ALU.mult))
                for lo, hi in HALVES:
                    v.tensor_tensor(hn[:, lo:hi, :], x_nm[:, lo:hi, :], wide(st[:, 0, lo:hi]), ALU.subtract
                                    ).then_inc(S("ln_centred"), 1)
                for h, (lo, hi) in enumerate(HALVES):
                    dve.wait_ge(S("ln_squared"), n + h)
                    v.tensor_reduce(st[:, 1, lo:hi], squares.rearrange("p (a b) -> p a b", b=D)[:, lo:hi, :], AX.X, ALU.add
                                    ).then_inc(S("ln_var"), 1)
                for h, (lo, hi) in enumerate(HALVES):
                    dve.wait_ge(S("ln_std"), n + h)
                    link(v.reciprocal(st[:, 3, lo:hi], st[:, 2, lo:hi]))
                    if scale is not None:
                        link(v.tensor_tensor(st[:, 3, lo:hi], st[:, 3, lo:hi], scale[:, lo:hi], ALU.mult))
                    v.tensor_tensor(hn[:, lo:hi, :], hn[:, lo:hi, :], wide(st[:, 3, lo:hi]), ALU.mult).then_inc(S("ln_ln"), 1)
                for h, (lo, hi) in enumerate(HALVES):
                    dve.wait_ge(S("ln_high"), n + h)
                    v.scalar_tensor_tensor(out=op[:, lo:hi, 1, :], in0=hn[:, lo:hi, :], scalar=0.0, in1=op[:, lo:hi, 0, :],
                                           op0=ALU.max, op1=ALU.subtract).then_inc(S("ln_op"), 1)

            dve.wait_ge(S("x_in"), 32)
            dve.wait_ge(S("wt_copied"), 4)
            layernorm("l0")

            pk, lo, ct, cu, ty, rel, m = wa[0], wa[6], wa[1], wa[2], wa[3], wa[4], wa[5]
            I = lambda t: t.bitcast(I32)
            dve.wait_ge(S("windows_in"), 16 * WG)
            dve.wait_ge(S("packed_out"), 32)
            link(v.tensor_scalar(I(m), I(pk), 7, 31, ALU.logical_shift_right, ALU.bitwise_and))
            link(v.tensor_copy(cu, I(m)))
            link(v.tensor_scalar(I(m), I(pk), 12, 3, ALU.logical_shift_right, ALU.bitwise_and))
            link(v.tensor_copy(ty, I(m)))
            link(v.tensor_scalar(I(m), I(pk), 14, None, ALU.logical_shift_right))
            link(v.tensor_copy(rel, I(m)))
            r3 = lambda t: t.rearrange("p (g e) -> p g e", e=CAP)
            link(v.tensor_tensor(r3(rel), r3(rel), wbase[:, :].unsqueeze(2).broadcast_to([WP, WG, CAP]), ALU.subtract))
            link(v.tensor_scalar(I(m), I(pk), 127, None, ALU.bitwise_and))
            link(v.tensor_copy(lo, I(m)))
            link(v.tensor_copy(pk, lo))
            link(v.tensor_scalar(m, rel, 0.0, None, ALU.is_ge))
            link(v.scalar_tensor_tensor(out=m, in0=rel, scalar=float(WD), in1=m, op0=ALU.is_lt, op1=ALU.mult))
            link(v.tensor_reduce(fl[0:WP, 0:1], m, AX.X, ALU.add))
            link(v.scalar_tensor_tensor(out=cu, in0=cu, scalar=float(WD), in1=rel, op0=ALU.mult, op1=ALU.add))
            link(v.scalar_tensor_tensor(out=ct, in0=ty, scalar=float(NB * WD), in1=cu, op0=ALU.mult, op1=ALU.add))
            link(v.scalar_tensor_tensor(out=cu, in0=cu, scalar=1.0, in1=m, op0=ALU.add, op1=ALU.mult))
            link(v.scalar_tensor_tensor(out=ct, in0=ct, scalar=1.0, in1=m, op0=ALU.add, op1=ALU.mult))
            link(v.tensor_scalar(cu, cu, -1.0, None, ALU.add))
            link(v.tensor_scalar(ct, ct, -1.0, None, ALU.add))
            link(v.scalar_tensor_tensor(out=rel, in0=rel, scalar=float(KT), in1=ty, op0=ALU.mult, op1=ALU.add))
            link(v.scalar_tensor_tensor(out=rel, in0=rel, scalar=1.0, in1=m, op0=ALU.add, op1=ALU.mult))
            v.engine_nop().then_inc(S("codes"), 1)
            dve.sem_inc(S("quad_mm"), 2 * GQ)
            dve.wait_ge(S("keys"), 12)
            dve.wait_ge(S("tr_copied"), NQ)
            for s in range(2):
                v.memset(ps[:, 6 + s, 0:GW], 0.0)
            def most(s, g):
                return v.tensor_reduce(rowmax[:, g], ps[:, 6 + s, 0:GW], AX.X, ALU.max)
            link(v.memset(rowmax[:, :], 0.0))
            with dve.Fori(0, NG // 2) as i:
                for s in range(2):
                    dve.wait_ge(S("quad_mm"), i * (2 * GQ) + (s + 1) * GQ)
                    most(s, bass.ds(i * 2 + s, 1))
                    o = oh[:, s, :, :]
                    key = lambda q, n: keys[:, q, bass.ds(i * (2 * GW) + s * GW, GW), :].unsqueeze(2).broadcast_to([P, GW, n // 2, 2])
                    cols = lambda lo, n: o[:, :, lo:lo + n].rearrange("p w (c two) -> p w c two", two=2)
                    for q, lo, n in ((0, 0, P), (1, P, TCELL), (2, P + TCELL, CELL - TCELL)):
                        t = v.tensor_tensor(cols(lo, n), pairs(n), key(q, n), ALU.is_equal)
                    t.then_inc(S("oh_ready"), 1)
            for s in range(2):
                dve.wait_ge(S("quad_mm"), NG * GQ + (s + 1) * GQ)
                link(most(s, slice(NG + s, NG + s + 1)))
            v.tensor_reduce(fl[:, 1:2], rowmax[:, :], AX.X, ALU.max).then_inc(S("fl_a"), 1)

            dve.wait_ge(S("fl_b"), 1)
            link(v.tensor_scalar(fl[0:1, 2:3], ps[0:1, 5, 0:1], float(E), None, ALU.is_equal))
            link(v.tensor_reduce(fl[0:1, 3:4], ps[0:1, 5, 128:256], AX.X, ALU.max))
            link(v.tensor_scalar(fl[0:1, 4:5], fl[0:1, 3:4], float(MULT_MAX), None, ALU.is_le))
            link(v.tensor_tensor(fl[0:1, 5:6], fl[0:1, 2:3], fl[0:1, 4:5], ALU.mult))
            v.tensor_copy(flag_i[:, :], fl[0:1, 5:6]).then_inc(S("flag"), 1)
            dve.wait_ge(S("flag"), 1)
            fast = dve.value_load(flag_i[:, :], min_val=0, max_val=1)
            g_link = Chain(dve, S("g_chain"))

            def general(name, types=1):
                with dve.If(fast < 1):
                    dve.wait_ge(S("g_edges"), 48 * (GCALL.index(name) + 1))
                    dve.wait_ge(S("g_iota"), GCALL.index(name) + 1)
                    if name == "count":
                        dve.sem_inc(S("g_mm"), 1)
                    g_link(v.tensor_copy(g_iota, g_iota.bitcast(I32)))
                    g_link(v.tensor_copy(g_dst.bitcast(F32), g_dst))
                    g_link(v.tensor_copy(g_typ.bitcast(F32), g_typ))
                    v.memset(g_zero, 0.0).then_inc(S("g_zero"), 1)
                    for k in range(types):
                        n = GP[name] + k
                        if types > 1:
                            g_link(v.tensor_scalar(g_key, g_typ.bitcast(F32), float(k), 4096.0, ALU.not_equal, ALU.mult))
                            g_link(v.tensor_tensor(g_key, g_key, g_dst.bitcast(F32), ALU.add))
                        else:
                            g_link(v.tensor_copy(g_key, g_dst.bitcast(F32)))
                        with dve.Fori(0, EC) as e:
                            dve.wait_ge(S("g_mm"), e + n * EC + 1)
                            v.tensor_copy(g_idx, g_src[:, bass.ds(e, 1)]).then_inc(S("g_idx"), 1)
                            if name == "count":
                                v.tensor_scalar(g_thot, iota16[0:ER, 0:KT], g_typ.bitcast(F32)[:, bass.ds(e, 1)], None, ALU.is_equal)
                            v.tensor_scalar(g_hot, g_iota, g_key[:, bass.ds(e, 1)], None, ALU.is_equal).then_inc(S("g_hot"), 1)
                        dve.wait_ge(S("g_mm"), (n + 1) * EC + 1)
                        if n > 1:
                            dve.wait_ge(S("g_sums"), 16 * (n - 1))
                        for c in range(NCH):
                            if name == "count":
                                t = v.tensor_copy(cntT[:, c * CH:(c + 1) * CH], ps[0:KT, c, 0:CH])
                            else:
                                t = v.tensor_copy(g_out[:, c * CH:(c + 1) * CH], ps[:, c, 0:CH])
                        t.then_inc(S("g_evac"), 1)
                        dve.wait_ge(S("g_evac"), n + 1)

            general("count")

            def mean_row(name, row):
                n0 = DEG[name] * NCH
                for c in range(NCH):
                    cc = slice(c * CH, (c + 1) * CH)
                    dve.wait_ge(S("deg_mm"), 2 * n0 + c + 1)
                    v.tensor_scalar(row[:, cc], ps[:, 6 + c % 2, 0:CH], 1.0, None, ALU.max).then_inc(S("deg_used"), 1)
                    dve.wait_ge(S("deg_used"), n0 + c + 1)
                    link(v.reciprocal(row[:, cc], row[:, cc]))

            dve.wait_ge(S("adjacency_out"), 1)
            mean_row("deg0", row)
            dve.wait_ge(S("degn_root"), 1)
            link(v.tensor_scalar(deg_nm[:, :], ps[:, 5, 0:NB], 1.0, None, ALU.max))
            link(v.reciprocal(rdeg_nm[:, :], deg_nm[:, :]))
            link(v.reciprocal(dis_nm[:, :], dis_nm[:, :]))
            dve.wait_ge(S("w_in"), 16 * 11)
            link(v.tensor_tensor(brz[:, :], bcol[:, 2:4], bcol[:, 5:7], ALU.add))
            for Tb in (T1, T2, T3):
                t = v.memset(Tb[:, NT:NP], 0.0)
            t.then_inc(S("t_pads"), 1)
            dve.wait_ge(S("t_pads"), 1)

            def post(name, row, add=None, unit=None):
                general(name)
                at = AGG[name] * NCH

                turns = (AGG[name] * (NCH // 2 + 1), AGG[name] * (NCH // 2))

                def chunk(s, i, c):
                    n = c + at + 1
                    dve.wait_ge(S(f"ag_mm{s}"), i + turns[s] + 2)
                    cc = bass.ds(c * CH, CH)
                    if unit is not None:
                        t = v.scalar_tensor_tensor(out=T1[:, cc], in0=ps[:, s, 0:CH], scalar=unit, in1=row[:, cc],
                                                   op0=ALU.mult, op1=ALU.mult)
                    elif add is None:
                        t = v.tensor_tensor(T1[:, cc], ps[:, s, 0:CH], row[:, cc], ALU.mult)
                    else:
                        v.tensor_tensor(T1[:, cc], ps[:, s, 0:CH], add[:, cc], ALU.add).then_inc(S("self_loop"), 1)
                        dve.wait_ge(S("self_loop"), c + 1)
                        t = v.tensor_tensor(T1[:, cc], T1[:, cc], row[:, cc], ALU.mult)
                    t.then_inc(S("ag_post"), 1)
                    dve.wait_ge(S("ag_post"), n)
                    dve.sem_inc(S(f"ag_bank{s}"), 1)
                with dve.Fori(0, NCH // 2) as i:
                    for s in range(2):
                        chunk(s, i, i * 2 + s)
                chunk(0, NCH // 2, NCH - 1)

            def quads(name, f):
                for q in range(NQ):
                    n = min(4, NB - 4 * q)
                    dve.wait_ge(S("blk_mm"), BLK[name] * NQ + q + 1)
                    f(q, n, 4 * q, ps[:, 2 + q % 2, 0:n * P].rearrange("p (b d) -> p b d", d=D)).then_inc(S("blk_used"), 1)
                    dve.wait_ge(S("blk_used"), BLK[name] * NQ + q + 1)

            def product(name, use, f):
                def take(q, n, b0, p3):
                    link(f(q, n, b0, p3))
                    return v.tensor_reduce(most_q[:, q:q + 1], hn[:, b0:b0 + n, :], AX.XY, ALU.max, apply_absolute_value=True)
                quads(name, take)
                v.tensor_reduce(sc[:, 0:1], most_q[:, 0:NQ], AX.X, ALU.max).then_inc(S("scale_in"), 1)
                dve.wait_ge(S("scale_mm"), 2 * use + 1)
                v.tensor_reduce(sc[0:1, 1:2], ps[0:1, 4, 0:P], AX.X, ALU.max).then_inc(S("scale_in"), 1)
                dve.wait_ge(S("scale_mm"), 2 * use + 2)
                link(v.tensor_scalar(sc[:, 1:2], ps[:, 4, P:P + 1], 1e-30, None, ALU.max))
                link(v.tensor_scalar(sc[:, 2:3].bitcast(I32), sc[:, 1:2].bitcast(I32), 255 << 23, None, ALU.bitwise_and))
                link(v.tensor_scalar(sc[:, 2:3], sc[:, 2:3], 2.0 ** -13, None, ALU.mult))
                v.reciprocal(sc[:, 3:4], sc[:, 2:3]).then_inc(S("scaled"), 1)
                for h, (lo, hi) in enumerate(HALVES):
                    dve.wait_ge(S("q_high"), 2 * use + h + 1)
                    v.scalar_tensor_tensor(out=op[:, lo:hi, 1, :], in0=hn[:, lo:hi, :], scalar=sc[:, 3:4], in1=op[:, lo:hi, 0, :],
                                           op0=ALU.mult, op1=ALU.subtract).then_inc(S("q_op"), 1)

            def add_bias(i):
                link(v.tensor_tensor(x_nm[:, :, :], x_nm[:, :, :], biasb[:, i, :].unsqueeze(1).broadcast_to([P, NB, D]), ALU.add))

            add_x = lambda q, n, b0, p3: v.tensor_tensor(x_nm[:, b0:b0 + n, :], x_nm[:, b0:b0 + n, :], p3, ALU.add)

            for s in range(2):
                dve.sem_inc(S(f"ag_bank{s}"), 1)
                dve.sem_inc(S(f"ty_bank{s}"), 1)
            dve.sem_inc(S("gru_h"), 1)
            post("l0a", row)
            product("l0p", 0, lambda q, n, b0, p3: v.tensor_copy(hn[:, b0:b0 + n, :], p3))
            dve.wait_ge(S("bias_copied"), 1)
            add_bias(BL2)
            post("l0b", row, unit=sc[:, 2:3])
            quads("l0o", add_x)

            layernorm("l1")
            dve.wait_ge(S("tr_copied"), (TR["l1h"] + 1) * NQ)
            for c in range(NCH):
                dve.wait_ge(S("deg2_root"), c + 1)
                link(v.reciprocal(row[:, c * CH:(c + 1) * CH], row[:, c * CH:(c + 1) * CH]))
            mean_row("deg3", T3)
            for step in range(NSTEP):
                general(f"l1s{step}", KT)
                with dve.Fori(0, NCH) as i:
                    link.enter(i, 4)
                    c = i + step * NCH
                    hc = T1[:, bass.ds(i * CH, CH)]
                    pre, nt, zs, rs = tmp[:, 7, :], tmp[:, 8, :], tmp[:, 6, :], tmp[:, 5, :]
                    t1, t2 = tmp[:, 9, :], tmp[:, 10, :]
                    dve.wait_ge(S("gru_msg"), c + 1)
                    v.tensor_tensor(tmp[:, 4, :], ps[:, 2, 0:CH], T2[:, bass.ds(i * CH, CH)], ALU.add).then_inc(S("gru_a"), 1)
                    dve.wait_ge(S("gru_r"), c + 1)
                    link(v.scalar_tensor_tensor(out=t1, in0=ps[:, 5, 0:CH], scalar=bcol[:, 7:8], in1=rs, op0=ALU.add, op1=ALU.mult))
                    dve.wait_ge(S("gru_mm"), c * 3 + 3)
                    v.tensor_tensor(pre, t1, ps[:, 6, 0:CH], ALU.add).then_inc(S("gru_pre"), 1)
                    dve.wait_ge(S("gru_n"), c + 1)
                    link(v.tensor_tensor(t2, hc, nt, ALU.subtract))
                    dve.wait_ge(S("gru_z"), c + 1)
                    link(v.tensor_tensor(t2, t2, zs, ALU.mult))
                    link(v.tensor_tensor(hc, t2, nt, ALU.add))
                    dve.sem_inc(S("gru_h"), 1)
                link.leave(NCH)
                if step < NSTEP - 1:
                    for q in range(NQ):
                        n = min(4, NB - 4 * q)
                        dve.wait_ge(S("high"), step * NQ + q + 1)
                        v.tensor_tensor(op[:, 4 * q:4 * q + n, 1, :], ps[:, 6 + q % 2, 0:n * P].rearrange("p (b d) -> p b d", d=D),
                                        op[:, 4 * q:4 * q + n, 0, :], ALU.subtract).then_inc(S("tr_copied"), 1)
            for q in range(NQ):
                n = min(4, NB - 4 * q)
                sig = tmp[:, 2 * (q % 2):2 * (q % 2) + 2, :].rearrange("p a b -> p (a b)")[:, 0:n * P]
                dve.wait_ge(S("l1o_sig"), q + 1)
                val = tmp[:, 4 + 2 * (q % 2):6 + 2 * (q % 2), :].rearrange("p a b -> p (a b)")[:, 0:n * P]
                link(v.tensor_tensor(val.rearrange("p (b d) -> p b d", d=D), ps[:, 2 * (q % 2) + 1, 0:n * P].rearrange("p (b d) -> p b d", d=D),
                                     biasb[:, BJ, :].unsqueeze(1).broadcast_to([P, n, D]), ALU.add))
                link(v.tensor_tensor(sig, sig, val, ALU.mult))
                v.tensor_tensor(x_nm[:, 4 * q:4 * q + n, :], x_nm[:, 4 * q:4 * q + n, :], sig.rearrange("p (b d) -> p b d", d=D),
                                ALU.add).then_inc(S("l1o_used"), 1)
                dve.wait_ge(S("l1o_used"), q + 1)

            layernorm("l2", dis_nm[:, :])
            dve.wait_ge(S("tr_copied"), (TR["l2h"] + 1) * NQ)
            post("l2a", row, T0)
            with dve.Fori(0, NCH) as c:
                cc = bass.ds(c * CH, CH)
                dve.wait_ge(S("l2d_bias"), c + 1)
                v.scalar_tensor_tensor(out=T2[:, cc], in0=T2[:, cc], scalar=0.01, in1=T2[:, cc], op0=ALU.mult, op1=ALU.max
                                       ).then_inc(S("l2d_done"), 1)
            product("l2p", 1, lambda q, n, b0, p3: v.tensor_tensor(
                hn[:, b0:b0 + n, :], p3, dis_nm[:, b0:b0 + n].unsqueeze(2).broadcast_to([P, n, D]), ALU.mult))
            own = squares.rearrange("p (a b) -> p a b", b=D)
            link(v.tensor_tensor(own, hn[:, :, :], wide(dis_nm[:, :]), ALU.mult))
            link(v.tensor_tensor(x_nm[:, :, :], x_nm[:, :, :], own, ALU.add))
            add_bias(B2)
            post("l2b", row, unit=sc[:, 2:3])
            quads("l2o", add_x)

            layernorm("l3", rdeg_nm[:, :])
            add_bias(B3)
            post("l3a", T3)
            for q in range(NQ):
                n = min(4, NB - 4 * q)
                dve.wait_ge(S("blk_mm"), BLK["l3o"] * NQ + q + 1)
                add_x(q, n, 4 * q, ps[:, 2 + q % 2, 0:n * P].rearrange("p (b d) -> p b d", d=D)).then_inc(S("blk_used"), 1)
                dve.wait_ge(S("blk_used"), BLK["l3o"] * NQ + q + 1)
                dve.sem_inc(S("l3_out"), 1)


INPUTS = ["x", "src", "dst", "edge_type_4", "L0_gnn_W_l1", "L0_gnn_b_l1", "L0_gnn_W_r1", "L0_gnn_W_l2", "L0_gnn_b_l2",
          "L0_gnn_W_r2", "L1_gnn_W_et", "L1_gnn_b_et", "L1_gnn_W_ih", "L1_gnn_b_ih", "L1_gnn_W_hh", "L1_gnn_b_hh",
          "L1_gnn_i_w", "L1_gnn_i_b", "L1_gnn_j_w", "L1_gnn_j_b", "L2_gnn_W1", "L2_gnn_b1", "L2_gnn_W2", "L2_gnn_b2",
          "L3_gnn_W", "L3_gnn_b"]


def kernel(**inputs):
    import numpy as _np
    import concourse.bacc as _bacc
    from concourse import mybir as _mybir
    from concourse.bass_utils import run_bass_kernel_spmd as _run

    nc = _bacc.Bacc("TRN2", target_bir_lowering=False, num_devices=1)
    arrays, aps = {}, {}
    for name in INPUTS:
        arr = _np.ascontiguousarray(inputs[name])
        arrays[f"in_{name}"] = arr
        aps[name] = nc.dram_tensor(f"in_{name}", arr.shape, _mybir.dt.from_np(arr.dtype), kind="ExternalInput").ap()
    out = nc.dram_tensor("out_0", (N, D), _mybir.dt.float32, kind="ExternalOutput").ap()
    packed = nc.dram_tensor("packed_edges", (E + CAP,), _mybir.dt.int32, kind="Internal").ap()
    adj = nc.dram_tensor("adjacency", (KT + 1, NCH, P, PIECE), _mybir.dt.uint8, kind="Internal").ap()
    table = nc.dram_tensor("operand_rows", (NP, 2 * D), _mybir.dt.float16, kind="Internal").ap()
    sums = nc.dram_tensor("general_sums", (KT, NCH, P, CH), _mybir.dt.float32, kind="Internal").ap()
    build(nc, aps, out, packed, adj, table, sums)
    r = _run(nc, [arrays], core_ids=[0])
    return r.results[0]["out_0"]
```

```python
from contextlib import ExitStack

import concourse.bass as bass
from concourse import mybir

ALU = mybir.AluOpType
ACT = mybir.ActivationFunctionType
AX = mybir.AxisListType
F32, F16 = mybir.dt.float32, mybir.dt.float16
I32, U8, F8 = mybir.dt.int32, mybir.dt.uint8, mybir.dt.float8e4

P = 128
N = 3125
D = 128
E = 100000
KT = 4
NB = (N + P - 1) // P
NLAST = N - (NB - 1) * P
CH = 448
NCH = (N + CH - 1) // CH
NT = NCH * CH
NP = NB * P
ER, EC = 125, 800
WD = 2
NW = NT // WD
WP = 112
WG = NW // WP
CAP = 128
CELL = (KT + 1) * NB * WD
TCELL = KT * NB * WD
GD = 32
GW = GD // WD
NG = NT // GD
GC = CH // GD
SS = GC // 2
PIECE = NB * CH
EPS = 1e-5
KEY_QUADS = [(h, k, g) for h in range(2) for k in range(3) for g in (8 * h, 8 * h + 4)]
CELL1 = CELL + WD
OHW = P + CELL1
QW = 8
GQ = GW // QW
RING = 4
UNTYPED = KT
NQ = NB // 4 + 1
AGG = {"l0a": 0, "l0b": 1, "l2a": 2, "l2b": 3, "l3a": 4}
BLK = {"l0p": 0, "l0o": 1, "l2p": 2, "l2o": 3, "l3o": 4}
TR = {"l0h": 0, "l1h": 1, "l1t0": 2, "l1t1": 3, "l2h": 4}
LN = {"l0": 0, "l1": 1, "l2": 2, "l3": 3}
GP = {"count": 0, "l0a": 1, "l0b": 2, "l1s0": 3, "l1s1": 7, "l1s2": 11, "l2a": 15, "l2b": 16, "l3a": 17}
GCALL = list(GP)
GX = 5
HALVES = ((0, 12), (12, NB))
QUADS = [(4 * q, min(4 * q + 4, NB)) for q in range(NQ)]
EARLY = (NCH - 1) * CH // (4 * P)
STEP_BANKS = (2, 7, 3, 4)
OUT_BANKS = ((0, 1), (2, 7))
WHALVES = ((0, 8), (8, WG))
ROW_CODE = 87


class Chain:

    def __init__(self, eng, sem):
        self.eng, self.sem, self.n, self.i, self.m = eng, sem, 0, None, 0

    def __call__(self, ins):
        self.n += 1
        ins.then_inc(self.sem, 1)
        at = self.n if self.i is None else self.i * self.m + self.n
        self.eng.wait_ge(self.sem, at)

    def enter(self, i, m):
        self.i, self.m, self.start = i, m, self.n

    def leave(self, trips):
        assert self.n - self.start == self.m, (self.n - self.start, self.m)
        self.n, self.i = self.start + trips * self.m, None


def build(nc, a, out, packed, adj, table, sums):
    ctx = ExitStack()
    with ctx:
        def sb(name, shape, dt):
            return ctx.enter_context(nc.sbuf_tensor(name, shape, dt))

        sems = {}

        def S(name):
            if name not in sems:
                sems[name] = ctx.enter_context(nc.semaphore(name))
            return sems[name]

        ctx.enter_context(nc.allow_non_contiguous_dma(reason="small bias columns and row heads"))

        ident = sb("ident", [P, P], F32)
        ones = sb("ones", [P, P], F32)
        epsc = sb("epsc", [P, 1], F32)
        iota_i = sb("iota_i", [P, CELL], I32)
        iota16 = sb("iota16", [P, CELL], F16)
        pairs = lambda n: iota16[:, 0:n].rearrange("p (c two) -> p c two", two=2).unsqueeze(1).broadcast_to([P, GW, n // 2, 2])
        wbase_i = sb("wbase_i", [WP, WG], I32)
        wbase = sb("wbase", [WP, WG], F32)

        x_nm = sb("x_nm", [P, NB, D], F32)
        hn = sb("hn", [P, NB, D], F32)
        op = sb("op", [P, NB, 2, D], F16)
        T = sb("T", [P, 4 * NP], F32)
        T0, T1, T2, T3 = (T[:, i * NP:(i + 1) * NP] for i in range(4))
        ring = sb("ring", [P, RING, PIECE], U8)
        ring8 = ring[:, :, :].bitcast(F8).rearrange("p s (g h d) -> p s h g d", g=GC, h=NB)
        tmp = sb("tmp", [P, 11, CH], F32)
        tmpf = tmp[:, :, :].rearrange("p a b -> p (a b)")
        squares = tmpf[:, 0:NP]
        sig2 = tmpf[:, NP:NP + 2 * 4 * P].rearrange("p (s c) -> p s c", s=2)
        keys = tmp[:, :, :].rearrange("p a b -> p (a b)").bitcast(F16)[:, 0:6 * NW].rearrange("p (q w two) -> p q w two", q=3, two=2)
        cntT = sb("cntT", [KT, NP], F32)
        row = sb("row", [P, NT], F32)
        deg_nm = sb("deg_nm", [P, NB], F32)
        rdeg_nm = sb("rdeg_nm", [P, NB], F32)
        dis_nm = sb("dis_nm", [P, NB], F32)
        st = sb("st", [P, 4, NB], F32)
        small = sb("small", [P, 8, WG], F32)
        small_i = sb("small_i", [P, 2, WG], I32)
        cnt8 = sb("cnt8", [WP, WG, WD * KT], F32)
        rowmax = sb("rowmax", [P, NG + 3], F32)
        fl = sb("fl", [P, 8], F32)
        most_q = sb("most_q", [P, NQ + 1], F32)
        sc = sb("sc", [P, 4], F32)
        biasb = sb("biasb", [P, 5, D], F32)
        flag_i = sb("flag_i", [1, 1], I32)
        rf_i = sb("rf_i", [1, ER], I32)
        rf = sb("rf", [1, ER], F32)
        rfb = sb("rfb", [P, ER], F32)
        pad_i = sb("pad_i", [1, CAP], I32)
        wl1 = sb("wl1", [D, 2 * D], F32)
        wr1 = sb("wr1", [D, 2 * D], F32)
        wl2 = sb("wl2", [D, 2, D], F32)
        wr2 = sb("wr2", [D, 2, D], F32)
        w1 = sb("w1", [D, D], F32)
        w2 = sb("w2", [D, D], F32)
        WT = sb("WT", [D, 14, D], F32)
        ET, IH, HH, IW, JW, W3 = 0, 4, 7, 10, 12, 13
        bet = sb("bet", [KT, D], F32)
        bcol = sb("bcol", [D, 9], F32)
        brz = sb("brz", [D, 2], F32)
        brow = sb("brow", [1, 5, D], F32)
        BL2, BI, BJ, B2, B3 = range(5)
        raww = hn[:, :, :].rearrange("p a b -> p (a b)")[:, 0:14 * D].rearrange("p (w d) -> p w d", w=14)
        e_dst, e_src, e_typ = (T[0:ER, i * EC:(i + 1) * EC].bitcast(I32) for i in range(3))
        rows_i = [T[0:WP, (3 + i) * EC:(4 + i) * EC].bitcast(I32) for i in range(4)]
        junk = T[0:WP, 8 * EC:9 * EC]
        WA = WG * CAP
        wa = [T[0:WP, i * WA:(i + 1) * WA] for i in range(7)]
        ring_b = ring[:, :, :].rearrange("p s b -> p (s b)")
        OHB = GW * OHW * 2
        oh = ring_b[:, 0:2 * OHB].bitcast(F16).rearrange("p (s w c) -> p s w c", s=2, c=OHW)
        SB = (KT + 1) * NB * GD
        SB1 = SB + GD
        row_b = row[:, :].bitcast(U8)
        stage = [ring_b[:, 2 * OHB + z * SB1:2 * OHB + (z + 1) * SB1] if 2 * OHB + (z + 1) * SB1 <= RING * PIECE else
                 row_b[:, (SS - 1 - z) * SB1:(SS - z) * SB1] for z in range(SS)]
        stage8 = [z.bitcast(F8).rearrange("p (c d) -> p c d", d=GD) for z in stage]

        at = [0]

        def carve(cols, dt, rows=P):
            size = cols * (2 if dt == F16 else 4)
            at[0] += size
            return ring_b[0:rows, at[0] - size:at[0]].bitcast(dt)

        g_out = carve(NT, F32)
        g_iota = carve(NT, F32, ER)
        g_hot = carve(NT, F16, ER)
        g_src, g_dst, g_typ = (carve(EC, I32, ER) for _ in range(3))
        g_x = carve(2 * D, F16, ER)
        g_idx = carve(1, I32, ER)
        g_thot = carve(KT, F16, ER)
        g_zero = carve(CH, F16)
        g_key = tmp[0:ER, 0:2, :].rearrange("p a b -> p (a b)")[:, 0:EC]
        ringf = ring[:, :, 0:4 * CH].bitcast(F32)

        ps = ctx.enter_context(nc.psum_tensor("ps", [P, 8, 512], F32))

        adj_w = adj.rearrange("k c p (g b) -> p k c g b", g=GC)
        NSTEP = 3

        block = ctx.enter_context(nc.Block())

        @block.sync
        def _(sp):
            def gate(sem, value):
                sp.wait_ge(sem, value)
                sp.sem_inc(S("sp_passed"), 1)

            for t, name in ((e_dst, "dst"), (e_src, "src"), (e_typ, "edge_type_4")):
                sp.dma_start(t, a[name].rearrange("(r c) -> r c", c=EC)).then_inc(S("edges_in"), 16)
            sp.dma_start(rf_i[:, :], a["dst"].rearrange("(o r c) -> o r c", o=1, c=EC)[:, :, 0]).then_inc(S("heads_in"), 16)
            sp.wait_ge(S("pack_ready"), 1)
            sp.wait_ge(S("pad"), 1)
            sp.dma_start(packed[0:E].rearrange("(r c) -> r c", c=EC), e_dst).then_inc(S("packed_out"), 16)
            sp.dma_start(packed[E:E + CAP].rearrange("(o c) -> o c", o=1), pad_i[:, :]).then_inc(S("packed_out"), 16)
            for z in range(SS):
                sp.sem_inc(S(f"stage_out{z}"), 16)
            with sp.Fori(0, NCH) as c:
                for g in range(GC):
                    gate(S("stage_ready"), c * (GC * GQ) + (g + 1) * GQ + 2)
                    dst = adj_w[:, :, bass.ds(c, 1), g:g + 1, :]
                    sp.dma_start(dst, stage[g % SS][:, 0:SB].rearrange("p (k c g b) -> p k c g b", k=KT + 1, c=1, g=1)
                                 ).then_inc(S(f"stage_out{g % SS}"), 16)
            for z in range(SS):
                sp.wait_ge(S(f"stage_out{z}"), 16 * (NCH * GC // SS + 1))
            sp.sem_inc(S("adjacency_out"), 1)

            sp.wait_ge(S("flag"), 1)
            fast = sp.value_load(flag_i[:, :], min_val=0, max_val=1)

            def general(name, ready, types=1):
                with sp.If(fast < 1):
                    for sem, n in ready:
                        sp.wait_ge(S(sem), n)
                    call = GCALL.index(name)
                    if name != "count":
                        sp.dma_start(table.rearrange("(b p) f -> p b f", p=P), op[:, :, :, :].rearrange("p b r d -> p b (r d)")
                                     ).then_inc(S("g_table"), 16)
                    for t, e in ((g_src, "src"), (g_dst, "dst"), (g_typ, "edge_type_4")):
                        sp.dma_start(t, a[e].rearrange("(r c) -> r c", c=EC)).then_inc(S("g_edges"), 16)
                    if name != "count":
                        sp.wait_ge(S("g_table"), 16 * call)
                        sp.sem_inc(S("g_rows"), 1)
                        for k in range(types):
                            sp.wait_ge(S("g_evac"), GP[name] + k + 1)
                            sp.dma_start(sums[k].rearrange("c p d -> p c d"), g_out.rearrange("p (c d) -> p c d", d=CH)
                                         ).then_inc(S("g_sums"), 16)
                            sp.wait_ge(S("g_sums"), 16 * (GP[name] + k))

            def piece(k, c, slot, sem):
                with sp.If(fast > 0):
                    sp.dma_start(ring[:, slot:slot + 1, :], adj[k, c].rearrange("c p b -> p c b")).then_inc(S(sem), 16)
                with sp.Else():
                    sp.dma_start(ringf[:, slot:slot + 1, :], sums[k % KT, c].rearrange("c p d -> p c d")).then_inc(S(sem), 16)

            general("count", [("adjacency_out", 1)])

            def untyped(name):
                def load(c, s, n):
                    gate(S(f"ag_mm{s}"), n)
                    piece(UNTYPED, c, s, f"ag_piece{s}")
                n0, n1 = AGG[name] * (NCH // 2 + 1), AGG[name] * (NCH // 2)
                with sp.Fori(0, NCH // 2) as i:
                    load(bass.ds(i * 2, 1), 0, i + n0 + 1)
                    load(bass.ds(i * 2 + 1, 1), 1, i + n1 + 1)
                load(slice(NCH - 1, NCH), 0, n0 + NCH // 2 + 1)

            def typed(step):
                with sp.Fori(0, NCH) as c:
                    for k in range(KT):
                        gate(S(f"ty_mm{k}"), c + step * NCH + 1)
                        piece(k, bass.ds(c, 1), k, f"ty_piece{k}")

            for s in range(2):
                sp.sem_inc(S(f"ag_mm{s}"), 1)
            for k in range(KT):
                sp.sem_inc(S(f"ty_mm{k}"), 1)
            general("l0a", [("ln_op", 2), ("deg_used", NCH)])
            untyped("l0a")
            general("l0b", [("q_op", 2)])
            untyped("l0b")
            sp.wait_ge(S("ag_mm0"), 1 + 2 * (NCH // 2 + 1))
            sp.wait_ge(S("ag_mm1"), 1 + 2 * (NCH // 2))
            for step in range(NSTEP):
                general(f"l1s{step}", [("ln_op", 4), ("tr_copied", (step + 2) * NQ)] +
                        [(f"ty_mm{k}", 1 + step * NCH) for k in range(KT)], KT)
                typed(step)
            for k in range(2):
                sp.wait_ge(S(f"ty_mm{k}"), 1 + NSTEP * NCH)
            general("l2a", [("ln_op", 6)])
            untyped("l2a")
            general("l2b", [("q_op", 4)])
            untyped("l2b")
            general("l3a", [("ln_op", 8)])
            untyped("l3a")

            sp.wait_ge(S("l3_out"), NQ)
            sp.dma_start(out[0:(NB - 1) * P, :].rearrange("(b p) d -> p b d", p=P), x_nm[:, 0:NB - 1, :]).then_inc(S("stored"), 16)
            sp.dma_start(out[(NB - 1) * P:N, :], x_nm[0:NLAST, NB - 1, :]).then_inc(S("stored"), 16)
            sp.wait_ge(S("stored"), 32)

        @block.gpsimd
        def _(pool):
            g = nc.gpsimd
            g.iota(iota_i[:, :], [[1, CELL]], base=1, channel_multiplier=0).then_inc(S("consts"), 1)
            g.iota(pad_i[:, :], [[1, CAP]], base=4095 << 14, channel_multiplier=0).then_inc(S("pad"), 1)
            g.iota(wbase_i[:, :], [[WD * WP, WG]], base=0, channel_multiplier=WD).then_inc(S("consts"), 1)
            g.memset(ident[:, :], 0.0).then_inc(S("ident_zero"), 1)
            pool.wait_ge(S("ident_zero"), 1)
            g.affine_select(out=ident[:, :], in_=ident[:, :], compare_op=ALU.not_equal, fill=1.0, base=0,
                            pattern=[[-1, P]], channel_multiplier=1).then_inc(S("ident"), 1)
            pool.wait_ge(S("rowidx"), 1)
            for w in range(WG):
                if w >= 4:
                    pool.wait_ge(S("row_used"), w - 3)
                pool.indirect_dma_start(out=rows_i[w % 4], out_offset=None, in_=a["dst"].rearrange("(r c) -> r c", c=EC),
                                        in_offset=bass.IndirectOffsetOnAxis(ap=small_i[0:WP, 0, w:w + 1], axis=0)
                                        ).then_inc(S(f"row_in{w % 4}"), 16)
            pool.wait_ge(S("startidx"), 1)
            pool.wait_ge(S("packed_out"), 32)
            for w in range(WG):
                pool.indirect_dma_start(out=wa[0][:, w * CAP:(w + 1) * CAP].bitcast(I32), out_offset=None,
                                        in_=packed.rearrange("(e o) -> e o", o=1),
                                        in_offset=bass.IndirectOffsetOnAxis(ap=small_i[0:WP, 1, w:w + 1], axis=0)
                                        ).then_inc(S(f"windows_in{int(w >= WHALVES[0][1])}"), 16)

            pool_link = Chain(pool, S("pool_chain"))
            pool.wait_ge(S("pair_codes"), 1)
            for j in range(WD * KT):
                pool_link(g.tensor_scalar(wa[3], wa[4], float(j + 1), None, ALU.is_equal))
                half, hit = CAP // 2, wa[3].rearrange("p (g e) -> p g e", e=CAP)
                while half >= 1:
                    dst = hit[:, :, 0:half] if half > 1 else cnt8[:, :, j:j + 1]
                    pool_link(g.tensor_tensor(dst, hit[:, :, 0:half], hit[:, :, half:2 * half], ALU.add))
                    half //= 2
            pool.sem_inc(S("cnt8"), 1)

            pool.wait_ge(S("flag"), 1)
            fast = pool.value_load(flag_i[:, :], min_val=0, max_val=1)
            with pool.If(fast < 1):
                for name, first in GP.items():
                    pool.wait_ge(S("g_edges"), 48 * (GCALL.index(name) + 1))
                    g.iota(g_iota.bitcast(I32), [[1, NT]], base=0, channel_multiplier=0).then_inc(S("g_iota"), 1)
                    if name == "count":
                        continue
                    pool.wait_ge(S("g_rows"), GCALL.index(name))
                    for k in range(KT if name.startswith("l1") else 1):
                        with pool.Fori(0, EC) as e:
                            pool.wait_ge(S("g_idx"), e + (first + k) * EC + 1)
                            pool.sem_inc(S("pool_passed"), 1)
                            pool.indirect_dma_start(out=g_x, out_offset=None, in_=table,
                                                    in_offset=bass.IndirectOffsetOnAxis(ap=g_idx, axis=0)
                                                    ).then_inc(S(f"g_x{(first + k - 1) // GX}"), 16)

        @block.tensor
        def _(pe):
            mm = nc.tensor.matmul

            def transposes(name, src, wait, banks=(6, 7)):
                n0, nb = TR[name] * NQ, len(banks)
                for q in range(NQ):
                    wait(q)
                    if q >= nb or name != "l0h" and nb == 2:
                        pe.wait_ge(S("tr_copied"), n0 + q + 1 - nb)
                    for b in range(4 * q, min(4 * q + 4, NB)):
                        t = nc.tensor.transpose(ps[:, banks[q % nb], (b % 4) * P:(b % 4 + 1) * P], src(b), ident[:, :])
                    t.then_inc(S("tr_mm"), 1)

            def once(*waits):
                def f(q=0):
                    if q == 0:
                        for s, v in waits:
                            pe.wait_ge(S(s), v)
                return f

            pe.wait_ge(S("heads"), 1)
            pe.wait_ge(S("ones"), 1)
            mm(ps[:, 0, 0:ER], ones[0:1, :], rf[:, :], start=True, stop=True).then_inc(S("heads_mm"), 1)

            pe.wait_ge(S("ident"), 1)
            pe.wait_ge(S("raw_in"), 16 * 6)
            for q in range(4):
                if q >= 2:
                    pe.wait_ge(S("wt_copied"), q - 1)
                js = range(4 * q, min(4 * q + 4, 14))
                for j in js:
                    t = nc.tensor.transpose(ps[:, 1 + q % 2, (j % 4) * P:(j % 4 + 1) * P], raww[:, j, :], ident[:, :])
                t.then_inc(S("wt"), 1)

            pe.wait_ge(S("brow_in"), 80)
            mm(ps[:, 3, 0:4 * D], ones[0:1, :], brow[:, 0:4, :].rearrange("o a b -> o (a b)"), start=True, stop=True)
            mm(ps[:, 4, 0:D], ones[0:1, :], brow[:, 4, :], start=True, stop=True).then_inc(S("bias_mm"), 1)

            for q, (half, kq, g0) in enumerate(KEY_QUADS):
                pe.wait_ge(S("codes"), half + 1)
                if q >= 2:
                    pe.wait_ge(S("keys"), q - 1)
                for g in range(g0, min(g0 + 4, WG)):
                    t = nc.tensor.transpose(ps[:, 5 + q % 2, (g - g0) * WP:(g - g0 + 1) * WP],
                                            wa[kq][:, g * CAP:(g + 1) * CAP], ident[0:WP, 0:WP])
                t.then_inc(S("keys_t"), 1)
            pe.wait_ge(S("keys"), 12)
            pe.wait_ge(S("wt_copied"), 4)
            pe.wait_ge(S("heads_copied"), 1)

            transposes("l0h", lambda b: hn[:, b, :], once(("ln_ln", 2)))

            with pe.Fori(0, NCH) as i:
                for gr in range(GC):
                    s = gr % 2
                    pe.wait_ge(S("oh_ready"), i * GC + gr + 1)
                    for w in range(GW):
                        q = w // QW
                        if w % QW == 0:
                            pe.wait_ge(S("stage_ready"), i * (GC * GQ) + gr * GQ + q + 1)
                        at = w % QW % 2 * 256
                        t = mm(ps[:, q * 4 + w % QW // 2, at:at + CELL1], oh[:, s, w, 0:P], oh[:, s, w, P:OHW],
                               start=True, stop=True)
                        if w % QW == QW - 1:
                            t.then_inc(S("batch_mm"), 1)

            pe.wait_ge(S("cnt8"), 1)
            pe.wait_ge(S("batches_done"), 1)
            for q in range(8):
                d, g0 = q // 4, 4 * (q % 4)
                if q >= 2:
                    pe.wait_ge(S("cnt_copied"), q - 1)
                for g in range(g0, min(g0 + 4, WG)):
                    t = nc.tensor.transpose(ps[0:KT, 3 + q % 2, (g - g0) * WP:(g - g0 + 1) * WP],
                                            cnt8[:, g, d * KT:(d + 1) * KT], ident[0:WP, 0:WP])
                t.then_inc(S("cnt_t"), 1)

            pe.wait_ge(S("cnt_copied"), 8)
            pe.wait_ge(S("fl_a"), 1)
            mm(ps[0:1, 5, 0:1], fl[0:WP, 0:1], ones[0:WP, 0:1], start=True, stop=True)
            nc.tensor.transpose(ps[0:1, 5, 128:256], fl[:, 1:2], ident[:, :]).then_inc(S("fl_b"), 1)
            pe.wait_ge(S("flag"), 1)
            fast = pe.value_load(flag_i[:, :], min_val=0, max_val=1)

            def general(name, parts, types=1):
                with pe.If(fast < 1):
                    pe.wait_ge(S("g_zero"), GCALL.index(name) + 1)
                    for k in range(types):
                        n = GP[name] + k
                        rows = KT if name == "count" else P
                        for c in range(NCH):
                            mm(ps[0:rows, c, 0:CH], g_zero[:, 0:rows], g_zero[:, :], start=True, stop=False, skip_group_check=True)
                        with pe.Fori(0, EC) as e:
                            pe.wait_ge(S("g_hot"), e + n * EC + 1)
                            pe.sem_inc(S("pe_passed"), 1)
                            if name != "count":
                                pe.wait_ge(S(f"g_x{(n - 1) // GX}"), e * 16 + ((n - 1) % GX * EC + 1) * 16)
                                pe.sem_inc(S("pe_passed"), 1)
                            for r in range(parts):
                                lhs = g_thot if name == "count" else g_x[:, r * D:(r + 1) * D]
                                for c in range(NCH):
                                    t = mm(ps[0:rows, c, 0:CH], lhs, g_hot[:, c * CH:(c + 1) * CH], start=False, stop=False,
                                           skip_group_check=True)
                            t.then_inc(S("g_mm"), 1)
                        pe.wait_ge(S("g_evac"), n + 1)

            general("count", 1)

            def degree_row(n0, used):
                for c in range(NCH):
                    if n0 + c >= 2:
                        pe.wait_ge(S(used), n0 + c - 1)
                    mm(ps[:, 6 + (n0 + c) % 2, 0:CH], ones[0:KT, :], cntT[:, c * CH:(c + 1) * CH], start=True, stop=True
                       ).then_inc(S("deg_mm"), 1)

            degree_row(0, "deg_used")
            for b in range(NB):
                t = mm(ps[:, 5, b:b + 1], cntT[:, b * P:(b + 1) * P], ones[0:KT, 0:1], start=True, stop=True)
            t.then_inc(S("degn"), 1)
            def accumulate(bank, slot, sem, ready={}):
                with pe.If(fast > 0):
                    for b in range(NB):
                        if b in ready:
                            pe.wait_ge(S(ready[b][0]), ready[b][1])
                        for r in range(2):
                            t = mm(ps[:, bank, 0:CH].rearrange("p (g d) -> p g d", d=GD), op[:, b, r, :], ring8[:, slot, b],
                                   start=(b == 0 and r == 0), stop=(b == NB - 1 and r == 1))
                    t.then_inc(S(sem), 1)
                with pe.Else():
                    mm(ps[:, bank, 0:CH], ident[:, :], ringf[:, slot, :], start=True, stop=True).then_inc(S(sem), 1)

            def gate(sem, value):
                pe.wait_ge(sem, value)
                pe.sem_inc(S("pe_passed"), 1)

            def in_halves(sem, n):
                return {lo: (sem, n - 1 + h) for h, (lo, _) in enumerate(HALVES)}

            def untyped(name, ready):
                general(name, 2)
                turns = (AGG[name] * (NCH // 2 + 1), AGG[name] * (NCH // 2))

                def chunk(s, i):
                    gate(S(f"ag_piece{s}"), (i + turns[s] + 1) * 16)
                    gate(S(f"ag_bank{s}"), i + turns[s] + 1)
                    accumulate(s, s, f"ag_mm{s}", ready)
                with pe.Fori(0, NCH // 2) as i:
                    for s in range(2):
                        chunk(s, i)
                chunk(0, NCH // 2)

            def blocks(name, ready, terms, bank0=2):
                n0 = BLK[name] * NQ
                for q in range(NQ):
                    ready(q)
                    if n0 + q >= 2:
                        pe.wait_ge(S("blk_used"), n0 + q - 1)
                    for b in range(4 * q, min(4 * q + 4, NB)):
                        ts = terms(b)
                        for j, (l, r) in enumerate(ts):
                            t = mm(ps[:, bank0 + q % 2, (b % 4) * P:(b % 4 + 1) * P], l, r,
                                   start=(j == 0), stop=(j == len(ts) - 1))
                    t.then_inc(S("blk_mm"), 1)

            def blk(Tb):
                return lambda b: Tb[:, b * P:(b + 1) * P]

            def posted(n):
                return lambda q: pe.wait_ge(S("ag_post"), n * NCH - int(q < EARLY))

            def normed(n):
                return lambda q: pe.wait_ge(S("ln_ln"), n - int(4 * q < HALVES[0][1]))

            def largest(name, use):
                pe.wait_ge(S("scale_in"), 2 * use + 1)
                nc.tensor.transpose(ps[0:1, 4, 0:P], sc[:, 0:1], ident[:, :]).then_inc(S("scale_mm"), 1)
                pe.wait_ge(S("scale_in"), 2 * use + 2)
                mm(ps[:, 4, P:P + 1], ones[0:1, :], sc[0:1, 1:2], start=True, stop=True).then_inc(S("scale_mm"), 1)

            untyped("l0a", in_halves("ln_op", 2))
            pe.wait_ge(S("tr_copied"), NQ)
            with pe.Fori(0, NCH) as c:
                gate(S("ag_post"), c + 1)
                for m in range(2):
                    pe.wait_ge(S(f"l0d_bank{m}"), c + 1)
                    mm(ps[:, 2 + m, 0:CH], wl1[:, m * D:(m + 1) * D], T1[:, bass.ds(c * CH, CH)], start=True, stop=False)
                    mm(ps[:, 2 + m, 0:CH], wr1[:, m * D:(m + 1) * D], T0[:, bass.ds(c * CH, CH)], start=False, stop=True
                       ).then_inc(S("l0d"), 1)
            blocks("l0p", once(("l0d_copied", 2 * NCH)), lambda b: [(blk(T2)(b), wl2[:, 0, :]), (blk(T3)(b), wl2[:, 1, :])])
            largest("l0p", 0)
            untyped("l0b", in_halves("q_op", 2))
            blocks("l0o", posted(2), lambda b: [
                (blk(T1)(b), ident[:, :]), (blk(T2)(b), wr2[:, 0, :]), (blk(T3)(b), wr2[:, 1, :])])

            pe.wait_ge(S("deg_used"), NCH)
            degree_row(0, "deg_copied")
            degree_row(NCH, "deg_copied")
            pe.wait_ge(S("deg_copied"), 2 * NCH)
            transposes("l1h", lambda b: hn[:, b, :], normed(4))
            pe.wait_ge(S("tr_copied"), 2 * NQ)
            for c in range(NCH):
                if c >= 2:
                    pe.wait_ge(S("msg_bias"), c - 1)
                mm(ps[:, 6 + c % 2, 0:CH], bet[:, :], cntT[:, c * CH:(c + 1) * CH], start=True, stop=True).then_inc(S("msg_bias_mm"), 1)
            pe.wait_ge(S("msg_bias"), NCH)
            def after_step(step):
                def wait(q):
                    pe.wait_ge(S("gru_h"), (step + 1) * NCH + int(q >= EARLY))
                    if q == 2:
                        pe.wait_ge(S("gru_z"), (step + 1) * NCH)
                return wait

            for step in range(NSTEP):
                ready = {4 * q: ("tr_copied", (step + 1) * NQ + q + 1) for q in range(NQ)} if step else in_halves("ln_op", 4)
                general(f"l1s{step}", 2, KT)
                with pe.Fori(0, NCH) as i:
                    c = i + step * NCH
                    for k in range(KT):
                        gate(S(f"ty_piece{k}"), c * 16 + 16)
                        gate(S(f"ty_bank{k % 2}"), c * 2 + k // 2 + 1)
                        accumulate(k % 2, k, f"ty_mm{k}", ready if k == 0 else {})
                    hc = T1[:, bass.ds(i * CH, CH)]
                    pe.wait_ge(S("gru_h"), c + 1)
                    mm(ps[:, 3, 0:CH], WT[:, HH + 0, :], hc, start=True, stop=False)
                    mm(ps[:, 4, 0:CH], WT[:, HH + 1, :], hc, start=True, stop=False)
                    mm(ps[:, 5, 0:CH], WT[:, HH + 2, :], hc, start=True, stop=True)
                    for k in range(KT):
                        pe.wait_ge(S("ty_sum"), c * KT + k + 1)
                        t = mm(ps[:, 2, 0:CH], WT[:, ET + k, :], tmp[:, k, :], start=(k == 0), stop=(k == KT - 1))
                    t.then_inc(S("gru_msg"), 1)
                    pe.wait_ge(S("gru_a"), c + 1)
                    mm(ps[:, 3, 0:CH], WT[:, IH + 0, :], tmp[:, 4, :], start=False, stop=True).then_inc(S("gru_mm"), 1)
                    mm(ps[:, 4, 0:CH], WT[:, IH + 1, :], tmp[:, 4, :], start=False, stop=True).then_inc(S("gru_mm"), 1)
                    mm(ps[:, 6, 0:CH], WT[:, IH + 2, :], tmp[:, 4, :], start=True, stop=True).then_inc(S("gru_mm"), 1)
                if step < NSTEP - 1:
                    transposes(f"l1t{step}", blk(T1), after_step(step), STEP_BANKS)
            for q in range(NQ):
                pe.wait_ge(S("gru_h"), NSTEP * NCH + int(q >= EARLY))
                if q >= 2:
                    pe.wait_ge(S("l1o_used"), q - 1)
                for b in range(4 * q, min(4 * q + 4, NB)):
                    og = ps[:, OUT_BANKS[q % 2][0], (b % 4) * P:(b % 4 + 1) * P]
                    ov = ps[:, OUT_BANKS[q % 2][1], (b % 4) * P:(b % 4 + 1) * P]
                    mm(og, blk(T1)(b), WT[:, IW, :], start=True, stop=False)
                    mm(og, blk(T0)(b), WT[:, IW + 1, :], start=False, stop=False)
                    mm(og, ones[0:1, :], brow[:, BI, :], start=False, stop=True)
                    t = mm(ov, blk(T1)(b), WT[:, JW, :], start=True, stop=True)
                t.then_inc(S("l1o_mm"), 1)

            transposes("l2h", lambda b: hn[:, b, :], normed(6))
            untyped("l2a", in_halves("ln_op", 6))
            for c in range(NCH):
                pe.wait_ge(S("ag_post"), 2 * NCH + c + 1)
                if c >= 2:
                    pe.wait_ge(S("l2d_bias"), c - 1)
                mm(ps[:, 2 + c % 2, 0:CH], w1[:, :], T1[:, c * CH:(c + 1) * CH], start=True, stop=True).then_inc(S("l2d"), 1)
            blocks("l2p", once(("l2d_done", NCH)), lambda b: [(blk(T2)(b), w2[:, :])])
            largest("l2p", 1)
            untyped("l2b", in_halves("q_op", 4))
            blocks("l2o", posted(4), lambda b: [(blk(T1)(b), ident[:, :])])

            untyped("l3a", in_halves("ln_op", 8))
            blocks("l3o", posted(5), lambda b: [(blk(T1)(b), WT[:, W3, :])])

        @block.scalar
        def _(act):
            A = nc.scalar.activation
            act.dma_start(x_nm[:, 0:NB - 1, :], a["x"][0:(NB - 1) * P, :].rearrange("(b p) d -> p b d", p=P)).then_inc(S("x_in"), 16)
            raw = [("L1_gnn_W_et", lambda w: w.rearrange("k o d -> o k d"), 0, 4),
                   ("L1_gnn_W_ih", lambda w: w.rearrange("(g o) d -> o g d", o=D), 4, 7),
                   ("L1_gnn_W_hh", lambda w: w.rearrange("(g o) d -> o g d", o=D), 7, 10),
                   ("L1_gnn_i_w", lambda w: w.rearrange("g (h d) -> g h d", d=D), 10, 12)]
            for name, f, lo, hi in raw:
                act.dma_start(raww[:, lo:hi, :], f(a[name])).then_inc(S("raw_in"), 16)
            act.dma_start(raww[:, 12, :], a["L1_gnn_j_w"]).then_inc(S("raw_in"), 16)
            act.dma_start(raww[:, 13, :], a["L3_gnn_W"]).then_inc(S("raw_in"), 16)
            act.dma_start(wl1[:, :], a["L0_gnn_W_l1"]).then_inc(S("w_in"), 16)
            act.dma_start(wr1[:, :], a["L0_gnn_W_r1"]).then_inc(S("w_in"), 16)
            act.dma_start(wl2[:, :, :], a["L0_gnn_W_l2"].rearrange("(h d) o -> d h o", d=D)).then_inc(S("w_in"), 16)
            act.dma_start(wr2[:, :, :], a["L0_gnn_W_r2"].rearrange("(h d) o -> d h o", d=D)).then_inc(S("w_in"), 16)
            act.dma_start(w1[:, :], a["L2_gnn_W1"]).then_inc(S("w_in"), 16)
            act.dma_start(w2[:, :], a["L2_gnn_W2"]).then_inc(S("w_in"), 16)
            act.dma_start(bet[:, :], a["L1_gnn_b_et"]).then_inc(S("w_in"), 16)
            for name, lo, n in (("L0_gnn_b_l1", 0, 2), ("L1_gnn_b_ih", 2, 3), ("L1_gnn_b_hh", 5, 3), ("L2_gnn_b1", 8, 1)):
                act.dma_start(bcol[:, lo:lo + n], a[name].rearrange("(g o) -> o g", o=D)).then_inc(S("w_in"), 16)
            for i, name in enumerate(("L0_gnn_b_l2", "L1_gnn_i_b", "L1_gnn_j_b", "L2_gnn_b2", "L3_gnn_b")):
                act.dma_start(brow[:, i, :], a[name].rearrange("(o d) -> o d", o=1)).then_inc(S("brow_in"), 16)
            act.wait_ge(S("x_pad"), 1)
            act.dma_start(x_nm[0:NLAST, NB - 1, :], a["x"][(NB - 1) * P:N, :]).then_inc(S("x_in"), 16)

            for q in range(4):
                act.wait_ge(S("wt"), q + 1)
                n = min(4, 14 - 4 * q)
                A(WT[:, 4 * q:4 * q + n, :].rearrange("p a b -> p (a b)"), ps[:, 1 + q % 2, 0:n * P], ACT.Copy).then_inc(S("wt_copied"), 1)
            act.wait_ge(S("w_in"), 16 * 11)
            act.wait_ge(S("bias_mm"), 1)
            A(biasb[:, 0:4, :].rearrange("p a b -> p (a b)"), ps[:, 3, 0:4 * D], ACT.Copy)
            A(biasb[:, 4, :], ps[:, 4, 0:D], ACT.Copy).then_inc(S("bias_copied"), 1)

            def square(name, q):
                lo, hi = QUADS[q]
                act.wait_ge(S("ln_centred"), LN[name] * NQ + q + 1)
                A(squares[:, lo * D:hi * D], hn[:, lo:hi, :].rearrange("p a b -> p (a b)"), ACT.Square).then_inc(S("ln_squared"), 1)

            def layernorm(name, after_squares=None, after_roots=None, first=0):
                n = 2 * LN[name] + 1
                for q in range(first, NQ):
                    square(name, q)
                if after_squares is not None:
                    after_squares()
                for h, (lo, hi) in enumerate(HALVES):
                    act.wait_ge(S("ln_var"), n + h)
                    A(st[:, 2, lo:hi], st[:, 1, lo:hi], ACT.Sqrt, bias=epsc[:, 0:1], scale=1.0 / D).then_inc(S("ln_std"), 1)
                if after_roots is not None:
                    after_roots()
                for h, (lo, hi) in enumerate(HALVES):
                    act.wait_ge(S("ln_ln"), n + h)
                    A(op[:, lo:hi, 0, :], hn[:, lo:hi, :], ACT.Relu).then_inc(S("ln_high"), 1)

            def copy_blocks(name, dst):
                for q in range(NQ):
                    n = min(4, NB - 4 * q) * P
                    act.wait_ge(S("tr_mm"), TR[name] * NQ + q + 1)
                    A(dst(q, n), ps[:, 6 + q % 2, 0:n], ACT.Relu).then_inc(S("tr_copied"), 1)

            def high_part(use):
                act.wait_ge(S("scaled"), use + 1)
                for lo, hi in HALVES:
                    A(op[:, lo:hi, 0, :], hn[:, lo:hi, :], ACT.Copy, scale=sc[:, 3:4]).then_inc(S("q_high"), 1)

            cols = lambda Tb: (lambda q, n: Tb[:, 4 * q * P:4 * q * P + n])

            layernorm("l0")
            for q, (half, kq, g0) in enumerate(KEY_QUADS):
                n = min(4, WG - g0)
                act.wait_ge(S("keys_t"), q + 1)
                A(keys[:, kq, g0 * WP:(g0 + n) * WP, :], ps[:, 5 + q % 2, 0:n * WP].unsqueeze(2).broadcast_to([P, n * WP, 2]),
                  ACT.Copy).then_inc(S("keys"), 1)

            copy_blocks("l0h", cols(T0))

            act.sem_inc(S("stage_ready"), 2)
            with act.Fori(0, NCH) as i:
                for gr in range(GC):
                    s = gr % SS
                    act.wait_ge(S(f"stage_out{s}"), i * (GC // SS * 16) + (gr // SS + 1) * 16)
                    act.sem_inc(S("act_passed"), 1)
                    for q in range(GQ):
                        act.wait_ge(S("batch_mm"), i * (GC * GQ) + gr * GQ + q + 1 + 2 * GQ)
                        act.sem_inc(S("act_passed"), 1)
                        src = ps[:, q * 4:q * 4 + 4, :].rearrange("p b (h c) -> p (b h) c", h=2)[:, :, 0:CELL1]
                        src = src.rearrange("p w (c d) -> p c w d", d=WD)
                        dst = stage8[s][:, :, QW * WD * q:QW * WD * (q + 1)].rearrange("p c (w d) -> p c w d", w=QW)
                        A(dst, src, ACT.Copy, saturate=False).then_inc(S("stage_ready"), 1)
            act.wait_ge(S("stage_ready"), NG * GQ + 2)
            act.sem_inc(S("batches_done"), 1)
            act.wait_ge(S("cnt_pad"), 1)
            for q in range(8):
                d, g0 = q // 4, 4 * (q % 4)
                n = min(4, WG - g0)
                act.wait_ge(S("cnt_t"), q + 1)
                dst = cntT[:, g0 * WP * WD:(g0 + n) * WP * WD].rearrange("k (w d) -> k w d", d=WD)[:, :, d]
                A(dst, ps[0:KT, 3 + q % 2, 0:n * WP], ACT.Copy).then_inc(S("cnt_copied"), 1)

            act.wait_ge(S("degn"), 1)
            A(dis_nm[:, :], ps[:, 5, 0:NB], ACT.Sqrt, bias=ones[:, 0:1]).then_inc(S("degn_root"), 1)

            for m in range(2):
                act.sem_inc(S(f"l0d_bank{m}"), 1)
            act.wait_ge(S("t_pads"), 1)
            with act.Fori(0, NCH) as c:
                for m in range(2):
                    act.wait_ge(S("l0d"), c * 2 + m + 1)
                    A((T2, T3)[m][:, bass.ds(c * CH, CH)], ps[:, 2 + m, 0:CH], ACT.Identity, bias=bcol[:, m:m + 1]
                      ).then_inc(S("l0d_copied"), 1)
                    act.wait_ge(S("l0d_copied"), c * 2 + m + 1)
                    act.sem_inc(S(f"l0d_bank{m}"), 1)

            high_part(0)

            def degrees(n0, f):
                def copies():
                    for c in range(NCH):
                        act.wait_ge(S("deg_mm"), NCH + n0 + c + 1)
                        f(slice(c * CH, (c + 1) * CH), ps[:, 6 + (n0 + c) % 2, 0:CH]).then_inc(S("deg_copied"), 1)
                return copies

            layernorm("l1", degrees(0, lambda cc, p: A(T3[:, cc], p, ACT.Copy)),
                      degrees(NCH, lambda cc, p: A(row[:, cc], p, ACT.Sqrt, bias=ones[:, 0:1])))
            for q in range(NQ):
                n = min(4, NB - 4 * q) * P
                act.wait_ge(S("tr_mm"), TR["l1h"] * NQ + q + 1)
                A(T0[:, 4 * q * P:4 * q * P + n], ps[:, 6 + q % 2, 0:n], ACT.Relu)
                A(T1[:, 4 * q * P:4 * q * P + n], ps[:, 6 + q % 2, 0:n], ACT.Relu).then_inc(S("tr_copied"), 1)
            for c in range(NCH):
                act.wait_ge(S("msg_bias_mm"), c + 1)
                A(T2[:, c * CH:(c + 1) * CH], ps[:, 6 + c % 2, 0:CH], ACT.Copy).then_inc(S("msg_bias"), 1)
            for step in range(NSTEP):
                with act.Fori(0, NCH) as i:
                    c = i + step * NCH
                    for k in range(KT):
                        act.wait_ge(S(f"ty_mm{k}"), c + 2)
                        A(tmp[:, k, :], ps[:, k % 2, 0:CH], ACT.Copy).then_inc(S("ty_sum"), 1)
                        act.wait_ge(S("ty_sum"), c * KT + k + 1)
                        act.sem_inc(S(f"ty_bank{k % 2}"), 1)
                    act.wait_ge(S("gru_mm"), c * 3 + 1)
                    A(tmp[:, 5, :], ps[:, 3, 0:CH], ACT.Sigmoid, bias=brz[:, 0:1]).then_inc(S("gru_r"), 1)
                    act.wait_ge(S("gru_mm"), c * 3 + 2)
                    A(tmp[:, 6, :], ps[:, 4, 0:CH], ACT.Sigmoid, bias=brz[:, 1:2]).then_inc(S("gru_z"), 1)
                    act.wait_ge(S("gru_pre"), c + 1)
                    A(tmp[:, 8, :], tmp[:, 7, :], ACT.Tanh, bias=bcol[:, 4:5]).then_inc(S("gru_n"), 1)
                if step < NSTEP - 1:
                    for q in range(NQ):
                        n = min(4, NB - 4 * q)
                        act.wait_ge(S("tr_mm"), TR[f"l1t{step}"] * NQ + q + 1)
                        A(op[:, 4 * q:4 * q + n, 0, :], ps[:, STEP_BANKS[q % 4], 0:n * P].rearrange("p (b d) -> p b d", d=D), ACT.Copy
                          ).then_inc(S("high"), 1)
            act.wait_ge(S("gru_h"), NSTEP * NCH + 1)
            for q in range(NQ):
                n = min(4, NB - 4 * q) * P
                act.wait_ge(S("l1o_mm"), q + 1)
                if q >= 2:
                    act.wait_ge(S("l1o_used"), q - 1)
                A(sig2[:, q % 2, 0:n], ps[:, OUT_BANKS[q % 2][0], 0:n], ACT.Sigmoid
                  ).then_inc(S("l1o_sig"), 1)
                if q >= 1:
                    square("l2", q - 1)

            layernorm("l2", first=NQ - 1)
            copy_blocks("l2h", cols(T0))
            for c in range(NCH):
                act.wait_ge(S("l2d"), c + 1)
                A(T2[:, c * CH:(c + 1) * CH], ps[:, 2 + c % 2, 0:CH], ACT.Identity, bias=bcol[:, 8:9]).then_inc(S("l2d_bias"), 1)
            high_part(1)
            layernorm("l3")

        @block.vector
        def _(dve):
            v = nc.vector
            link = Chain(dve, S("dve_chain"))
            v.memset(ones[:, :], 1.0).then_inc(S("ones"), 1)
            link(v.memset(epsc[:, :], EPS))
            v.memset(x_nm[:, NB - 1, :], 0.0).then_inc(S("x_pad"), 1)
            v.memset(cntT[:, :], 0.0).then_inc(S("cnt_pad"), 1)
            dve.wait_ge(S("consts"), 2)
            v.tensor_copy(iota16[:, :], iota_i[:, :])
            link(v.tensor_copy(wbase[:, :], wbase_i[:, :]))
            dve.wait_ge(S("heads_in"), 16)
            v.tensor_copy(rf[:, :], rf_i[:, :]).then_inc(S("heads"), 1)
            dve.wait_ge(S("edges_in"), 48)
            link(v.tensor_scalar(e_dst, e_dst, 14, None, ALU.logical_shift_left))
            link(v.tensor_scalar(e_typ, e_typ, 12, None, ALU.logical_shift_left))
            link(v.tensor_tensor(e_dst, e_dst, e_typ, ALU.bitwise_or))
            v.tensor_tensor(e_dst, e_dst, e_src, ALU.bitwise_or).then_inc(S("pack_ready"), 1)

            dve.wait_ge(S("heads_mm"), 1)
            v.tensor_copy(rfb[:, :], ps[:, 0, 0:ER]).then_inc(S("heads_copied"), 1)
            dve.wait_ge(S("heads_copied"), 1)
            for w in range(WG):
                t = v.tensor_scalar(junk[:, 0:ER], rfb[0:WP, :], wbase[:, w:w + 1], None, ALU.is_lt, ALU.add,
                                    accum_out=small[0:WP, 0, w:w + 1])
                link(t)
            link(v.tensor_scalar(small[0:WP, 1, :], small[0:WP, 0, :], -1.0, 0.0, ALU.add, ALU.max))
            v.tensor_copy(small_i[0:WP, 0, :], small[0:WP, 1, :]).then_inc(S("rowidx"), 1)
            for w in range(WG):
                dve.wait_ge(S(f"row_in{w % 4}"), 16 * (w // 4 + 1))
                link(v.tensor_scalar(junk, rows_i[w % 4], wbase[:, w:w + 1], None, ALU.is_lt, ALU.add,
                                     accum_out=small[0:WP, 2, w:w + 1]))
                dve.sem_inc(S("row_used"), 1)
            link(v.scalar_tensor_tensor(out=small[0:WP, 3, :], in0=small[0:WP, 1, :], scalar=float(EC), in1=small[0:WP, 2, :],
                                        op0=ALU.mult, op1=ALU.add))
            v.tensor_copy(small_i[0:WP, 1, :], small[0:WP, 3, :]).then_inc(S("startidx"), 1)

            def wide(col):
                return col.unsqueeze(2).broadcast_to([P, col.shape[1], D])

            def centre(name, q):
                lo, hi = QUADS[q]
                link(v.tensor_reduce(st[:, 0, lo:hi], x_nm[:, lo:hi, :], AX.X, ALU.add))
                link(v.tensor_scalar(st[:, 0, lo:hi], st[:, 0, lo:hi], 1.0 / D, None, ALU.mult))
                v.tensor_tensor(hn[:, lo:hi, :], x_nm[:, lo:hi, :], wide(st[:, 0, lo:hi]), ALU.subtract).then_inc(S("ln_centred"), 1)
                for r in ([q - 1] if q > 0 else []) + ([q] if q == NQ - 1 else []):
                    lo, hi = QUADS[r]
                    dve.wait_ge(S("ln_squared"), LN[name] * NQ + r + 1)
                    t = v.tensor_reduce(st[:, 1, lo:hi], squares.rearrange("p (a b) -> p a b", b=D)[:, lo:hi, :], AX.X, ALU.add)
                    if hi in (HALVES[0][1], NB):
                        t.then_inc(S("ln_var"), 1)

            def layernorm(name, scale=None):
                n = 2 * LN[name] + 1
                for h, (lo, hi) in enumerate(HALVES):
                    dve.wait_ge(S("ln_std"), n + h)
                    link(v.reciprocal(st[:, 3, lo:hi], st[:, 2, lo:hi]))
                    if scale is not None:
                        link(v.tensor_tensor(st[:, 3, lo:hi], st[:, 3, lo:hi], scale[:, lo:hi], ALU.mult))
                    v.tensor_tensor(hn[:, lo:hi, :], hn[:, lo:hi, :], wide(st[:, 3, lo:hi]), ALU.mult).then_inc(S("ln_ln"), 1)
                for h, (lo, hi) in enumerate(HALVES):
                    dve.wait_ge(S("ln_high"), n + h)
                    v.scalar_tensor_tensor(out=op[:, lo:hi, 1, :], in0=hn[:, lo:hi, :], scalar=0.0, in1=op[:, lo:hi, 0, :],
                                           op0=ALU.max, op1=ALU.subtract).then_inc(S("ln_op"), 1)

            dve.wait_ge(S("x_in"), 32)
            dve.wait_ge(S("wt_copied"), 4)
            for q in range(NQ):
                centre("l0", q)
            layernorm("l0")

            I = lambda t: t.bitcast(I32)
            for h, (g0, g1) in enumerate(WHALVES):
                pk, ct, cu, ty, rel, m = (wa[i][:, g0 * CAP:g1 * CAP] for i in (0, 1, 2, 3, 4, 5))
                dve.wait_ge(S(f"windows_in{h}"), 16 * (g1 - g0))
                link(v.tensor_scalar(I(m), I(pk), 14, None, ALU.logical_shift_right))
                r3 = lambda t: t.rearrange("p (g e) -> p g e", e=CAP)
                link(v.tensor_tensor(r3(rel), r3(I(m)), wbase[:, g0:g1].unsqueeze(2).broadcast_to([WP, g1 - g0, CAP]), ALU.subtract))
                link(v.tensor_scalar(I(ty), I(pk), 12, 3, ALU.logical_shift_right, ALU.bitwise_and))
                link(v.tensor_scalar(I(m), I(pk), 7, 31, ALU.logical_shift_right, ALU.bitwise_and))
                link(v.scalar_tensor_tensor(out=cu, in0=I(m), scalar=float(WD), in1=rel, op0=ALU.mult, op1=ALU.add))
                link(v.scalar_tensor_tensor(out=ct, in0=I(ty), scalar=float(NB * WD), in1=cu, op0=ALU.mult, op1=ALU.add))
                link(v.tensor_scalar(I(m), I(pk), 127, None, ALU.bitwise_and))
                link(v.tensor_scalar(pk, I(m), 1.0, None, ALU.add))
                link(v.tensor_scalar(m, rel, 0.0, None, ALU.is_ge))
                link(v.scalar_tensor_tensor(out=m, in0=rel, scalar=float(WD), in1=m, op0=ALU.is_lt, op1=ALU.mult))
                link(v.scalar_tensor_tensor(out=cu, in0=cu, scalar=1.0, in1=m, op0=ALU.add, op1=ALU.mult))
                v.scalar_tensor_tensor(out=ct, in0=ct, scalar=1.0, in1=m, op0=ALU.add, op1=ALU.mult).then_inc(S("codes"), 1)
            rel, ty, m = wa[4], wa[3], wa[5]
            dve.wait_ge(S("codes"), 2)
            link(v.tensor_reduce(fl[0:WP, 0:1], m, AX.X, ALU.add))
            link(v.scalar_tensor_tensor(out=rel, in0=rel, scalar=float(KT), in1=I(ty), op0=ALU.mult, op1=ALU.add))
            v.scalar_tensor_tensor(out=rel, in0=rel, scalar=1.0, in1=m, op0=ALU.add, op1=ALU.mult).then_inc(S("pair_codes"), 1)
            dve.sem_inc(S("batch_mm"), 2 * GQ)
            dve.wait_ge(S("keys"), 12)
            dve.wait_ge(S("tr_copied"), NQ)
            link(v.memset(oh[:, :, :, P + CELL:OHW], 1.0))
            for z in range(SS - 3, SS):
                link(v.memset(stage[z][:, SB:SB1], 0))

            def most(z, g):
                return v.tensor_reduce(rowmax[:, g], stage[z % SS][:, SB:SB1], AX.X, ALU.max)
            with dve.Fori(0, NCH) as i:
                for gr in range(GC):
                    s = gr % 2
                    dve.wait_ge(S("batch_mm"), i * (GC * GQ) + (gr + 1) * GQ)
                    most(gr - 3, bass.ds(i * GC + gr, 1))
                    o = oh[:, s, :, :]
                    key = lambda q, n: keys[:, q, bass.ds(i * (GC * GW) + gr * GW, GW), :].unsqueeze(2).broadcast_to([P, GW, n // 2, 2])
                    cols = lambda lo, n: o[:, :, lo:lo + n].rearrange("p w (c two) -> p w c two", two=2)
                    for q, lo, n in ((0, 0, P), (1, P, TCELL), (2, P + TCELL, CELL - TCELL)):
                        t = v.tensor_tensor(cols(lo, n), pairs(n), key(q, n), ALU.is_equal)
                    t.then_inc(S("oh_ready"), 1)
            dve.wait_ge(S("stage_ready"), NG * GQ + 2)
            for z in range(3):
                link(most(NG - 3 + z, slice(NG + z, NG + z + 1)))
            v.tensor_reduce(fl[:, 1:2], rowmax[:, :], AX.X, ALU.max).then_inc(S("fl_a"), 1)

            dve.wait_ge(S("fl_b"), 1)
            link(v.tensor_scalar(fl[0:1, 2:3], ps[0:1, 5, 0:1], float(E), None, ALU.is_equal))
            link(v.tensor_reduce(fl[0:1, 3:4], ps[0:1, 5, 128:256], AX.X, ALU.max))
            link(v.tensor_scalar(fl[0:1, 4:5], fl[0:1, 3:4], float(ROW_CODE), None, ALU.is_le))
            link(v.tensor_tensor(fl[0:1, 5:6], fl[0:1, 2:3], fl[0:1, 4:5], ALU.mult))
            v.tensor_copy(flag_i[:, :], fl[0:1, 5:6]).then_inc(S("flag"), 1)
            dve.wait_ge(S("flag"), 1)
            fast = dve.value_load(flag_i[:, :], min_val=0, max_val=1)
            g_link = Chain(dve, S("g_chain"))

            def general(name, types=1):
                with dve.If(fast < 1):
                    dve.wait_ge(S("g_edges"), 48 * (GCALL.index(name) + 1))
                    dve.wait_ge(S("g_iota"), GCALL.index(name) + 1)
                    if name == "count":
                        dve.sem_inc(S("g_mm"), 1)
                    g_link(v.tensor_copy(g_iota, g_iota.bitcast(I32)))
                    g_link(v.tensor_copy(g_dst.bitcast(F32), g_dst))
                    g_link(v.tensor_copy(g_typ.bitcast(F32), g_typ))
                    v.memset(g_zero, 0.0).then_inc(S("g_zero"), 1)
                    for k in range(types):
                        n = GP[name] + k
                        if types > 1:
                            g_link(v.tensor_scalar(g_key, g_typ.bitcast(F32), float(k), 4096.0, ALU.not_equal, ALU.mult))
                            g_link(v.tensor_tensor(g_key, g_key, g_dst.bitcast(F32), ALU.add))
                        else:
                            g_link(v.tensor_copy(g_key, g_dst.bitcast(F32)))
                        with dve.Fori(0, EC) as e:
                            dve.wait_ge(S("g_mm"), e + n * EC + 1)
                            v.tensor_copy(g_idx, g_src[:, bass.ds(e, 1)]).then_inc(S("g_idx"), 1)
                            if name == "count":
                                v.tensor_scalar(g_thot, g_iota[:, 0:KT], g_typ.bitcast(F32)[:, bass.ds(e, 1)], None, ALU.is_equal)
                            v.tensor_scalar(g_hot, g_iota, g_key[:, bass.ds(e, 1)], None, ALU.is_equal).then_inc(S("g_hot"), 1)
                        dve.wait_ge(S("g_mm"), (n + 1) * EC + 1)
                        if n > 1:
                            dve.wait_ge(S("g_sums"), 16 * (n - 1))
                        for c in range(NCH):
                            if name == "count":
                                t = v.tensor_copy(cntT[:, c * CH:(c + 1) * CH], ps[0:KT, c, 0:CH])
                            else:
                                t = v.tensor_copy(g_out[:, c * CH:(c + 1) * CH], ps[:, c, 0:CH])
                        t.then_inc(S("g_evac"), 1)
                        dve.wait_ge(S("g_evac"), n + 1)

            general("count")

            def mean_row():
                for c in range(NCH):
                    dve.wait_ge(S("deg_mm"), c + 1)
                    v.tensor_scalar(row[:, c * CH:(c + 1) * CH], ps[:, 6 + c % 2, 0:CH], 1.0, None, ALU.max).then_inc(S("deg_used"), 1)
                dve.wait_ge(S("deg_used"), NCH)
                link(v.reciprocal(row[:, :], row[:, :]))

            dve.wait_ge(S("adjacency_out"), 1)
            for s in range(2):
                dve.sem_inc(S(f"ag_bank{s}"), 1)
                dve.sem_inc(S(f"ty_bank{s}"), 1)
            dve.sem_inc(S("gru_h"), 1)
            mean_row()
            dve.wait_ge(S("degn_root"), 1)
            link(v.tensor_scalar(deg_nm[:, :], ps[:, 5, 0:NB], 1.0, None, ALU.max))
            link(v.reciprocal(rdeg_nm[:, :], deg_nm[:, :]))
            link(v.reciprocal(dis_nm[:, :], dis_nm[:, :]))
            dve.wait_ge(S("w_in"), 16 * 11)
            link(v.tensor_tensor(brz[:, :], bcol[:, 2:4], bcol[:, 5:7], ALU.add))
            for Tb in (T1, T2, T3):
                t = v.memset(Tb[:, NT:NP], 0.0)
            t.then_inc(S("t_pads"), 1)
            dve.wait_ge(S("t_pads"), 1)

            def post(name, row, add=None, unit=None):
                general(name)
                at = AGG[name] * NCH

                turns = (AGG[name] * (NCH // 2 + 1), AGG[name] * (NCH // 2))

                def chunk(s, i, c):
                    n = c + at + 1
                    dve.wait_ge(S(f"ag_mm{s}"), i + turns[s] + 2)
                    cc = bass.ds(c * CH, CH)
                    if unit is not None:
                        t = v.scalar_tensor_tensor(out=T1[:, cc], in0=ps[:, s, 0:CH], scalar=unit, in1=row[:, cc],
                                                   op0=ALU.mult, op1=ALU.mult)
                    elif add is None:
                        t = v.tensor_tensor(T1[:, cc], ps[:, s, 0:CH], row[:, cc], ALU.mult)
                    else:
                        v.tensor_tensor(T1[:, cc], ps[:, s, 0:CH], add[:, cc], ALU.add).then_inc(S("self_loop"), 1)
                        dve.wait_ge(S("self_loop"), c + 1)
                        t = v.tensor_tensor(T1[:, cc], T1[:, cc], row[:, cc], ALU.mult)
                    t.then_inc(S("ag_post"), 1)
                    dve.wait_ge(S("ag_post"), n)
                    dve.sem_inc(S(f"ag_bank{s}"), 1)
                with dve.Fori(0, NCH // 2) as i:
                    for s in range(2):
                        chunk(s, i, i * 2 + s)
                chunk(0, NCH // 2, NCH - 1)

            def quads(name, f, after=None):
                for q in range(NQ):
                    n = min(4, NB - 4 * q)
                    dve.wait_ge(S("blk_mm"), BLK[name] * NQ + q + 1)
                    f(q, n, 4 * q, ps[:, 2 + q % 2, 0:n * P].rearrange("p (b d) -> p b d", d=D)).then_inc(S("blk_used"), 1)
                    dve.wait_ge(S("blk_used"), BLK[name] * NQ + q + 1)
                    if after is not None:
                        centre(after, q)

            def product(name, use, f):
                def take(q, n, b0, p3):
                    link(f(q, n, b0, p3))
                    return v.tensor_reduce(most_q[:, q:q + 1], hn[:, b0:b0 + n, :], AX.XY, ALU.max, apply_absolute_value=True)
                quads(name, take)
                v.tensor_reduce(sc[:, 0:1], most_q[:, 0:NQ], AX.X, ALU.max).then_inc(S("scale_in"), 1)
                dve.wait_ge(S("scale_mm"), 2 * use + 1)
                v.tensor_reduce(sc[0:1, 1:2], ps[0:1, 4, 0:P], AX.X, ALU.max).then_inc(S("scale_in"), 1)
                dve.wait_ge(S("scale_mm"), 2 * use + 2)
                link(v.tensor_scalar(sc[:, 1:2], ps[:, 4, P:P + 1], 1e-30, None, ALU.max))
                link(v.tensor_scalar(sc[:, 2:3].bitcast(I32), sc[:, 1:2].bitcast(I32), 255 << 23, None, ALU.bitwise_and))
                link(v.tensor_scalar(sc[:, 2:3], sc[:, 2:3], 2.0 ** -13, None, ALU.mult))
                v.reciprocal(sc[:, 3:4], sc[:, 2:3]).then_inc(S("scaled"), 1)
                for h, (lo, hi) in enumerate(HALVES):
                    dve.wait_ge(S("q_high"), 2 * use + h + 1)
                    v.scalar_tensor_tensor(out=op[:, lo:hi, 1, :], in0=hn[:, lo:hi, :], scalar=sc[:, 3:4], in1=op[:, lo:hi, 0, :],
                                           op0=ALU.mult, op1=ALU.subtract).then_inc(S("q_op"), 1)

            def add_bias(i):
                link(v.tensor_tensor(x_nm[:, :, :], x_nm[:, :, :], biasb[:, i, :].unsqueeze(1).broadcast_to([P, NB, D]), ALU.add))

            add_x = lambda q, n, b0, p3: v.tensor_tensor(x_nm[:, b0:b0 + n, :], x_nm[:, b0:b0 + n, :], p3, ALU.add)

            post("l0a", row)
            product("l0p", 0, lambda q, n, b0, p3: v.tensor_copy(hn[:, b0:b0 + n, :], p3))
            dve.wait_ge(S("bias_copied"), 1)
            add_bias(BL2)
            post("l0b", row, unit=sc[:, 2:3])
            quads("l0o", add_x, "l1")

            layernorm("l1")
            dve.wait_ge(S("tr_copied"), (TR["l1h"] + 1) * NQ)
            dve.wait_ge(S("deg_copied"), 2 * NCH)
            link(v.reciprocal(row[:, :], row[:, :]))
            link(v.tensor_scalar(T3[:, 0:NT], T3[:, 0:NT], 1.0, None, ALU.max))
            link(v.reciprocal(T3[:, 0:NT], T3[:, 0:NT]))
            for step in range(NSTEP):
                general(f"l1s{step}", KT)
                with dve.Fori(0, NCH) as i:
                    link.enter(i, 4)
                    c = i + step * NCH
                    hc = T1[:, bass.ds(i * CH, CH)]
                    pre, nt, zs, rs = tmp[:, 7, :], tmp[:, 8, :], tmp[:, 6, :], tmp[:, 5, :]
                    t1, t2 = tmp[:, 9, :], tmp[:, 10, :]
                    dve.wait_ge(S("gru_msg"), c + 1)
                    v.tensor_tensor(tmp[:, 4, :], ps[:, 2, 0:CH], T2[:, bass.ds(i * CH, CH)], ALU.add).then_inc(S("gru_a"), 1)
                    dve.wait_ge(S("gru_r"), c + 1)
                    link(v.scalar_tensor_tensor(out=t1, in0=ps[:, 5, 0:CH], scalar=bcol[:, 7:8], in1=rs, op0=ALU.add, op1=ALU.mult))
                    dve.wait_ge(S("gru_mm"), c * 3 + 3)
                    v.tensor_tensor(pre, t1, ps[:, 6, 0:CH], ALU.add).then_inc(S("gru_pre"), 1)
                    dve.wait_ge(S("gru_n"), c + 1)
                    link(v.tensor_tensor(t2, hc, nt, ALU.subtract))
                    dve.wait_ge(S("gru_z"), c + 1)
                    link(v.tensor_tensor(t2, t2, zs, ALU.mult))
                    link(v.tensor_tensor(hc, t2, nt, ALU.add))
                    dve.sem_inc(S("gru_h"), 1)
                link.leave(NCH)
                if step < NSTEP - 1:
                    for q in range(NQ):
                        n = min(4, NB - 4 * q)
                        dve.wait_ge(S("high"), step * NQ + q + 1)
                        v.tensor_tensor(op[:, 4 * q:4 * q + n, 1, :], ps[:, STEP_BANKS[q % 4], 0:n * P].rearrange("p (b d) -> p b d", d=D),
                                        op[:, 4 * q:4 * q + n, 0, :], ALU.subtract).then_inc(S("tr_copied"), 1)
            for q in range(NQ):
                n = min(4, NB - 4 * q)
                sig, val = sig2[:, q % 2, 0:n * P], tmpf[:, NP + 2 * 4 * P:NP + 3 * 4 * P][:, 0:n * P]
                dve.wait_ge(S("l1o_sig"), q + 1)
                link(v.tensor_tensor(val.rearrange("p (b d) -> p b d", d=D), ps[:, OUT_BANKS[q % 2][1], 0:n * P].rearrange("p (b d) -> p b d", d=D),
                                     biasb[:, BJ, :].unsqueeze(1).broadcast_to([P, n, D]), ALU.add))
                link(v.tensor_tensor(sig, sig, val, ALU.mult))
                v.tensor_tensor(x_nm[:, 4 * q:4 * q + n, :], x_nm[:, 4 * q:4 * q + n, :], sig.rearrange("p (b d) -> p b d", d=D),
                                ALU.add).then_inc(S("l1o_used"), 1)
                dve.wait_ge(S("l1o_used"), q + 1)
                centre("l2", q)

            layernorm("l2", dis_nm[:, :])
            dve.wait_ge(S("tr_copied"), (TR["l2h"] + 1) * NQ)
            post("l2a", row, T0)
            with dve.Fori(0, NCH) as c:
                cc = bass.ds(c * CH, CH)
                dve.wait_ge(S("l2d_bias"), c + 1)
                v.scalar_tensor_tensor(out=T2[:, cc], in0=T2[:, cc], scalar=0.01, in1=T2[:, cc], op0=ALU.mult, op1=ALU.max
                                       ).then_inc(S("l2d_done"), 1)
            product("l2p", 1, lambda q, n, b0, p3: v.tensor_tensor(
                hn[:, b0:b0 + n, :], p3, dis_nm[:, b0:b0 + n].unsqueeze(2).broadcast_to([P, n, D]), ALU.mult))
            own = squares.rearrange("p (a b) -> p a b", b=D)
            link(v.tensor_tensor(own, hn[:, :, :], wide(dis_nm[:, :]), ALU.mult))
            link(v.tensor_tensor(x_nm[:, :, :], x_nm[:, :, :], own, ALU.add))
            add_bias(B2)
            post("l2b", row, unit=sc[:, 2:3])
            quads("l2o", add_x, "l3")

            layernorm("l3", rdeg_nm[:, :])
            add_bias(B3)
            post("l3a", T3)
            for q in range(NQ):
                n = min(4, NB - 4 * q)
                dve.wait_ge(S("blk_mm"), BLK["l3o"] * NQ + q + 1)
                add_x(q, n, 4 * q, ps[:, 2 + q % 2, 0:n * P].rearrange("p (b d) -> p b d", d=D)).then_inc(S("blk_used"), 1)
                dve.wait_ge(S("blk_used"), BLK["l3o"] * NQ + q + 1)
                dve.sem_inc(S("l3_out"), 1)


INPUTS = ["x", "src", "dst", "edge_type_4", "L0_gnn_W_l1", "L0_gnn_b_l1", "L0_gnn_W_r1", "L0_gnn_W_l2", "L0_gnn_b_l2",
          "L0_gnn_W_r2", "L1_gnn_W_et", "L1_gnn_b_et", "L1_gnn_W_ih", "L1_gnn_b_ih", "L1_gnn_W_hh", "L1_gnn_b_hh",
          "L1_gnn_i_w", "L1_gnn_i_b", "L1_gnn_j_w", "L1_gnn_j_b", "L2_gnn_W1", "L2_gnn_b1", "L2_gnn_W2", "L2_gnn_b2",
          "L3_gnn_W", "L3_gnn_b"]


def kernel(**inputs):
    import numpy as _np
    import concourse.bacc as _bacc
    from concourse import mybir as _mybir
    from concourse.bass_utils import run_bass_kernel_spmd as _run

    nc = _bacc.Bacc("TRN2", target_bir_lowering=False, num_devices=1)
    arrays, aps = {}, {}
    for name in INPUTS:
        arr = _np.ascontiguousarray(inputs[name])
        arrays[f"in_{name}"] = arr
        aps[name] = nc.dram_tensor(f"in_{name}", arr.shape, _mybir.dt.from_np(arr.dtype), kind="ExternalInput").ap()
    out = nc.dram_tensor("out_0", (N, D), _mybir.dt.float32, kind="ExternalOutput").ap()
    packed = nc.dram_tensor("packed_edges", (E + CAP,), _mybir.dt.int32, kind="Internal").ap()
    adj = nc.dram_tensor("adjacency", (KT + 1, NCH, P, PIECE), _mybir.dt.uint8, kind="Internal").ap()
    table = nc.dram_tensor("operand_rows", (NP, 2 * D), _mybir.dt.float16, kind="Internal").ap()
    sums = nc.dram_tensor("general_sums", (KT, NCH, P, CH), _mybir.dt.float32, kind="Internal").ap()
    build(nc, aps, out, packed, adj, table, sums)
    r = _run(nc, [arrays], core_ids=[0])
    return r.results[0]["out_0"]
```
